# Optimizing a Trainium2 kernel written in Bass

```python
import numpy as np
import jax
import jax.numpy as jnp

def _softmax(x, axis=-1):
    return jax.nn.softmax(x, axis=axis)

def _gelu(x):
    return jax.nn.gelu(x, approximate=True)

def _silu(x):
    return jax.nn.silu(x)

def _sigmoid(x):
    return jax.nn.sigmoid(x)

def _layernorm(x, axis=-1, eps=1e-05):
    m = jnp.mean(x, axis=axis, keepdims=True)
    v = jnp.var(x, axis=axis, keepdims=True)
    return (x - m) / jnp.sqrt(v + eps)

def _scatter_add(tgt, idx, src, axis=0):
    return tgt.at[idx].add(src)

def _segment_sum(src, seg, n):
    return jax.ops.segment_sum(src, seg, n)
kernel_name = 'mk_gnn_preln_d2_gnn_r64_13ce04'

def setup_inputs(seed: int=0):
    np.random.seed(seed)
    _w = jnp.asarray

    def _rec_inputs():
        import jax
        import jax.numpy as jnp
        _gk = jax.random.key(seed)
        x = -0.0002117 + 1 * jax.random.normal(jax.random.fold_in(_gk, 1), (50000, 256), jnp.float32)
        src = jax.random.randint(jax.random.fold_in(_gk, 2), (12500,), 0, 50000, jnp.int32)
        dst = jnp.minimum((50000 * jax.random.uniform(jax.random.fold_in(_gk, 3), (12500,)) ** 2.0).astype(jnp.int32), 49999)
        _o = jnp.argsort(dst, stable=True)
        src = src[_o]
        dst = dst[_o]
        edge_attr_64 = -9.77346e-05 + 0.999888 * jax.random.normal(jax.random.fold_in(_gk, 12), (12500, 64), jnp.float32)
        edge_weight = jax.random.uniform(jax.random.fold_in(_gk, 13), (12500,), jnp.float32, 0.0, 1)
        return (x, src, dst, edge_attr_64, edge_weight)
    x, src, dst, edge_attr_64, edge_weight = _rec_inputs()

    def _L0_gnn_setup():
        import jax, jax.numpy as jnp
        import numpy as np
        N_NODES = 100000
        N_EDGES = 50000
        D_IN = 256
        D_OUT = 256
        key = jax.random.key(seed)
        k1, k2, k3, k4, k5 = jax.random.split(key, 5)
        inputs = jax.random.normal(k1, (N_NODES, D_IN), dtype=jnp.float32)
        init_range = np.sqrt(6.0 / (D_IN + D_OUT)).astype(np.float32)
        weight = jax.random.uniform(k2, (D_IN, D_OUT), dtype=jnp.float32, minval=-init_range, maxval=init_range)
        edge_src = jax.random.randint(k3, (N_EDGES,), 0, N_NODES, dtype=jnp.int32)
        edge_dst = jax.random.randint(k4, (N_EDGES,), 0, N_NODES, dtype=jnp.int32)
        edge_vals = jax.random.uniform(k5, (N_EDGES,), dtype=jnp.float32)
        return {'inputs': inputs, 'weight': weight, 'edge_src': edge_src, 'edge_dst': edge_dst, 'edge_vals': edge_vals}
    _L0_gnn_all = _L0_gnn_setup()
    _L0_gnn_in = {k: v for k, v in _L0_gnn_all.items() if k in ('weight',)}
    del _L0_gnn_all

    def _L1_gnn_setup():
        import jax, jax.numpy as jnp
        import numpy as np
        N, E, D, H, FE = (50000, 12500, 256, 8, 64)
        HD = D // H
        key = jax.random.key(seed)
        ks = jax.random.split(key, 14)
        sD = 1.0 / np.sqrt(D)
        sF = 1.0 / np.sqrt(FE)
        return {'h': jax.random.normal(ks[0], (N, D), jnp.float32), 'efeat': jax.random.normal(ks[1], (E, FE), jnp.float32), 'src': jax.random.randint(ks[2], (E,), 0, N), 'dst': jax.random.randint(ks[3], (E,), 0, N), 'Wq': jax.random.normal(ks[4], (D, D), jnp.float32) * sD, 'Wk': jax.random.normal(ks[5], (D, D), jnp.float32) * sD, 'Wv': jax.random.normal(ks[6], (D, D), jnp.float32) * sD, 'W1': jax.random.normal(ks[7], (FE, D), jnp.float32) * sF, 'b1': jnp.zeros((D,), jnp.float32), 'W2': jax.random.normal(ks[8], (D, H), jnp.float32) * sD, 'b2': jnp.zeros((H,), jnp.float32), 'Wo': jax.random.normal(ks[9], (D, D), jnp.float32) * sD, 'bo': jnp.zeros((D,), jnp.float32)}
    _L1_gnn_all = _L1_gnn_setup()
    _L1_gnn_in = {k: v for k, v in _L1_gnn_all.items() if k in ('Wq', 'Wk', 'Wv', 'W1', 'b1', 'W2', 'b2', 'Wo', 'bo')}
    del _L1_gnn_all
    return {'x': x, 'src': src, 'dst': dst, 'edge_attr_64': edge_attr_64, 'edge_weight': edge_weight, 'L0_gnn_weight': _L0_gnn_in['weight'], 'L1_gnn_Wq': _L1_gnn_in['Wq'], 'L1_gnn_Wk': _L1_gnn_in['Wk'], 'L1_gnn_Wv': _L1_gnn_in['Wv'], 'L1_gnn_W1': _L1_gnn_in['W1'], 'L1_gnn_b1': _L1_gnn_in['b1'], 'L1_gnn_W2': _L1_gnn_in['W2'], 'L1_gnn_b2': _L1_gnn_in['b2'], 'L1_gnn_Wo': _L1_gnn_in['Wo'], 'L1_gnn_bo': _L1_gnn_in['bo']}

def reference(x, src, dst, edge_attr_64, edge_weight, L0_gnn_weight, L1_gnn_Wq, L1_gnn_Wk, L1_gnn_Wv, L1_gnn_W1, L1_gnn_b1, L1_gnn_W2, L1_gnn_b2, L1_gnn_Wo, L1_gnn_bo):
    import jax
    import jax.numpy as jnp

    def _L0_gnn_ref(inputs, weight, edge_src, edge_dst, edge_vals):
        import jax, jax.numpy as jnp
        import numpy as np
        N_NODES = 100000
        N_EDGES = 50000
        D_IN = 256
        D_OUT = 256
        x = inputs @ weight
        msgs = edge_vals[:, None] * x[edge_src]
        out = jax.ops.segment_sum(msgs, edge_dst, num_segments=inputs.shape[0])
        return jax.nn.relu(out)

    def _L1_gnn_ref(h, efeat, src, dst, Wq, Wk, Wv, W1, b1, W2, b2, Wo, bo):
        import jax, jax.numpy as jnp
        import numpy as np
        N, E, D, H, FE = (50000, 12500, 256, 8, 64)
        HD = D // H
        n = h.shape[0]
        Q = (h @ Wq).reshape(n, H, HD)
        K = (h @ Wk).reshape(n, H, HD)
        V = (h @ Wv).reshape(n, H, HD)
        score = jnp.einsum('ehd,ehd->eh', Q[dst], K[src]) / np.sqrt(HD)
        score = score + jax.nn.relu(efeat @ W1 + b1) @ W2 + b2
        m = jax.ops.segment_max(score, dst, num_segments=n)
        ex = jnp.exp(score - m[dst])
        denom = jax.ops.segment_sum(ex, dst, num_segments=n)
        alpha = ex / denom[dst]
        out = jax.ops.segment_sum(alpha[:, :, None] * V[src], dst, num_segments=n)
        out = out.reshape(n, D)
        return out @ Wo + bo
    h = jnp.maximum(_layernorm(x, axis=-1), 0.0)
    x = x + _L0_gnn_ref(h, L0_gnn_weight, src, dst, edge_weight)
    h = jnp.maximum(_layernorm(x, axis=-1), 0.0)
    x = x + _L1_gnn_ref(h, edge_attr_64, src, dst, L1_gnn_Wq, L1_gnn_Wk, L1_gnn_Wv, L1_gnn_W1, L1_gnn_b1, L1_gnn_W2, L1_gnn_b2, L1_gnn_Wo, L1_gnn_bo)
    return x

_drawn_inputs = setup_inputs


def setup_inputs(seed=0):
    import zlib

    import numpy as np

    out = dict(_drawn_inputs(seed))
    spreads = {'L1_gnn_b1': (0.0, 2.0), 'L1_gnn_b2': (0.0, 2.0), 'L1_gnn_bo': (0.0, 0.1)}
    factors = {'L1_gnn_Wq': 9.737,
     'L1_gnn_Wk': 10.231,
     'edge_attr_64': 4.441,
     'L1_gnn_W1': 4.408,
     'L1_gnn_W2': 4.428}
    for name, (base, spread) in spreads.items():
        noise = np.random.default_rng([zlib.crc32(name.encode()), seed]).standard_normal(out[name].shape)
        drawn = base * np.exp(spread * noise) if base else spread * noise
        out[name] = jnp.asarray(drawn.astype(out[name].dtype))
    for name, factor in factors.items():
        out[name] = (out[name] * factor).astype(out[name].dtype)
    return out
```

```python
import concourse.bass as bass
import numpy as np
from concourse import mybir
from contextlib import ExitStack

N, E, D, H, FE = 50000, 12500, 256, 8, 64
HD = D // H
P = 128
J = 7
T = -(-E // P)
G = T // J
EP = T * P
GE = J * P
NC = D // P
GH = G * H
EPS = 1e-5
BIG = 1e30
PAD_DST = 65535
SKIP = 1000000.0
BR = 9
NROW = N // P
BULK = NROW // BR
REST = NROW - BULK * BR
TAIL = N - NROW * P


def gnn_program(nc, x, dst, src, wgt, eattr, W, Wq, Wk, Wv, W1, b1, W2, b2, Wo, bo, out):
    f32 = mybir.dt.float32
    i32 = mybir.dt.int32
    ALU = mybir.AluOpType
    ACT = mybir.ActivationFunctionType
    AX = mybir.AxisListType.X

    x1_d = nc.dram_tensor("x1_bo", (EP, D), f32, kind="Internal").ap()
    h2_d = nc.dram_tensor("h2", (EP, D), f32, kind="Internal").ap()
    q_d = nc.dram_tensor("q", (EP, D), f32, kind="Internal").ap()
    dstf_d = nc.dram_tensor("dst_f", (T, P), f32, kind="Internal").ap()
    key_d = nc.dram_tensor("key", (T, P), f32, kind="Internal").ap()
    cont_d = nc.dram_tensor("cont", (EP + 1,), f32, kind="Internal").ap()

    ctx = ExitStack()
    with ctx:
        def sb(name, shape, dt=f32):
            return ctx.enter_context(nc.sbuf_tensor(name, shape, dt))

        def pb(name, shape, dt=f32):
            return ctx.enter_context(nc.psum_tensor(name, shape, dt))

        def sem(name):
            return ctx.enter_context(nc.semaphore(name))

        def sem2(name):
            return [sem(name + "_0"), sem(name + "_1")]

        store = sb("store", [P, T * D])
        ringA = sb("ringA", [P, 2 * J * D])
        ringB = sb("ringB", [P, 2 * J * D])
        ringC = sb("ringC", [P, 2 * J * D])
        bulk = [sb(f"bulk{i}", [P, BR * D]) for i in range(2)]
        Wsb, Wqsb, Wosb = (sb(n, [P, NC, D]) for n in ("W_sb", "Wq_sb", "Wo_sb"))
        Wkv = sb("Wkv_sb", [P, NC, 2 * D])
        W1sb = sb("W1_sb", [FE, D])
        W2sb = sb("W2_sb", [P, NC, H])
        b1c = sb("b1_col", [P, NC])
        b2b = sb("b2_all", [P, H])
        bob = sb("bo_all", [P, D])
        ident = sb("ident", [P, P])
        ones = sb("ones", [P, P])
        iota1 = sb("iota1", [P, P])
        epsc = sb("eps", [P, 1])
        rows = sb("rows", [P, 2 * GE])
        Sr = sb("Sr", [P, 2 * GE])
        small = sb("small", [P, 4 * D])
        ind = sb("ind", [P, 4 * P])
        dcol = sb("dst_col", [P, T])
        scol = sb("src_col", [P, T])
        wcol = sb("w_col", [P, T])
        dg_i = sb("dst_gather", [P, T], i32)
        sg_i = sb("src_gather", [P, T], i32)
        out_i = sb("out_scatter", [P, T], i32)
        slot_i = sb("slot_gather", [P, T], i32)
        tauf = sb("tau", [P, T])
        ends = sb("ends", [P, 4, T])
        DP = sb("last_dst_before", [P, T])
        cnt = sb("cnt", [P, 4, T])
        edge_w = sb("edge_w", [P, T, 2])
        sums = sb("sums", [P, 2, NC, T])
        carr = sb("carr", [P, 2, NC, T])
        sc_all = sb("scores", [P, J, G, H])
        st6 = sb("st6", [P, J, 6])
        mv = sb("mv", [P, 2, J, 2])
        sd = sb("sd", [P, 2, J])
        rs = sb("rs", [P, 2, J])
        nm = sb("nm", [P, 2, J])
        pm = sb("pm", [P, J])
        pz = sb("pz", [P, J])
        ist = sb("ist", [P, 2 * J], i32)
        taui = sb("taui", [P, 2 * J], i32)
        ssum = sb("ssum", [P, J * H])
        carry = sb("carry", [GH, 1])
        whole = sb("whole", [GH, 2])

        store3 = store[:, :].rearrange("p (t d) -> p t d", d=D)
        aT = [small[:, i * D:(i + 1) * D].rearrange("p (c e) -> p c e", c=NC) for i in range(2)]
        hT = [small[:, (2 + i) * D:(3 + i) * D].rearrange("p (c e) -> p c e", c=NC) for i in range(2)]
        taucmp = small[:, 0:J * T].rearrange("p (j t) -> p j t", t=T)
        hid = Sr[:, :].rearrange("p (c e) -> p c e", c=NC)
        eT = rows[0:FE, 0:GE]
        ef = [rows[:, GE + i * J * FE:GE + (i + 1) * J * FE] for i in range(2)]
        row = [rows[:, i * GE:(i + 1) * GE] for i in range(2)]
        prod = Sr[:, :].rearrange("p (j d) -> p j d", d=D)

        w_dstf, w_src, w_nxt, w_eq, w_fin, w_key = (ringB[0:T, k * P:(k + 1) * P] for k in range(6))
        w_zero = ringB[0:1, 6 * P:6 * P + 1]
        w_diag = ringB[0:T, 7 * P:7 * P + 4 * T]
        anti = ringB[0:T, 14 * P:14 * P + T]
        dst_i, nxt_i, src_i = (ringB[0:T, k * P:(k + 1) * P].bitcast(i32) for k in (16, 17, 18))
        w_r = ringB[0:T, 19 * P:20 * P]
        iota_i = ringB[:, 12 * P:13 * P].bitcast(i32)
        f_cont, f_next, xs, tmp = (ringB[0:GH, k * GE:(k + 1) * GE] for k in range(4))
        f_neg, f_last, fwd, spread = (ringC[0:GH, k * GE:(k + 1) * GE] for k in range(4))
        ex = ringA[0:GH, 0:GE]
        lin = small[0:1, 0:4 * GH].rearrange("o (k r) -> o k r", k=4)

        def indF(u):
            return ind[:, (u % 2) * P:(u % 2 + 1) * P]

        def indL(u):
            return ind[:, (2 + u % 2) * P:(3 + u % 2) * P]

        def S(u):
            return Sr[:, u * P:(u + 1) * P]

        def A(u):
            return ringA[:, u * D:(u + 1) * D]

        def B(u):
            return ringB[:, u * D:(u + 1) * D]

        def C(u):
            return ringC[:, u * D:(u + 1) * D]

        def group(ring, b):
            return ring[:, b * J * D:(b + 1) * J * D].rearrange("p (j d) -> p j d", d=D)

        bank = [pb(f"bank{i}", [P, 512]) for i in range(8)]

        s_idx, s_wts = sem("index_rows_in"), sem("weights_in")
        s_cst, s_cst2 = sem("constants"), sem("constants_step")
        s_key = sem("rows_for_dram"), sem("rows_in_dram")
        s_tr, s_diag = sem("columns_in_psum"), sem("diagonals")
        s_pro = sem("columns_ready")
        pdve = sem("dve_prologue")
        ef_in, x_in, k_in = sem2("ef_in"), sem2("xsrc_in"), sem2("key_in")
        eT_ps, eT_sb, hid_ps, hid_sb = sem("eT_in_psum"), sem("eT_in_sbuf"), sem("hid_in_psum"), sem("hid_in_sbuf")
        b_ps, b_done = sem("bias_in_psum"), sem("bias_read")
        var1, sd1, rs1, h1a, h1, fl, fl_read = (sem(n) for n in (
            "var1", "sd1", "rstd1", "h1_written", "h1_stored", "end_sums_in_psum", "end_sums_read"))
        tau_rdy, cp = sem("tau_ready"), sem("pool_index_copied")
        lead1, lag1 = sem("dve_lead1"), sem("dve_lag1")
        bulk_ld, bulk_st, bulk_add = sem2("bulk_loaded"), sem2("bulk_stored"), sem("bulk_added")
        s_carr = sem("dve_carries")
        row_in, xd_in = sem2("rows_in"), sem2("xdst_in")
        hs, S2, ag, aT2, w2p, x1r = (sem(n) for n in (
            "h_copied", "S_ready", "agg_in_psum", "aggT_ready", "l0_in_psum", "x1_ready"))
        var2, sd2, rs2, h2r, t2, hT2, qp, q2, bo2 = (sem(n) for n in (
            "var2", "sd2", "rstd2", "h2_ready", "h2T_in_psum", "h2T_ready", "q_in_psum", "q_ready", "bo_added"))
        st_x, st_h, st_q = sem2("x1_stored"), sem2("h2_stored"), sem2("q_stored")
        lead2, lag2 = sem("dve_lead2"), sem("dve_lag2")
        c3, t3, hT3, kv, v3, k3 = (sem(n) for n in (
            "hsrc_copied", "hsrcT_in_psum", "hsrcT_ready", "kv_in_psum", "v_stored", "k_used"))
        o_in, ql = sem2("h2_overlaid"), sem2("q_loaded")
        lag3 = sem("dve_lag3")
        s_flag, x_ps, x_sb, s_sm, pe_sm, act_sm, al_ps, s_al = (sem(n) for n in (
            "flags_in", "scoresT_in_psum", "scoresT_ready", "dve_softmax", "pe_softmax", "act_softmax",
            "alpha_in_psum", "alpha_ready"))
        row4, x4 = sem2("rows4_in"), sem2("x1_loaded")
        s4, ag4, aT4, wo, o4 = (sem(n) for n in (
            "weighted_v_ready", "attn_in_psum", "attnT_ready", "wo_in_psum", "out_rows_ready"))
        lag4, cp4, sc_out = sem("dve_lag4"), sem("scatter_index_copied"), sem2("rows_scattered")

        def need(eng, s, value):
            if isinstance(value, int) and value <= 0:
                return
            eng.wait_ge(s, value)

        def hold(eng):
            eng.nop(nofuse=True)

        class Chain:

            def __init__(self, eng, s):
                self.eng, self.s, self.per, self.n = eng, s, None, 0

            def start(self, g):
                self.base = 0 if self.per is None else g * self.per
                self.n = 0

            def link(self, ins):
                self.n += 1
                ins.then_inc(self.s, 1)
                self.eng.wait_ge(self.s, self.base + self.n)
                if not isinstance(self.base, int):
                    hold(self.eng)

            def end(self):
                assert self.per in (None, self.n)
                self.per = self.n

        def turns(eng, turn):
            turn(0, 0, 0, True, False)
            turn(1, 0, 1, True, True)
            with eng.Fori(1, G // 2) as h:
                turn(2 * h, h, 0, True, True)
                turn(2 * h + 1, h, 1, True, True)
            turn(G, G // 2, 0, False, True)

        def lagging(g, h, b):
            return g - 1, (h if b else h - 1), 1 - b

        def edge_rows(dram, g):
            return dram.rearrange("(t p) d -> p t d", p=P)[:, bass.ds(g * J, J), :]

        xb = x[0:NROW * P, :].rearrange("(p n) d -> p (n d)", p=P)
        ob = out[0:NROW * P, :].rearrange("(p n) d -> p (n d)", p=P)

        def bulk_io(sp, base, g, h, b):
            need(sp, bulk_st[b], 16 * (base // 2 + h) if not (base == 0 and isinstance(h, int)) else 16 * h)
            sp.dma_start(bulk[b][:, :], xb[:, bass.ds((base + g) * (BR * D), BR * D)]).then_inc(bulk_ld[b], 16)
            if not (isinstance(g, int) and base + g == 0):
                sp.wait_ge(bulk_add, base + g)
                sp.dma_start(ob[:, bass.ds((base + g - 1) * (BR * D), BR * D)],
                             bulk[1 - b][:, :]).then_inc(bulk_st[1 - b], 16)

        def bulk_bo(dve, base, h, b):
            dve.wait_ge(bulk_ld[b], 16 * (base // 2 + h + 1))
            v = bulk[b][:, :].rearrange("p (r d) -> p r d", d=D)
            nc.vector.tensor_tensor(v, v, bob[:, None, :].to_broadcast([P, BR, D]), ALU.add).then_inc(bulk_add, 1)

        block = ctx.enter_context(nc.Block())

        @block.sync
        def _(sp):
            sp.dma_start(dst_i[:, :], dst[0:EP].rearrange("(t p) -> t p", p=P)).then_inc(s_idx, 16)
            sp.dma_start(nxt_i[:, :], dst[1:EP + 1].rearrange("(t p) -> t p", p=P)).then_inc(s_idx, 16)
            sp.dma_start(src_i[:, :], src.rearrange("(t p) -> t p", p=P)).then_inc(s_idx, 16)
            sp.dma_start(w_r[:, :], wgt.rearrange("(t p) -> t p", p=P)).then_inc(s_idx, 16)
            for m, sbuf in ((W, Wsb), (Wq, Wqsb), (Wo, Wosb), (W2, W2sb)):
                sp.dma_start(sbuf[:, :, :], m.rearrange("(c p) n -> p c n", p=P)).then_inc(s_wts, 16)
            sp.dma_start(Wkv[:, :, 0:D], Wk.rearrange("(c p) n -> p c n", p=P)).then_inc(s_wts, 16)
            sp.dma_start(Wkv[:, :, D:2 * D], Wv.rearrange("(c p) n -> p c n", p=P)).then_inc(s_wts, 16)
            sp.dma_start(W1sb[:, :], W1).then_inc(s_wts, 16)
            sp.dma_start(b1c[:, :], b1.rearrange("(c p) -> p c", p=P), allow_slow_non_contiguous=True).then_inc(s_wts, 16)
            sp.dma_start(b2b[:, :], b2[None, :].to_broadcast([P, H])).then_inc(s_wts, 16)
            sp.dma_start(bob[:, :], bo[None, :].to_broadcast([P, D])).then_inc(s_wts, 16)
            sp.wait_ge(s_key[0], 1)
            sp.dma_start(dstf_d, w_dstf[:, :]).then_inc(s_key[1], 16)
            sp.dma_start(key_d, w_key[:, :]).then_inc(s_key[1], 16)
            sp.dma_start(cont_d[1:EP + 1].rearrange("(t p) -> t p", p=P), w_eq[:, :]).then_inc(s_key[1], 16)
            sp.dma_start(cont_d[0:1].rearrange("(a b) -> a b", a=1), w_zero[0:1, 0:1]).then_inc(s_key[1], 16)

            def phase1(g, h, b, lead, lag):
                if lead:
                    need(sp, eT_ps, g - 1)
                    sp.dma_start(ef[b].rearrange("p (j f) -> p j f", f=FE),
                                 edge_rows(eattr, g)).then_inc(ef_in[b], 16)
                    bulk_io(sp, 0, g, h, b)
            turns(sp, phase1)

            sp.wait_ge(s_key[1], 64)
            sp.wait_ge(eT_ps, G)
            sp.wait_ge(b_ps, G)

            def phase2(g, h, b, lead, lag):
                if lead:
                    need(sp, aT2, J * (g - 1))
                    sp.dma_start(row[b], dstf_d.rearrange("t p -> (t p)")[bass.ds(g * GE, GE)][None, :]
                                 .to_broadcast([P, GE])).then_inc(row_in[b], 16)
                    bulk_io(sp, G, g, h, b)
                if lag:
                    g, h, b = lagging(g, h, b)
                    sp.wait_ge(h2r, J * (g + 1))
                    sp.dma_start(edge_rows(h2_d, g), group(ringB, b)).then_inc(st_h[b], 16)
                    sp.wait_ge(bo2, g + 1)
                    sp.dma_start(edge_rows(x1_d, g), group(ringA, b)).then_inc(st_x[b], 16)
                    sp.wait_ge(q2, J * (g + 1))
                    sp.dma_start(edge_rows(q_d, g), group(ringC, b)).then_inc(st_q[b], 16)
            turns(sp, phase2)

            for i in range(2):
                sp.wait_ge(st_q[i], 16 * (G // 2))
                sp.wait_ge(st_h[i], 16 * (G // 2))
                sp.wait_ge(st_x[i], 16 * (G // 2))
            sp.dma_start(f_cont, cont_d[0:EP].rearrange("(g e) -> g e", g=G)[:, None, :].to_broadcast([G, H, GE])).then_inc(s_flag, 16)
            sp.dma_start(f_next, cont_d[1:EP + 1].rearrange("(g e) -> g e", g=G)[:, None, :].to_broadcast([G, H, GE])).then_inc(s_flag, 16)

            def phase3(g, h, b, lead, lag):
                if lead:
                    need(sp, k3, J * (g - 1))
                    sp.dma_start(group(ringC, b), edge_rows(q_d, g)).then_inc(ql[b], 16)
                    bulk_io(sp, 2 * G, g, h, b)
            turns(sp, phase3)
            last = BULK - 1
            sp.wait_ge(bulk_st[0], 16 * (last // 2))
            sp.dma_start(bulk[0][:, :], xb[:, last * BR * D:BULK * BR * D]).then_inc(bulk_ld[0], 16)
            sp.wait_ge(bulk_add, last)
            sp.dma_start(ob[:, (last - 1) * BR * D:last * BR * D], bulk[1][:, :]).then_inc(bulk_st[1], 16)
            sp.wait_ge(bulk_st[1], 16 * ((last + 1) // 2))
            sp.dma_start(bulk[1][:, 0:REST * D], xb[:, BULK * BR * D:NROW * D]).then_inc(bulk_ld[1], 16)
            sp.dma_start(bulk[1][0:TAIL, REST * D:(REST + 1) * D], x[NROW * P:N, :]).then_inc(bulk_ld[1], 16)
            sp.wait_ge(bulk_add, last + 1)
            sp.dma_start(ob[:, last * BR * D:BULK * BR * D], bulk[0][:, :]).then_inc(bulk_st[0], 16)
            sp.wait_ge(bulk_add, last + 3)
            sp.dma_start(ob[:, BULK * BR * D:NROW * D], bulk[1][:, 0:REST * D]).then_inc(bulk_st[1], 16)
            sp.dma_start(out[NROW * P:N, :], bulk[1][0:TAIL, REST * D:(REST + 1) * D]).then_inc(bulk_st[1], 16)

            sp.wait_ge(s_al, 1)

            def phase4(g, h, b, lead, lag):
                if lead:
                    need(sp, aT4, J * (g - 1))
                    sp.dma_start(row[b], dstf_d.rearrange("t p -> (t p)")[bass.ds(g * GE, GE)][None, :]
                                 .to_broadcast([P, GE])).then_inc(row4[b], 16)
                    need(sp, sc_out[b], 16 * J * h)
                    sp.dma_start(group(ringB, b), edge_rows(x1_d, g)).then_inc(x4[b], 16)
            turns(sp, phase4)

        @block.gpsimd
        def _(pool):
            nc.gpsimd.memset(ident[:, :], 0.0).then_inc(s_cst2, 1)
            nc.gpsimd.memset(anti[:, :], 0.0).then_inc(s_cst2, 1)
            nc.gpsimd.iota(iota_i, pattern=[[1, P]], base=1, channel_multiplier=0).then_inc(s_cst2, 1)
            pool.wait_ge(s_cst2, 3)
            nc.gpsimd.affine_select(out=ident[:, :], in_=ident[:, :], compare_op=ALU.not_equal, fill=1.0, base=0,
                                    pattern=[[-1, P]], channel_multiplier=1).then_inc(s_cst, 1)
            nc.gpsimd.affine_select(out=anti[:, :], in_=anti[:, :], compare_op=ALU.not_equal, fill=1.0, base=-(T - 1),
                                    pattern=[[1, T]], channel_multiplier=1).then_inc(s_cst, 1)
            pool.wait_ge(s_pro, 1)
            copies = [0]

            def indices(table, g, b):
                nc.gpsimd.tensor_copy(ist[:, b * J:(b + 1) * J], table[:, bass.ds(g * J, J)]).then_inc(cp, 1)
                pool.wait_ge(cp, copies[0] + g + 1)
                pool.nop(nofuse=True)

            def phase1(g, h, b, lead, lag):
                if lead:
                    need(pool, fl, g - 1)
                    indices(sg_i, g, b)
                    for j in range(J):
                        pool.indirect_dma_start(A(b * J + j), None, x, bass.IndirectOffsetOnAxis(
                            ap=ist[:, b * J + j:b * J + j + 1], axis=0)).then_inc(x_in[b], 16)
                    if isinstance(g, int) and g == 0:
                        pool.wait_ge(s_key[1], 64)
                    pool.wait_ge(tau_rdy, g + 1)
                    pool.nop(nofuse=True)
                    for j in range(J):
                        pool.indirect_dma_start(C(b * J + j)[:, 0:P], None, key_d, bass.IndirectOffsetOnAxis(
                            ap=taui[:, b * J + j:b * J + j + 1], axis=0)).then_inc(k_in[b], 16)
            turns(pool, phase1)
            copies[0] += G

            def phase2(g, h, b, lead, lag):
                if lead:
                    if isinstance(g, int):
                        pool.wait_ge(fl, G - 1 + g)
                    else:
                        pool.wait_ge(st_x[b], 16 * h)
                    indices(dg_i, g, b)
                    for j in range(J):
                        pool.indirect_dma_start(A(b * J + j), None, x, bass.IndirectOffsetOnAxis(
                            ap=ist[:, b * J + j:b * J + j + 1], axis=0)).then_inc(xd_in[b], 16)
                if lag:
                    g, h, b = lagging(g, h, b)
                    pool.wait_ge(h2r, J * (g + 1))
                    v = group(ringA, b)
                    nc.gpsimd.tensor_tensor(v, v, bob[:, None, :].to_broadcast([P, J, D]), ALU.add).then_inc(bo2, 1)
            turns(pool, phase2)
            copies[0] += G
            for i in range(2):
                pool.wait_ge(st_h[i], 16 * (G // 2))

            def phase3(g, h, b, lead, lag):
                if lead:
                    pool.wait_ge(c3, J * (g + 1))
                    indices(slot_i, g, b)
                    for j in range(J):
                        pool.indirect_dma_start(A(b * J + j), None, h2_d, bass.IndirectOffsetOnAxis(
                            ap=ist[:, b * J + j:b * J + j + 1], axis=0), bounds_check=EP - 1,
                            oob_is_err=False).then_inc(o_in[b], 16)
            turns(pool, phase3)
            copies[0] += G
            pool.wait_ge(bulk_st[0], 16 * ((BULK + 1) // 2))
            pool.wait_ge(bulk_st[1], 16 * ((BULK - 1) // 2 + 2))

            def phase4(g, h, b, lead, lag):
                if lag:
                    g, h, b = lagging(g, h, b)
                    need(pool, sc_out[b], 16 * J * h)
                    indices(out_i, g, b)
                    for j in range(J):
                        pool.wait_ge(o4, J * g + j + 1)
                        pool.nop(nofuse=True)
                        pool.indirect_dma_start(out, bass.IndirectOffsetOnAxis(
                            ap=ist[:, b * J + j:b * J + j + 1], axis=0), B(b * J + j), None,
                            bounds_check=N - 1, oob_is_err=False).then_inc(sc_out[b], 16)
            turns(pool, phase4)
            for i in range(2):
                pool.wait_ge(sc_out[i], 16 * J * (G // 2))

        @block.scalar
        def _(act):
            act.wait_ge(s_wts, 160)
            act.wait_ge(s_pro, 1)

            def phase1(g, h, b, lead, lag):
                if lead:
                    act.wait_ge(eT_ps, g + 1)
                    nc.scalar.copy(eT[:, 0:512], bank[1][0:FE, :])
                    nc.scalar.copy(eT[:, 512:GE], bank[2][0:FE, 0:GE - 512]).then_inc(eT_sb, 1)
                    need(act, b_ps, g)
                    for m in range(4):
                        act.wait_ge(hid_ps, 4 * g + m + 1)
                        c, half = m // 2, m % 2
                        nc.scalar.activation(hid[:, c, half * (GE // 2):(half + 1) * (GE // 2)],
                                             bank[3 + m % 2][:, 0:GE // 2], ACT.Relu,
                                             bias=b1c[:, c:c + 1]).then_inc(hid_sb, 1)
                    act.wait_ge(var1, g + 1)
                    nc.scalar.activation(sd[:, b, :], mv[:, b, :, 1], ACT.Sqrt, bias=epsc[:, :]).then_inc(sd1, 1)
                if lag:
                    g, h, b = lagging(g, h, b)
                    act.wait_ge(rs1, g + 1)
                    for j in range(J):
                        nc.scalar.activation(A(b * J + j), A(b * J + j), ACT.Relu, bias=nm[:, b, j:j + 1],
                                             scale=rs[:, b, j:j + 1]).then_inc(h1a, 1)
                    act.wait_ge(h1a, J * (g + 1))
                    hold(act)
                    for j in range(J):
                        nc.scalar.activation(store3[:, bass.ds(J * g + j, 1), :],
                                             A(b * J + j)[:, None, :], ACT.Copy).then_inc(h1, 1)
            turns(act, phase1)

            def phase2(g, h, b, lead, lag):
                if lead:
                    if isinstance(g, int):
                        act.wait_ge(fl_read, G)
                        act.wait_ge(lag1, 1)
                    need(act, st_q[b], 16 * h)
                    hold(act)
                    for j in range(J):
                        nc.scalar.activation(C(b * J + j)[:, None, :],
                                             store3[:, bass.ds(J * g + j, 1), :], ACT.Copy).then_inc(hs, 1)
                if lag:
                    lg, lh, lb = lagging(g, h, b)
                    act.wait_ge(rs2, lg + 1)
                    need(act, st_h[lb], 16 * lh)
                    for j in range(J):
                        u = lb * J + j
                        nc.scalar.activation(B(u), A(u), ACT.Relu, bias=nm[:, lb, j:j + 1],
                                             scale=rs[:, lb, j:j + 1]).then_inc(h2r, 1)
                    for j in range(J + 1):
                        u = lb * J + j
                        if j < J:
                            act.wait_ge(t2, J * lg + j + 1)
                            need(act, qp, J * lg + j - 1)
                            nc.scalar.copy(hT[u % 2], bank[4 + u % 2][:, 0:D]
                                           .rearrange("p (c e) -> p c e", c=NC)).then_inc(hT2, 1)
                        if j > 0:
                            act.wait_ge(qp, J * lg + j)
                            nc.scalar.copy(C(u - 1), bank[6 + (u - 1) % 2][:, 0:D]).then_inc(q2, 1)
                if lead:
                    act.wait_ge(var2, g + 1)
                    nc.scalar.activation(sd[:, b, :], mv[:, b, :, 1], ACT.Sqrt, bias=epsc[:, :]).then_inc(sd2, 1)
            turns(act, phase2)
            for i in range(2):
                act.wait_ge(st_x[i], 16 * (G // 2))

            def phase3(g, h, b, lead, lag):
                if lead:
                    need(act, t3, J * (g - 1))
                    hold(act)
                    for j in range(J):
                        nc.scalar.activation(A(b * J + j)[:, None, :],
                                             store3[:, bass.ds(J * g + j, 1), :], ACT.Copy).then_inc(c3, 1)
                if lag:
                    g, h, b = lagging(g, h, b)
                    for j in range(J + 1):
                        u = b * J + j
                        if j < J:
                            act.wait_ge(t3, J * g + j + 1)
                            need(act, kv, J * g + j - 1)
                            nc.scalar.copy(hT[u % 2], bank[4 + u % 2][:, 0:D]
                                           .rearrange("p (c e) -> p c e", c=NC)).then_inc(hT3, 1)
                        if j > 0:
                            act.wait_ge(kv, J * g + j)
                            hold(act)
                            nc.scalar.activation(store3[:, bass.ds(J * g + j - 1, 1), :],
                                                 bank[2 + (u - 1) % 2][:, None, 0:D], ACT.Copy).then_inc(v3, 1)
            turns(act, phase3)
            act.wait_ge(act_sm, 1)
            nc.scalar.activation(ex, xs, ACT.Exp).then_inc(act_sm, 1)

        @block.vector
        def _(dve):
            pro = Chain(dve, pdve)
            pro.start(0)
            nc.vector.memset(ones[:, :], 1.0)
            nc.vector.memset(epsc[:, :], EPS)
            nc.vector.memset(w_zero, 0.0)
            dve.wait_ge(s_idx, 64)
            nc.vector.tensor_copy(w_src, src_i[:, :])
            nc.vector.tensor_copy(w_dstf, dst_i[:, :])
            pro.link(nc.vector.tensor_copy(w_nxt, nxt_i[:, :]))
            pro.link(nc.vector.tensor_tensor(w_eq, w_dstf, w_nxt, ALU.is_equal))
            pro.link(nc.vector.scalar_tensor_tensor(w_fin, w_eq, SKIP, w_dstf, ALU.mult, ALU.add))
            nc.vector.tensor_copy(w_key[:, 0:P - 1], w_fin[:, 0:P - 1])
            nc.vector.tensor_copy(w_key[:, P - 1:P], w_dstf[:, P - 1:P])
            dve.wait_ge(s_cst, 2)
            for k in range(4):
                sel = ident[0:T, 0:T] if k < 2 else anti[:, :]
                endcol = w_dstf[:, 0:1] if k % 2 == 0 else w_dstf[:, P - 1:P]
                nc.vector.tensor_scalar(w_diag[:, k * T:(k + 1) * T], sel, endcol, None, ALU.mult)
            nc.vector.tensor_copy(iota1[:, :], iota_i).then_inc(s_key[0], 1)
            dve.wait_ge(s_tr, 8)
            nc.vector.tensor_copy(dcol[:, :], bank[0][:, 0:T])
            nc.vector.tensor_copy(scol[:, :], bank[0][:, T:2 * T])
            nc.vector.tensor_copy(sg_i[:, :], bank[0][:, T:2 * T])
            nc.vector.tensor_copy(wcol[:, :], bank[0][:, 2 * T:3 * T])
            nc.vector.tensor_copy(out_i[:, :], bank[0][:, 3 * T:4 * T])
            nc.vector.tensor_scalar(dg_i[:, :], bank[0][:, 0:T], float(N - 1), None, ALU.min)
            nc.vector.memset(DP[:, 0:1], -1.0)
            nc.vector.tensor_copy(DP[:, 1:T], bank[1][:, T:2 * T - 1])
            pro.link(nc.vector.tensor_copy(ends[:, :, :], bank[1][:, 0:4 * T].rearrange("p (k t) -> p k t", k=4)))
            first, last, first_r, last_r = (ends[:, k, :] for k in range(4))
            nc.vector.memset(cnt[:, 2, 0:1], 0.0)
            nc.vector.tensor_tensor(cnt[:, 0, :], first, DP[:, :], ALU.is_equal)
            nc.vector.tensor_tensor(cnt[:, 2, 1:T], last_r[:, 1:T], first_r[:, 0:T - 1], ALU.is_equal)
            nc.vector.tensor_tensor(cnt[:, 1, :], first, last, ALU.is_equal)
            pro.link(nc.vector.tensor_tensor(cnt[:, 3, :], first_r, last_r, ALU.is_equal))
            nc.vector.tensor_tensor(cnt[:, 1, :], cnt[:, 1, :], cnt[:, 0, :], ALU.mult)
            nc.vector.tensor_tensor(cnt[:, 3, :], cnt[:, 3, :], cnt[:, 2, :], ALU.mult)
            nc.vector.tensor_tensor(edge_w[:, :, 0], dcol[:, :], first, ALU.is_equal)
            pro.link(nc.vector.tensor_tensor(edge_w[:, :, 1], dcol[:, :], last, ALU.is_equal))
            pro.link(nc.vector.tensor_tensor(edge_w[:, :, :], edge_w[:, :, :],
                                             wcol[:, :, None].to_broadcast([P, T, 2]), ALU.mult))
            nc.vector.memset(carry[:, :], 0.0).then_inc(s_pro, 1)
            dve.wait_ge(s_wts, 160)

            lead_c, lag_c = Chain(dve, lead1), Chain(dve, lag1)

            def phase1(g, h, b, lead, lag):
                if lead:
                    lead_c.start(g)
                    lead_c.link(nc.vector.tensor_tensor(
                        taucmp, last[:, None, :].to_broadcast([P, J, T]),
                        scol[:, bass.ds(J * g, J)][:, :, None].to_broadcast([P, J, T]), ALU.is_lt))
                    lead_c.link(nc.vector.tensor_reduce(tauf[:, bass.ds(J * g, J)], taucmp, AX, ALU.add))
                    nc.vector.tensor_copy(taui[:, b * J:(b + 1) * J], tauf[:, bass.ds(J * g, J)]).then_inc(tau_rdy, 1)
                    dve.wait_ge(x_in[b], 16 * J * (h + 1))
                    for j in range(J):
                        ins = nc.vector.bn_stats(st6[:, j, :], A(b * J + j))
                    lead_c.link(ins)
                    for j in range(J):
                        ins = nc.vector.bn_aggr(mv[:, b, j, :], st6[:, j, :])
                    ins.then_inc(var1, 1)
                    lead_c.end()
                    bulk_bo(dve, 0, h, b)
                if lag:
                    g, h, b = lagging(g, h, b)
                    lag_c.start(g)
                    dve.wait_ge(sd1, g + 1)
                    lag_c.link(nc.vector.reciprocal(rs[:, b, :], sd[:, b, :]))
                    nc.vector.scalar_tensor_tensor(nm[:, b, :], mv[:, b, :, 0], -1.0, rs[:, b, :],
                                                   ALU.mult, ALU.mult).then_inc(rs1, 1)
                    dve.wait_ge(k_in[b], 16 * J * (h + 1))
                    for j in range(J):
                        ins = nc.vector.scalar_tensor_tensor(C(b * J + j)[:, 0:P], C(b * J + j)[:, 0:P],
                                                             scol[:, bass.ds(J * g + j, 1)], iota1[:, :],
                                                             ALU.is_equal, ALU.mult, accum_out=pm[:, j:j + 1])
                    lag_c.link(ins)
                    lag_c.link(nc.vector.tensor_scalar(pz[:, :], pm[:, :], 0.0, SKIP, ALU.is_equal, ALU.mult))
                    lag_c.link(nc.vector.scalar_tensor_tensor(pm[:, :], tauf[:, bass.ds(J * g, J)], float(P), pm[:, :],
                                                              ALU.mult, ALU.add))
                    lag_c.link(nc.vector.scalar_tensor_tensor(slot_i[:, bass.ds(J * g, J)], pm[:, :], -1.0, pz[:, :],
                                                              ALU.add, ALU.add))
                    dve.wait_ge(b_ps, g + 1)
                    nc.vector.tensor_tensor(sc_all[:, :, bass.ds(g, 1), :],
                                            bank[7][:, 0:J * H].rearrange("p (j o n) -> p j o n", o=1, n=H),
                                            b2b[:, None, None, :].to_broadcast([P, J, 1, H]), ALU.add).then_inc(b_done, 1)
                    dve.wait_ge(fl, g + 1)
                    hold(dve)
                    for c in range(NC):
                        v = bank[5 * b][:, c * 2 * J:(c + 1) * 2 * J].rearrange("p (j k) -> p k j", k=2)
                        nc.vector.tensor_copy(sums[:, 0, c, bass.ds(J * g, J)], v[:, 1, :])
                        ins = nc.vector.tensor_copy(sums[:, 1, c, bass.ds(T - J - J * g, J)], v[:, 0, ::-1])
                    ins.then_inc(fl_read, 1)
                    lag_c.end()
            turns(dve, phase1)

            cc = Chain(dve, s_carr)
            cc.start(0)
            dve.wait_ge(b_done, G)
            dve.wait_ge(fl_read, G)
            for k in range(2):
                for c in range(NC):
                    cc.link(nc.vector.tensor_tensor_scan(carr[:, k, c, :], cnt[:, 2 * k + 1, :], sums[:, k, c, :],
                                                         0.0, ALU.mult, ALU.add))
                    nc.vector.memset(sums[:, k, c, 0:1], 0.0)
                    cc.link(nc.vector.tensor_tensor(sums[:, k, c, 1:T], carr[:, k, c, 0:T - 1],
                                                    cnt[:, 2 * k, 1:T], ALU.mult))
            lead_2, lag_2 = Chain(dve, lead2), Chain(dve, lag2)

            def phase2(g, h, b, lead, lag):
                if lag:
                    lg, lh, lb = lagging(g, h, b)
                    lag_2.start(lg)
                    dve.wait_ge(sd2, lg + 1)
                    lag_2.link(nc.vector.reciprocal(rs[:, lb, :], sd[:, lb, :]))
                    nc.vector.scalar_tensor_tensor(nm[:, lb, :], mv[:, lb, :, 0], -1.0, rs[:, lb, :],
                                                   ALU.mult, ALU.mult).then_inc(rs2, 1)
                    lag_2.end()
                if lead:
                    lead_2.start(g)
                    dve.wait_ge(row_in[b], 16 * (h + 1))
                    for j in range(J):
                        nc.vector.tensor_scalar(S(b * J + j), row[b][:, j * P:(j + 1) * P],
                                                dcol[:, bass.ds(J * g + j, 1)], wcol[:, bass.ds(J * g + j, 1)],
                                                ALU.is_equal, ALU.mult).then_inc(S2, 1)
                    dve.wait_ge(xd_in[b], 16 * J * (h + 1))
                    for j in range(J + 1):
                        u = b * J + j
                        if j < J:
                            t = J * g + j
                            nc.vector.tensor_scalar(indF(u), row[b][:, j * P:(j + 1) * P],
                                                    ends[:, 0, bass.ds(t, 1)], None, ALU.is_equal)
                            lead_2.link(nc.vector.tensor_scalar(indL(u), row[b][:, j * P:(j + 1) * P],
                                                                ends[:, 1, bass.ds(t, 1)], None, ALU.is_equal))
                            dve.wait_ge(ag, t + 1)
                            need(dve, w2p, t - 1)
                            for c in range(NC):
                                ins = nc.vector.scalar_tensor_tensor(
                                    aT[u % 2][:, c, :], indF(u), sums[:, 0, c, bass.ds(t, 1)],
                                    bank[u % 2][:, c * P:(c + 1) * P], ALU.mult, ALU.add)
                            lead_2.link(ins)
                            for c in range(NC):
                                ins = nc.vector.scalar_tensor_tensor(
                                    aT[u % 2][:, c, :], indL(u), sums[:, 1, c, bass.ds(T - 1 - t, 1)],
                                    aT[u % 2][:, c, :], ALU.mult, ALU.add)
                            ins.then_inc(aT2, 1)
                        if j > 0:
                            dve.wait_ge(w2p, J * g + j)
                            ins = nc.vector.scalar_tensor_tensor(A(u - 1), bank[2 + (u - 1) % 2][:, 0:D], 0.0,
                                                                 A(u - 1), ALU.max, ALU.add)
                            ins.then_inc(x1r, 1)
                    dve.wait_ge(x1r, J * (g + 1))
                    for j in range(J):
                        ins = nc.vector.bn_stats(st6[:, j, :], A(b * J + j))
                    lead_2.link(ins)
                    for j in range(J):
                        ins = nc.vector.bn_aggr(mv[:, b, j, :], st6[:, j, :])
                    ins.then_inc(var2, 1)
                    lead_2.end()
                    bulk_bo(dve, G, h, b)
            turns(dve, phase2)
            lag_3 = Chain(dve, lag3)

            def phase3(g, h, b, lead, lag):
                if lead:
                    bulk_bo(dve, 2 * G, h, b)
                if lag:
                    g, h, b = lagging(g, h, b)
                    lag_3.start(g)
                    dve.wait_ge(ql[b], 16 * (h + 1))
                    for j in range(J):
                        u = b * J + j
                        dve.wait_ge(kv, J * g + j + 1)
                        nc.vector.tensor_tensor(prod[:, j, :], bank[6 + u % 2][:, 0:D], C(u), ALU.mult).then_inc(k3, 1)
                    dve.wait_ge(k3, J * (g + 1))
                    lag_3.link(nc.vector.tensor_reduce(ssum[:, :], Sr[:, :].rearrange("p (k e) -> p k e", e=HD), AX, ALU.add))
                    v = sc_all[:, :, bass.ds(g, 1), :]
                    nc.vector.scalar_tensor_tensor(v, ssum[:, :].rearrange("p (j o n) -> p j o n", o=1, n=H),
                                                   float(1.0 / np.sqrt(HD)), v, ALU.mult, ALU.add).then_inc(x_sb, 1)
                    lag_3.end()
            turns(dve, phase3)
            last_k = BULK - 1
            dve.wait_ge(bulk_ld[0], 16 * (last_k // 2 + 1))
            v = bulk[0][:, :].rearrange("p (r d) -> p r d", d=D)
            nc.vector.tensor_tensor(v, v, bob[:, None, :].to_broadcast([P, BR, D]), ALU.add).then_inc(bulk_add, 1)
            dve.wait_ge(bulk_ld[1], 16 * (last_k // 2 + 2))
            v = bulk[1][:, 0:REST * D].rearrange("p (r d) -> p r d", d=D)
            nc.vector.tensor_tensor(v, v, bob[:, None, :].to_broadcast([P, REST, D]), ALU.add).then_inc(bulk_add, 1)
            v = bulk[1][0:TAIL, REST * D:(REST + 1) * D]
            nc.vector.tensor_tensor(v, v, bob[0:TAIL, :], ALU.add).then_inc(bulk_add, 1)

            sm = Chain(dve, s_sm)
            sm.start(0)
            dve.wait_ge(s_flag, 32)
            dve.wait_ge(x_ps, 2)
            nc.vector.tensor_scalar(f_neg, f_cont, -1.0, BIG, ALU.add, ALU.mult)
            nc.vector.tensor_scalar(f_last, f_next, -1.0, 1.0, ALU.mult, ALU.add)
            nc.vector.tensor_reduce(whole[:, 0:1], f_cont, AX, ALU.min)
            nc.vector.tensor_reduce(whole[:, 1:2], f_next, AX, ALU.min)
            nc.vector.tensor_copy(xs[:, 0:512], bank[0][0:GH, :])
            sm.link(nc.vector.tensor_copy(xs[:, 512:GE], bank[1][0:GH, 0:GE - 512]))
            passes = [0]

            def across(end, k, is_max, backward):
                nc.vector.tensor_copy(carry[:, :], end)
                sm.link(nc.vector.tensor_copy(ssum[0:GH, 0:1], whole[:, k:k + 1]))
                nc.vector.engine_nop().then_inc(pe_sm, 1)
                passes[0] += 1
                dve.wait_ge(al_ps, 2 * passes[0] - 1)
                for i in range(2):
                    v = bank[2][0:1, i * GH:(i + 1) * GH].rearrange("o (g n) -> o n g", n=H)
                    if backward:
                        v = v[:, :, ::-1]
                    ins = nc.vector.tensor_copy(lin[:, i, :].rearrange("o (n g) -> o n g", n=H), v)
                sm.link(ins)
                heads = lin[:, 1, :].rearrange("o (n g) -> o n g", n=H)
                sm.link(nc.vector.memset(heads[:, :, 0:1], 0.0))
                if is_max:
                    sm.link(nc.vector.tensor_scalar(lin[:, 1, :], lin[:, 1, :], -1.0, BIG, ALU.add, ALU.mult))
                    sm.link(nc.vector.tensor_tensor_scan(lin[:, 2, :], lin[:, 1, :], lin[:, 0, :], -BIG, ALU.add, ALU.max))
                else:
                    sm.link(nc.vector.tensor_tensor_scan(lin[:, 2, :], lin[:, 1, :], lin[:, 0, :], 0.0, ALU.mult, ALU.add))
                res = lin[:, 2, :].rearrange("o (n g) -> o n g", n=H)
                dst_v = lin[:, 3, :].rearrange("o (g n) -> o n g", n=H)
                if backward:
                    dst_v = dst_v[:, :, ::-1]
                nc.vector.memset(dst_v[:, :, 0:1], -BIG if is_max else 0.0)
                sm.link(nc.vector.tensor_copy(dst_v[:, :, 1:G], res[:, :, 0:G - 1]))
                nc.vector.engine_nop().then_inc(pe_sm, 1)
                dve.wait_ge(al_ps, 2 * passes[0])
                sm.link(nc.vector.tensor_copy(carry[:, :], bank[3][0:GH, 0:1]))

            def to_all(total):
                sm.link(nc.vector.tensor_tensor(tmp, total, f_last, ALU.mult))
                sm.link(nc.vector.tensor_tensor_scan(spread[:, ::-1], f_next[:, ::-1], tmp[:, ::-1], 0.0, ALU.mult, ALU.add))
                across(spread[:, 0:1], 1, False, True)
                sm.link(nc.vector.tensor_tensor_scan(spread[:, ::-1], f_next[:, ::-1], tmp[:, ::-1], carry[:, :], ALU.mult, ALU.add))

            sm.link(nc.vector.tensor_tensor_scan(fwd, f_neg, xs, -BIG, ALU.add, ALU.max))
            across(fwd[:, GE - 1:GE], 0, True, False)
            sm.link(nc.vector.tensor_tensor_scan(fwd, f_neg, xs, carry[:, :], ALU.add, ALU.max))
            to_all(fwd)
            nc.vector.tensor_tensor(xs, xs, spread, ALU.subtract).then_inc(act_sm, 1)
            dve.wait_ge(act_sm, 2)
            sm.link(nc.vector.tensor_tensor_scan(fwd, f_cont, ex, 0.0, ALU.mult, ALU.add))
            across(fwd[:, GE - 1:GE], 0, False, False)
            sm.link(nc.vector.tensor_tensor_scan(fwd, f_cont, ex, carry[:, :], ALU.mult, ALU.add))
            to_all(fwd)
            sm.link(nc.vector.reciprocal(tmp, spread))
            sm.link(nc.vector.tensor_tensor(xs, ex, tmp, ALU.mult))
            nc.vector.engine_nop().then_inc(pe_sm, 1)
            dve.wait_ge(al_ps, 2 * passes[0] + 1)
            nc.vector.memset(aT[1], 0.0)
            nc.vector.tensor_copy(sc_all[:, 0:4, :, :], bank[4][:, 0:4 * GH].rearrange("p (j g n) -> p j g n", j=4, n=H))
            sm.link(nc.vector.tensor_copy(sc_all[:, 4:J, :, :], bank[5][:, 0:3 * GH].rearrange("p (j g n) -> p j g n", j=3, n=H)))
            nc.vector.engine_nop().then_inc(s_al, 1)

            lag_4 = Chain(dve, lag4)

            def phase4(g, h, b, lead, lag):
                if lead:
                    dve.wait_ge(row4[b], 16 * (h + 1))
                    for j in range(J):
                        u = b * J + j
                        nc.vector.tensor_scalar(S(u), row[b][:, j * P:(j + 1) * P],
                                                dcol[:, bass.ds(J * g + j, 1)], None, ALU.is_equal)
                        al = sc_all[:, j, bass.ds(g, 1), :].rearrange("p o n -> p n o").to_broadcast([P, H, HD])
                        nc.vector.tensor_tensor(A(u).rearrange("p (n e) -> p n e", n=H),
                                                store[:, bass.ds((J * g + j) * D, D)].rearrange("p (n e) -> p n e", n=H),
                                                al, ALU.mult).then_inc(s4, 1)
                if lag:
                    g, h, b = lagging(g, h, b)
                    lag_4.start(g)
                    dve.wait_ge(x4[b], 16 * (h + 1))
                    for j in range(J + 1):
                        u = b * J + j
                        if j < J:
                            t = J * g + j
                            lag_4.link(nc.vector.tensor_scalar(indF(u), row[b][:, j * P:(j + 1) * P],
                                                               DP[:, bass.ds(t, 1)], None, ALU.is_equal))
                            dve.wait_ge(ag4, t + 1)
                            need(dve, wo, t - 1)
                            need(dve, aT4, t)
                            for c in range(NC):
                                ins = nc.vector.scalar_tensor_tensor(
                                    aT[u % 2][:, c, :], indF(u), aT[(u + 1) % 2][:, c, P - 1:P],
                                    bank[u % 2][:, c * P:(c + 1) * P], ALU.mult, ALU.add)
                            ins.then_inc(aT4, 1)
                        if j > 0:
                            dve.wait_ge(wo, J * g + j)
                            nc.vector.tensor_tensor(B(u - 1), bank[2 + (u - 1) % 2][:, 0:D], B(u - 1),
                                                    ALU.add).then_inc(o4, 1)
                    lag_4.end()
            turns(dve, phase4)

        @block.tensor
        def _(pe):
            def mm(o, lhsT, rhs, start=True, stop=True):
                return nc.tensor.matmul(o, lhsT, rhs, start=start, stop=stop)

            pe.wait_ge(s_key[0], 1)
            for k, r in enumerate((w_dstf, w_src, w_r[:, :], w_fin)):
                nc.tensor.transpose(bank[0][:, k * T:(k + 1) * T], r, ident[0:T, 0:T]).then_inc(s_tr, 1)
            for k in range(4):
                mm(bank[1][:, k * T:(k + 1) * T], ones[0:T, :], w_diag[:, k * T:(k + 1) * T]).then_inc(s_tr, 1)
            pe.wait_ge(s_wts, 160)
            pe.wait_ge(s_pro, 1)

            def phase1(g, h, b, lead, lag):
                if lead:
                    pe.wait_ge(ef_in[b], 16 * (h + 1))
                    need(pe, eT_sb, g)
                    hold(pe)
                    for j in range(J):
                        ins = nc.tensor.transpose(bank[1 + j // 4][0:FE, (j % 4) * P:(j % 4 + 1) * P],
                                                  ef[b][:, j * FE:(j + 1) * FE], ident[:, :])
                    ins.then_inc(eT_ps, 1)
                    pe.wait_ge(eT_sb, g + 1)
                    for m in range(4):
                        c, half = m // 2, m % 2
                        need(pe, hid_sb, 4 * g + m - 1)
                        mm(bank[3 + m % 2][:, 0:GE // 2], W1sb[:, c * P:(c + 1) * P],
                           eT[:, half * (GE // 2):(half + 1) * (GE // 2)]).then_inc(hid_ps, 1)
                    pe.wait_ge(hid_sb, 4 * g + 4)
                    need(pe, b_done, g)
                    for j in range(J):
                        for c in range(NC):
                            ins = mm(bank[7][:, j * H:(j + 1) * H], hid[:, c, j * P:(j + 1) * P], W2sb[:, c, :],
                                     start=(c == 0), stop=(c == NC - 1))
                    ins.then_inc(b_ps, 1)
                if lag:
                    g, h, b = lagging(g, h, b)
                    need(pe, fl_read, g - 1)
                    for j in range(J):
                        pe.wait_ge(h1, J * g + j + 1)
                        for c in range(NC):
                            o = c * 2 * J + 2 * j
                            ins = mm(bank[5 * b][:, o:o + 2], A(b * J + j)[:, c * P:(c + 1) * P],
                                     edge_w[:, bass.ds(J * g + j, 1), :].rearrange("p o k -> p (o k)"))
                    ins.then_inc(fl, 1)
            turns(pe, phase1)
            pe.wait_ge(fl_read, G)

            def phase2(g, h, b, lead, lag):
                lg, lh, lb = lagging(g, h, b)
                for j in range(J + 1):
                    u, lu = b * J + j, lb * J + j
                    if lead and j < J:
                        t = J * g + j
                        pe.wait_ge(S2, t + 1)
                        pe.wait_ge(hs, t + 1)
                        need(pe, aT2, t - 1)
                        for c in range(NC):
                            ins = mm(bank[u % 2][:, c * P:(c + 1) * P], C(u)[:, c * P:(c + 1) * P], S(u))
                        ins.then_inc(ag, 1)
                    if lag and j < J:
                        t = J * lg + j
                        pe.wait_ge(h2r, t + 1)
                        need(pe, hT2, t - 1)
                        for c in range(NC):
                            ins = nc.tensor.transpose(bank[4 + lu % 2][:, c * P:(c + 1) * P],
                                                      B(lu)[:, c * P:(c + 1) * P], ident[:, :])
                        ins.then_inc(t2, 1)
                    if lead and j > 0:
                        t, v = J * g + j - 1, u - 1
                        pe.wait_ge(aT2, t + 1)
                        need(pe, x1r, t - 1)
                        for c in range(NC):
                            ins = mm(bank[2 + v % 2][:, 0:D], aT[v % 2][:, c, :], Wsb[:, c, :],
                                     start=(c == 0), stop=(c == NC - 1))
                        ins.then_inc(w2p, 1)
                    if lag and j > 0:
                        t, v = J * lg + j - 1, lu - 1
                        pe.wait_ge(hT2, t + 1)
                        need(pe, q2, t - 1)
                        for c in range(NC):
                            ins = mm(bank[6 + v % 2][:, 0:D], hT[v % 2][:, c, :], Wqsb[:, c, :],
                                     start=(c == 0), stop=(c == NC - 1))
                        ins.then_inc(qp, 1)
            turns(pe, phase2)
            pe.wait_ge(q2, T)

            def phase3(g, h, b, lead, lag):
                if lag:
                    g, h, b = lagging(g, h, b)
                    pe.wait_ge(o_in[b], 16 * J * (h + 1))
                    for j in range(J + 1):
                        u = b * J + j
                        if j < J:
                            t = J * g + j
                            need(pe, hT3, t - 1)
                            for c in range(NC):
                                ins = nc.tensor.transpose(bank[4 + u % 2][:, c * P:(c + 1) * P],
                                                          A(u)[:, c * P:(c + 1) * P], ident[:, :])
                            ins.then_inc(t3, 1)
                        if j > 0:
                            t, v = J * g + j - 1, u - 1
                            pe.wait_ge(hT3, t + 1)
                            need(pe, k3, t - 1)
                            need(pe, v3, t - 1)
                            for c in range(NC):
                                mm(bank[6 + v % 2][:, 0:D], hT[v % 2][:, c, :], Wkv[:, c, 0:D],
                                   start=(c == 0), stop=(c == NC - 1))
                                ins = mm(bank[2 + v % 2][:, 0:D], hT[v % 2][:, c, :], Wkv[:, c, D:2 * D],
                                         start=(c == 0), stop=(c == NC - 1))
                            ins.then_inc(kv, 1)
            turns(pe, phase3)
            pe.wait_ge(x_sb, G)
            pe.wait_ge(v3, T)
            for j in range(J):
                ins = nc.tensor.transpose(bank[j // 4][0:GH, (j % 4) * P:(j % 4 + 1) * P],
                                          sc_all[:, j, :, :].rearrange("p g n -> p (g n)"), ident[:, :])
                if j in (3, J - 1):
                    ins.then_inc(x_ps, 1)
            for k in range(4):
                pe.wait_ge(pe_sm, 2 * k + 1)
                mm(bank[2][0:1, 0:GH], carry[:, :], ident[0:GH, 0:GH])
                mm(bank[2][0:1, GH:2 * GH], ssum[0:GH, 0:1], ident[0:GH, 0:GH]).then_inc(al_ps, 1)
                pe.wait_ge(pe_sm, 2 * k + 2)
                mm(bank[3][0:GH, 0:1], lin[:, 3, :], ones[0:1, 0:1]).then_inc(al_ps, 1)
            pe.wait_ge(pe_sm, 9)
            for j in range(J):
                ins = nc.tensor.transpose(bank[4 + j // 4][:, (j % 4) * GH:(j % 4 + 1) * GH],
                                          xs[:, j * P:(j + 1) * P], ident[0:GH, 0:GH])
            ins.then_inc(al_ps, 1)

            def phase4(g, h, b, lead, lag):
                if lag:
                    g, h, b = lagging(g, h, b)
                    for j in range(J + 1):
                        u = b * J + j
                        if j < J:
                            t = J * g + j
                            pe.wait_ge(s4, t + 1)
                            need(pe, aT4, t - 1)
                            for c in range(NC):
                                ins = mm(bank[u % 2][:, c * P:(c + 1) * P], A(u)[:, c * P:(c + 1) * P], S(u))
                            ins.then_inc(ag4, 1)
                        if j > 0:
                            t, v = J * g + j - 1, u - 1
                            pe.wait_ge(aT4, t + 1)
                            need(pe, o4, t - 1)
                            for c in range(NC):
                                ins = mm(bank[2 + v % 2][:, 0:D], aT[v % 2][:, c, :], Wosb[:, c, :],
                                         start=(c == 0), stop=(c == NC - 1))
                            ins.then_inc(wo, 1)
            turns(pe, phase4)


def kernel(**inputs):
    import numpy as _np
    import concourse.bacc as _bacc
    from concourse import mybir as _mybir
    from concourse.bass_utils import run_bass_kernel_spmd as _run

    a = {k: _np.ascontiguousarray(v) for k, v in inputs.items()}
    pad = EP - E
    dst = _np.full(EP + 1, PAD_DST, a['dst'].dtype)
    dst[0:E] = a['dst']
    dst[EP] = -1
    src = _np.zeros(EP, a['src'].dtype)
    src[0:E] = a['src']
    wgt = _np.zeros(EP, a['edge_weight'].dtype)
    wgt[0:E] = a['edge_weight']
    eattr = _np.zeros((EP, FE), a['edge_attr_64'].dtype)
    eattr[0:E] = a['edge_attr_64']
    arrays = {'x': a['x'], 'dst': dst, 'src': src, 'wgt': wgt, 'eattr': eattr, 'W': a['L0_gnn_weight']}
    for n in ('Wq', 'Wk', 'Wv', 'W1', 'b1', 'W2', 'b2', 'Wo', 'bo'):
        arrays[n] = a['L1_gnn_' + n]
    nc = _bacc.Bacc("TRN2", target_bir_lowering=False, num_devices=1)
    arrays = {'in_' + k: v for k, v in arrays.items()}
    args = [nc.dram_tensor(k, v.shape, _mybir.dt.from_np(v.dtype), kind="ExternalInput").ap() for k, v in arrays.items()]
    out = nc.dram_tensor("out_x", (N, D), _mybir.dt.float32, kind="ExternalOutput").ap()
    gnn_program(nc, *args, out)
    r = _run(nc, [arrays], core_ids=[0])
    return r.results[0]["out_x"]
```

```python
import concourse.bass as bass
import numpy as np
from concourse import mybir
from contextlib import ExitStack

N, E, D, H, FE = 50000, 12500, 256, 8, 64
HD = D // H
P = 128
J = 7
T = -(-E // P)
G = T // J
EP = T * P
GE = J * P
NC = D // P
GH = G * H
EPS = 1e-5
BIG = 1e30
PAD_DST = 65535
SKIP = 1000000.0
BR = 9
NROW = N // P
BULK = NROW // BR
REST = NROW - BULK * BR
TAIL = N - NROW * P
PARTS = ((0, 4), (4, J))


def gnn_program(nc, x, dst, src, wgt, eattr, W, Wq, Wk, Wv, W1, b1, W2, b2, Wo, bo, out):
    f32 = mybir.dt.float32
    i32 = mybir.dt.int32
    ALU = mybir.AluOpType
    ACT = mybir.ActivationFunctionType
    AX = mybir.AxisListType.X

    x1_d = nc.dram_tensor("x1_bo", (EP, D), f32, kind="Internal").ap()
    h2_d = nc.dram_tensor("h2", (EP, D), f32, kind="Internal").ap()
    q_d = nc.dram_tensor("q", (EP, D), f32, kind="Internal").ap()
    dstf_d = nc.dram_tensor("dst_f", (T, P), f32, kind="Internal").ap()
    srcf_d = nc.dram_tensor("src_f", (T, P), f32, kind="Internal").ap()
    sums_d = nc.dram_tensor("end_sums", (T, 2 * D), f32, kind="Internal").ap()
    bias_d = nc.dram_tensor("bias_t", (G, H, GE), f32, kind="Internal").ap()
    cont_d = nc.dram_tensor("cont", (EP + 1,), f32, kind="Internal").ap()

    ctx = ExitStack()
    with ctx:
        def sb(name, shape, dt=f32):
            return ctx.enter_context(nc.sbuf_tensor(name, shape, dt))

        def pb(name, shape, dt=f32):
            return ctx.enter_context(nc.psum_tensor(name, shape, dt))

        def sem(name):
            return ctx.enter_context(nc.semaphore(name))

        def sem2(name):
            return [sem(name + "_0"), sem(name + "_1")]

        store = sb("store", [P, T * D])
        ringA = sb("ringA", [P, 2 * J * D])
        ringB = sb("ringB", [P, 2 * J * D])
        ringC = sb("ringC", [P, 2 * J * D])
        bulk = [sb(f"bulk{i}", [P, BR * D]) for i in range(2)]
        Wsb, Wqsb, Wosb = (sb(n, [P, NC, D]) for n in ("W_sb", "Wq_sb", "Wo_sb"))
        Wkv = sb("Wkv_sb", [P, NC, 2 * D])
        W1sb = sb("W1_sb", [FE, D])
        W2sb = sb("W2_sb", [P, NC, H])
        b1c = sb("b1_col", [P, NC])
        b2c = sb("b2_col", [H, 1])
        bob = sb("bo_all", [P, D])
        ident = sb("ident", [P, P])
        ones = sb("ones", [P, P])
        iota1 = sb("iota1", [P, P])
        epsc = sb("eps", [P, 1])
        rows = sb("rows", [P, 2 * GE])
        Sr = sb("Sr", [P, 2 * GE])
        small = sb("small", [P, 4 * D])
        ind = sb("ind", [P, 4 * P])
        scol = sb("src_col", [P, T])
        dg_i = sb("dst_gather", [P, T], i32)
        sg_i = sb("src_gather", [P, T], i32)
        out_i = sb("out_scatter", [P, T], i32)
        slot_i = sb("slot_gather", [P, T], i32)
        tauf = sb("tau", [P, T])
        per_tile = sb("per_tile", [P, 9, T])
        here = sb("here", [P, 2, 9, J])
        al_here = sb("al_here", [P, 2, J, H])
        ends_r = sb("ends_r", [P, 2, T])
        pick = sb("pick", [P, J, J, 2])
        pick_w = sb("pick_w", [P, 2, J, J, 2])
        cnt = sb("cnt", [P, 4, T])
        edge_w = sb("edge_w", [P, T, 2])
        sc_all = sb("scores", [P, J, G, H])
        st6 = sb("st6", [P, J, 6])
        mv = sb("mv", [P, 2, J, 2])
        sd = sb("sd", [P, 2, J])
        rs = sb("rs", [P, 2, J])
        nm = sb("nm", [P, 2, J])
        pm = sb("pm", [P, J])
        pz = sb("pz", [P, J])
        ist = sb("ist", [P, 2 * J], i32)
        last_before = sb("last_before", [P, 1])
        ssum = sb("ssum", [P, J * H])
        col = sb("col", [GH, 4])
        carry = sb("carry", [GH, 2])

        dcol, wcol, first, last, DP = (per_tile[:, k, :] for k in range(5))
        store3 = store[:, :].rearrange("p (t d) -> p t d", d=D)
        aT = [small[:, i * D:(i + 1) * D].rearrange("p (c e) -> p c e", c=NC) for i in range(2)]
        hT = [small[:, (2 + i) * D:(3 + i) * D].rearrange("p (c e) -> p c e", c=NC) for i in range(2)]
        taucmp = small[:, 0:J * T].rearrange("p (j t) -> p j t", t=T)
        hid = Sr[:, :].rearrange("p (c e) -> p c e", c=NC)
        eT = rows[0:FE, 0:GE]
        ef = [rows[:, GE + i * J * FE:GE + (i + 1) * J * FE] for i in range(2)]
        row = [rows[:, i * GE:(i + 1) * GE] for i in range(2)]
        prod = Sr[:, :].rearrange("p (j d) -> p j d", d=D)

        w_dstf, w_src, w_nxt, w_eq, w_fin, w_key = (ringB[0:T, k * P:(k + 1) * P] for k in range(6))
        w_zero = ringB[0:1, 6 * P:6 * P + 1]
        key_step = ringB[0:T, 15 * P:16 * P]
        w_diag = ringB[0:T, 7 * P:7 * P + 4 * T]
        anti = ringB[0:T, 14 * P:14 * P + T]
        diff = ringB[0:T, 20 * P:20 * P + T]
        dst_i, nxt_i, src_i = (ringB[0:T, k * P:(k + 1) * P].bitcast(i32) for k in (16, 17, 18))
        w_r = ringB[0:T, 19 * P:20 * P]
        iota_i = ringB[:, 12 * P:13 * P].bitcast(i32)
        src_row = [ringC[0:T, i * GE:(i + 1) * GE] for i in range(2)]
        above = [ringC[0:T, (2 + i) * GE:(3 + i) * GE] for i in range(2)]
        biasT = [ringB[0:H, i * GE:(i + 1) * GE] for i in range(2)]
        end_sums = [ringB[0:2 * J, (20 + 2 * i) * P:(22 + 2 * i) * P] for i in range(2)]
        sums_in = ringB[0:T, 24 * P:28 * P]
        sums = ringB[:, 0:4 * T].rearrange("p (m c t) -> p m c t", m=2, c=NC)
        carr = ringB[:, 14 * P:14 * P + 4 * T].rearrange("p (m c t) -> p m c t", m=2, c=NC)
        bias_all = rows[0:GH, 0:GE]
        f_cont, f_next, neg_cont, neg_next = (ringB[0:GH, k * GE:(k + 1) * GE] for k in range(4))
        xs, fwd, bwd, total = (ringC[0:GH, k * GE:(k + 1) * GE] for k in range(4))
        ex = ringA[0:GH, 0:GE]
        lin_in = small[0:1, 0:4 * GH].rearrange("o (k r) -> o k r", k=4)
        lin_out = small[0:1, 4 * GH:6 * GH].rearrange("o (k r) -> o k r", k=2)
        lin_carry = small[0:1, 6 * GH:8 * GH].rearrange("o (k r) -> o k r", k=2)

        def indF(u):
            return ind[:, (u % 2) * P:(u % 2 + 1) * P]

        def indL(u):
            return ind[:, (2 + u % 2) * P:(3 + u % 2) * P]

        def keys_ps(j):
            return bank[5 + j // 4 * 2][:, (j % 4) * P:(j % 4 + 1) * P]

        def runs_on(u):
            return bulk[0][:, u * P:(u + 1) * P]

        def S(u):
            return Sr[:, u * P:(u + 1) * P]

        def A(u):
            return ringA[:, u * D:(u + 1) * D]

        def B(u):
            return ringB[:, u * D:(u + 1) * D]

        def C(u):
            return ringC[:, u * D:(u + 1) * D]

        def group(ring, b):
            return ring[:, b * J * D:(b + 1) * J * D].rearrange("p (j d) -> p j d", d=D)

        bank = [pb(f"bank{i}", [P, 512]) for i in range(8)]
        bias_ps = [bank[6][0:H, 0:GE // 2], bank[2][0:H, 0:GE // 2]]

        s_idx, s_wts = sem("index_rows_in"), sem("weights_in")
        s_cst, s_cst2 = sem("constants"), sem("constants_step")
        s_key = sem("rows_for_dram"), sem("rows_in_dram")
        s_tr, s_diag = sem("columns_in_psum"), sem("diagonals")
        s_pro = sem("columns_ready")
        pdve = sem("dve_prologue")
        ef_in, x_in, sr_in = sem2("ef_in"), sem2("xsrc_in"), sem2("src_rows_in")
        eT_ps, eT_sb, hid_ps, hid_sb = sem("eT_in_psum"), sem("eT_in_sbuf"), sem("hid_in_psum"), sem("hid_in_sbuf")
        b_ps, b_done = sem("bias_in_psum"), sem("bias_read")
        var1, sd1, rs1, h1a, h1, fl, fl_read = (sem(n) for n in (
            "var1", "sd1", "rstd1", "h1_written", "h1_stored", "end_sums_in_psum", "unused_fl"))
        abv, keys, cp = sem("above_ready"), sem("keys_in_psum"), sem("pool_index_copied")
        lead1, lag1 = sem("dve_lead1"), sem("dve_lag1")
        bulk_ld, bulk_st = sem2("bulk_loaded"), sem2("bulk_stored")
        bulk_add, bulk_rest = sem("bulk_added"), sem("bulk_rest_added")
        s_carr = sem("dve_carries")
        st_b, st_s, bT_sb, fl_sb, pk = sem2("bias_stored"), sem2("end_sums_stored"), sem("biasT_ready"), sem("end_sums_ready"), sem("pick_ready")
        s_sums, s_bias, sumsT = sem("end_sums_loaded"), sem("bias_loaded"), sem("sumsT_in_psum")
        row_in, xd_in = sem2("rows_in"), sem2("xdst_in")
        hs, S2, ag, aT2, w2p, x1r = (sem(n) for n in (
            "h_copied", "S_ready", "agg_in_psum", "aggT_ready", "l0_in_psum", "x1_ready"))
        var2, sd2, rs2, h2r, t2, hT2, qp, q2, bo4 = (sem(n) for n in (
            "var2", "sd2", "rstd2", "h2_ready", "h2T_in_psum", "h2T_ready", "q_in_psum", "q_ready", "bo_added"))
        st_x = [sem2("x1_stored_part0"), sem2("x1_stored_part1")]
        st_h, st_q = sem2("h2_stored"), sem2("q_stored_part")
        fetched2, fetched4 = sem("per_tile_fetched2"), sem("per_tile_fetched4")
        lead2, lag2 = sem("dve_lead2"), sem("dve_lag2")
        c3, t3, hT3, kv, v3, k3 = (sem(n) for n in (
            "hsrc_copied", "hsrcT_in_psum", "hsrcT_ready", "kv_in_psum", "v_stored", "k_used"))
        o_in, ql = sem2("h2_overlaid"), sem2("q_loaded")
        lag3 = sem("dve_lag3")
        s_flag, x_ps, x_sb, s_sm, pe_sm, act_sm, al_ps, s_al = (sem(n) for n in (
            "flags_in", "scoresT_in_psum", "scoresT_ready", "dve_softmax", "pe_softmax", "act_softmax",
            "alpha_in_psum", "alpha_ready"))
        row4, x4 = sem2("rows4_in"), sem2("x1_loaded")
        s4, ag4, aT4, wo, o4 = (sem(n) for n in (
            "weighted_v_ready", "attn_in_psum", "attnT_ready", "wo_in_psum", "out_rows_ready"))
        lag4, sc_out, slots_done = sem("carry_mark_ready"), sem2("rows_scattered"), sem("slots_ready")

        def need(eng, s, value):
            if isinstance(value, int) and value <= 0:
                return
            eng.wait_ge(s, value)

        def hold(eng):
            eng.nop(nofuse=True)

        class Chain:

            def __init__(self, eng, s):
                self.eng, self.s, self.per, self.n = eng, s, None, 0

            def start(self, g):
                self.base = 0 if self.per is None else g * self.per
                self.n = 0

            def link(self, ins):
                self.n += 1
                ins.then_inc(self.s, 1)
                self.eng.wait_ge(self.s, self.base + self.n)
                if not isinstance(self.base, int):
                    hold(self.eng)

            def mark(self, ins):
                self.n += 1
                ins.then_inc(self.s, 1)
                return self.base + self.n

            def wait(self, value):
                self.eng.wait_ge(self.s, value)
                if not isinstance(value, int):
                    hold(self.eng)

            def end(self):
                assert self.per in (None, self.n)
                self.per = self.n

        def turns(eng, turn, ahead=0, behind=1):
            first = 2 + behind // 2 * 2
            pairs = (G - ahead - first) // 2

            def peeled(g):
                turn(g, g // 2, g % 2, lambda k: 0 <= g - k < G)
            for g in range(-ahead, first):
                peeled(g)
            with eng.Fori(first // 2, first // 2 + pairs) as h:
                turn(2 * h, h, 0, lambda k: True)
                turn(2 * h + 1, h, 1, lambda k: True)
            for g in range(first + 2 * pairs, G + behind):
                peeled(g)

        def behind(k, g, h, b):
            return g - k, h + (b - k) // 2, (b - k) % 2

        def edge_rows(dram, g):
            return dram.rearrange("(t p) d -> p t d", p=P)[:, bass.ds(g * J, J), :]

        xb = x[0:NROW * P, :].rearrange("(p n) d -> p (n d)", p=P)
        ob = out[0:NROW * P, :].rearrange("(p n) d -> p (n d)", p=P)

        def bulk_io(sp, base, g, h, b):
            need(sp, bulk_st[b], 16 * (base // 2 + h) if not (base == 0 and isinstance(h, int)) else 16 * h)
            sp.dma_start(bulk[b][:, :], xb[:, bass.ds((base + g) * (BR * D), BR * D)]).then_inc(bulk_ld[b], 16)
            if not (isinstance(g, int) and base + g == 0):
                sp.wait_ge(bulk_add, base + g)
                sp.dma_start(ob[:, bass.ds((base + g - 1) * (BR * D), BR * D)],
                             bulk[1 - b][:, :]).then_inc(bulk_st[1 - b], 16)

        def bulk_bo(pool, base, h, b):
            pool.wait_ge(bulk_ld[b], 16 * (base // 2 + h + 1))
            v = bulk[b][:, :].rearrange("p (r d) -> p r d", d=D)
            nc.gpsimd.tensor_tensor(v, v, bob[:, None, :].to_broadcast([P, BR, D]), ALU.add).then_inc(bulk_add, 1)

        block = ctx.enter_context(nc.Block())

        @block.sync
        def _(sp):
            sp.dma_start(dst_i[:, :], dst[0:EP].rearrange("(t p) -> t p", p=P)).then_inc(s_idx, 16)
            sp.dma_start(nxt_i[:, :], dst[1:EP + 1].rearrange("(t p) -> t p", p=P)).then_inc(s_idx, 16)
            sp.dma_start(src_i[:, :], src.rearrange("(t p) -> t p", p=P)).then_inc(s_idx, 16)
            sp.dma_start(w_r[:, :], wgt.rearrange("(t p) -> t p", p=P)).then_inc(s_idx, 16)
            for m, sbuf in ((W, Wsb), (Wq, Wqsb), (Wo, Wosb), (W2, W2sb)):
                sp.dma_start(sbuf[:, :, :], m.rearrange("(c p) n -> p c n", p=P)).then_inc(s_wts, 16)
            sp.dma_start(Wkv[:, :, 0:D], Wk.rearrange("(c p) n -> p c n", p=P)).then_inc(s_wts, 16)
            sp.dma_start(Wkv[:, :, D:2 * D], Wv.rearrange("(c p) n -> p c n", p=P)).then_inc(s_wts, 16)
            sp.dma_start(W1sb[:, :], W1).then_inc(s_wts, 16)
            sp.dma_start(b1c[:, :], b1.rearrange("(c p) -> p c", p=P), allow_slow_non_contiguous=True).then_inc(s_wts, 16)
            sp.dma_start(b2c[:, :], b2.rearrange("(n o) -> n o", o=1), allow_slow_non_contiguous=True).then_inc(s_wts, 16)
            sp.dma_start(bob[:, :], bo[None, :].to_broadcast([P, D])).then_inc(s_wts, 16)
            sp.wait_ge(s_key[0], 1)
            sp.dma_start(dstf_d, w_dstf[:, :]).then_inc(s_key[1], 16)
            sp.dma_start(srcf_d, w_src).then_inc(s_key[1], 16)
            sp.dma_start(cont_d[1:EP + 1].rearrange("(t p) -> t p", p=P), w_eq[:, :]).then_inc(s_key[1], 16)
            sp.dma_start(cont_d[0:1].rearrange("(a b) -> a b", a=1), w_zero[0:1, 0:1]).then_inc(s_key[1], 16)

            def phase1(g, h, b, on):
                if on(-1):
                    a, _, ab = behind(-1, g, h, b)
                    need(sp, eT_ps, a - 1)
                    sp.dma_start(ef[ab].rearrange("p (j f) -> p j f", f=FE),
                                 edge_rows(eattr, a)).then_inc(ef_in[ab], 16)
                    if isinstance(a, int) and a == 0:
                        sp.wait_ge(s_key[1], 64)
                    need(sp, abv, a - 1)
                    sp.dma_start(src_row[ab], srcf_d.rearrange("t p -> (t p)")[bass.ds(a * GE, GE)][None, :]
                                 .to_broadcast([T, GE])).then_inc(sr_in[ab], 16)
                if on(0):
                    bulk_io(sp, 0, g, h, b)
                if on(1):
                    l, _, lb = behind(1, g, h, b)
                    sp.wait_ge(bT_sb, 2 * l + 2)
                    sp.dma_start(bias_d[bass.ds(l, 1)].rearrange("o n e -> (o n) e"), biasT[lb]).then_inc(st_b[lb], 16)
                if on(2):
                    l, _, lb = behind(2, g, h, b)
                    sp.wait_ge(fl_sb, l + 1)
                    sp.dma_start(sums_d.rearrange("(g j) (k d) -> g (j k) d", j=J, k=2)[bass.ds(l, 1)]
                                 .rearrange("o r d -> (o r) d"), end_sums[lb]).then_inc(st_s[lb], 16)
            turns(sp, phase1, ahead=1, behind=2)

            for i in range(2):
                sp.wait_ge(st_s[i], 16 * (G // 2))
            sp.dma_start(sums_in, sums_d).then_inc(s_sums, 16)
            sp.wait_ge(eT_ps, G)
            sp.wait_ge(b_ps, 2 * G)

            def phase2(g, h, b, on):
                if on(-1):
                    a, _, ab = behind(-1, g, h, b)
                    need(sp, aT2, J * (a - 1))
                    sp.dma_start(row[ab], dstf_d.rearrange("t p -> (t p)")[bass.ds(a * GE, GE)][None, :]
                                 .to_broadcast([P, GE])).then_inc(row_in[ab], 16)
                if on(0):
                    bulk_io(sp, G, g, h, b)
                if on(1):
                    l, _, lb = behind(1, g, h, b)
                    for part, (lo, hi) in enumerate(PARTS):
                        sp.wait_ge(h2r, J * l + hi)
                        sp.dma_start(edge_rows(x1_d, l)[:, lo:hi, :],
                                     group(ringA, lb)[:, lo:hi, :]).then_inc(st_x[part][lb], 16)
                    sp.dma_start(edge_rows(h2_d, l), group(ringB, lb)).then_inc(st_h[lb], 16)
                if on(2):
                    l, _, lb = behind(2, g, h, b)
                    for part, (lo, hi) in enumerate(PARTS):
                        sp.wait_ge(q2, J * l + hi)
                        sp.dma_start(edge_rows(q_d, l)[:, lo:hi, :],
                                     group(ringC, 1)[:, lo:hi, :]).then_inc(st_q[part], 16)
            turns(sp, phase2, ahead=1, behind=2)

            for i in range(2):
                sp.wait_ge(st_q[i], 16 * G)
                sp.wait_ge(st_h[i], 16 * (G // 2))
            sp.wait_ge(aT2, T)
            for i in range(2):
                sp.wait_ge(st_b[i], 16 * (G // 2))
            sp.dma_start(bias_all, bias_d.rearrange("g n e -> (g n) e")).then_inc(s_bias, 16)
            sp.dma_start(f_cont, cont_d[0:EP].rearrange("(g e) -> g e", g=G)[:, None, :].to_broadcast([G, H, GE])).then_inc(s_flag, 16)
            sp.dma_start(f_next, cont_d[1:EP + 1].rearrange("(g e) -> g e", g=G)[:, None, :].to_broadcast([G, H, GE])).then_inc(s_flag, 16)

            def phase3(g, h, b, on):
                if on(0):
                    need(sp, k3, J * (g - 1))
                    sp.dma_start(group(ringC, b), edge_rows(q_d, g)).then_inc(ql[b], 16)
                    bulk_io(sp, 2 * G, g, h, b)
            turns(sp, phase3)
            last = BULK - 1
            sp.wait_ge(bulk_st[0], 16 * (last // 2))
            sp.dma_start(bulk[0][:, :], xb[:, last * BR * D:BULK * BR * D]).then_inc(bulk_ld[0], 16)
            sp.wait_ge(bulk_add, last)
            sp.dma_start(ob[:, (last - 1) * BR * D:last * BR * D], bulk[1][:, :]).then_inc(bulk_st[1], 16)
            sp.wait_ge(bulk_st[1], 16 * ((last + 1) // 2))
            sp.dma_start(bulk[1][:, 0:REST * D], xb[:, BULK * BR * D:NROW * D]).then_inc(bulk_ld[1], 16)
            sp.dma_start(bulk[1][0:TAIL, REST * D:(REST + 1) * D], x[NROW * P:N, :]).then_inc(bulk_ld[1], 16)
            sp.wait_ge(bulk_rest, 1)
            sp.dma_start(ob[:, last * BR * D:BULK * BR * D], bulk[0][:, :]).then_inc(bulk_st[0], 16)
            sp.wait_ge(bulk_rest, 3)
            sp.dma_start(ob[:, BULK * BR * D:NROW * D], bulk[1][:, 0:REST * D]).then_inc(bulk_st[1], 16)
            sp.dma_start(out[NROW * P:N, :], bulk[1][0:TAIL, REST * D:(REST + 1) * D]).then_inc(bulk_st[1], 16)

            sp.wait_ge(s_al, 1)

            def phase4(g, h, b, on):
                if on(-1):
                    a, ah, ab = behind(-1, g, h, b)
                    need(sp, s4, J * (a - 1))
                    sp.dma_start(row[ab], dstf_d.rearrange("t p -> (t p)")[bass.ds(a * GE, GE)][None, :]
                                 .to_broadcast([P, GE])).then_inc(row4[ab], 16)
                    need(sp, o4, J * (a - 1))
                    sp.dma_start(group(ringB, ab), edge_rows(x1_d, a)).then_inc(x4[ab], 16)
            turns(sp, phase4, ahead=1, behind=0)

        @block.gpsimd
        def _(pool):
            nc.gpsimd.memset(ident[:, :], 0.0).then_inc(s_cst2, 1)
            nc.gpsimd.memset(anti[:, :], 0.0).then_inc(s_cst2, 1)
            nc.gpsimd.iota(iota_i, pattern=[[1, P]], base=1, channel_multiplier=0).then_inc(s_cst2, 1)
            nc.gpsimd.memset(diff, 0.0).then_inc(s_cst2, 1)
            pool.wait_ge(s_cst2, 4)
            nc.gpsimd.affine_select(out=ident[:, :], in_=ident[:, :], compare_op=ALU.not_equal, fill=1.0, base=0,
                                    pattern=[[-1, P]], channel_multiplier=1).then_inc(s_cst, 1)
            nc.gpsimd.affine_select(out=anti[:, :], in_=anti[:, :], compare_op=ALU.not_equal, fill=1.0, base=-(T - 1),
                                    pattern=[[1, T]], channel_multiplier=1).then_inc(s_cst, 1)
            nc.gpsimd.affine_select(out=diff, in_=diff, compare_op=ALU.not_equal, fill=1.0, base=0,
                                    pattern=[[-1, T]], channel_multiplier=1).then_inc(s_cst, 1)
            pool.wait_ge(s_cst, 3)
            nc.gpsimd.affine_select(out=diff, in_=diff, compare_op=ALU.not_equal, fill=-1.0, base=1,
                                    pattern=[[-1, T]], channel_multiplier=1).then_inc(s_cst, 1)
            pool.wait_ge(s_pro, 1)
            copies = [0]

            def indices(table, g, b):
                nc.gpsimd.tensor_copy(ist[:, b * J:(b + 1) * J], table[:, bass.ds(g * J, J)]).then_inc(cp, 1)
                pool.wait_ge(cp, copies[0] + g + 1)
                pool.nop(nofuse=True)

            def phase1(g, h, b, on):
                if on(0):
                    need(pool, fl, g - 1)
                    need(pool, h1, J * (g - 1))
                    indices(sg_i, g, b)
                    for j in range(J):
                        pool.indirect_dma_start(A(b * J + j), None, x, bass.IndirectOffsetOnAxis(
                            ap=ist[:, b * J + j:b * J + j + 1], axis=0)).then_inc(x_in[b], 16)
                if on(1):
                    _, lh, lb = behind(1, g, h, b)
                    bulk_bo(pool, 0, lh, lb)
            turns(pool, phase1)
            copies[0] += G

            def phase2(g, h, b, on):
                if on(1):
                    _, lh, lb = behind(1, g, h, b)
                    bulk_bo(pool, G, lh, lb)
                if on(0):
                    if isinstance(g, int) and g < 2:
                        pool.wait_ge(fl, G - 1 + g)
                        pool.wait_ge(h1, J * (G - 1 + g))
                    else:
                        pool.wait_ge(st_x[0][b], 16 * h)
                    indices(dg_i, g, b)
                    for j in range(J):
                        if j == PARTS[1][0] and not (isinstance(g, int) and g < 2):
                            pool.wait_ge(st_x[1][b], 16 * h)
                            pool.nop(nofuse=True)
                        pool.indirect_dma_start(A(b * J + j), None, x, bass.IndirectOffsetOnAxis(
                            ap=ist[:, b * J + j:b * J + j + 1], axis=0)).then_inc(xd_in[b], 16)
            turns(pool, phase2)
            copies[0] += G
            for i in range(2):
                pool.wait_ge(st_h[i], 16 * (G // 2))

            def phase3(g, h, b, on):
                if on(1):
                    _, lh, lb = behind(1, g, h, b)
                    bulk_bo(pool, 2 * G, lh, lb)
                if on(0):
                    indices(slot_i, g, b)
                    for j in range(J):
                        pool.wait_ge(c3, J * g + j + 1)
                        pool.nop(nofuse=True)
                        pool.indirect_dma_start(A(b * J + j), None, h2_d, bass.IndirectOffsetOnAxis(
                            ap=ist[:, b * J + j:b * J + j + 1], axis=0), bounds_check=EP - 1,
                            oob_is_err=False).then_inc(o_in[b], 16)
            turns(pool, phase3)
            copies[0] += G
            pool.wait_ge(bulk_st[0], 16 * ((BULK + 1) // 2))
            pool.wait_ge(bulk_st[1], 16 * ((BULK - 1) // 2 + 2))

            def phase4(g, h, b, on):
                if on(0):
                    need(pool, sc_out[b], 16 * J * h)
                    indices(out_i, g, b)
                for j in range(J):
                    if on(-1) and j == J - 3:
                        _, ah, ab = behind(-1, g, h, b)
                        pool.wait_ge(x4[ab], 16 * (ah + 1))
                        v = group(ringB, ab)
                        nc.gpsimd.tensor_tensor(v, v, bob[:, None, :].to_broadcast([P, J, D]), ALU.add).then_inc(bo4, 1)
                    if on(0):
                        pool.wait_ge(o4, J * g + j + 1)
                        pool.nop(nofuse=True)
                        pool.indirect_dma_start(out, bass.IndirectOffsetOnAxis(
                            ap=ist[:, b * J + j:b * J + j + 1], axis=0), C(b * J + j), None,
                            bounds_check=N - 1, oob_is_err=False).then_inc(sc_out[b], 16)
            turns(pool, phase4, ahead=1, behind=0)
            for i in range(2):
                pool.wait_ge(sc_out[i], 16 * J * (G // 2))

        @block.scalar
        def _(act):
            act.wait_ge(s_wts, 160)
            act.wait_ge(s_pro, 1)
            act.wait_ge(s_key[1], 64)

            def phase1(g, h, b, on):
                def hidden(m):
                    act.wait_ge(hid_ps, 4 * g + m + 1)
                    c, half = m // 2, m % 2
                    nc.scalar.activation(hid[:, c, half * (GE // 2):(half + 1) * (GE // 2)],
                                         bank[3 + m % 2][:, 0:GE // 2], ACT.Relu,
                                         bias=b1c[:, c:c + 1]).then_inc(hid_sb, 1)
                if on(1):
                    l, lh, lb = behind(1, g, h, b)
                    act.wait_ge(rs1, l + 1)
                    for j in range(J):
                        nc.scalar.activation(A(lb * J + j), A(lb * J + j), ACT.Relu, bias=nm[:, lb, j:j + 1],
                                             scale=rs[:, lb, j:j + 1]).then_inc(h1a, 1)
                    act.wait_ge(h1a, J * (l + 1))
                    hold(act)
                    for j in range(J):
                        nc.scalar.activation(store3[:, bass.ds(J * l + j, 1), :],
                                             A(lb * J + j)[:, None, :], ACT.Copy).then_inc(h1, 1)
                if on(0):
                    need(act, b_ps, 2 * g)
                    for m in range(4):
                        hidden(m)
                    act.wait_ge(var1, g + 1)
                    nc.scalar.activation(sd[:, b, :], mv[:, b, :, 1], ACT.Sqrt, bias=epsc[:, :]).then_inc(sd1, 1)
                if on(-1):
                    act.wait_ge(eT_ps, g + 2)
                    need(act, hid_ps, 4 * (g + 1))
                    nc.scalar.copy(eT[:, 0:512], bank[1][0:FE, :])
                    nc.scalar.copy(eT[:, 512:GE], bank[2][0:FE, 0:GE - 512]).then_inc(eT_sb, 1)
            turns(act, phase1, ahead=1)

            act.wait_ge(keys, G)
            act.wait_ge(abv, G)

            def phase2(g, h, b, on):
                if on(1):
                    l, lh, lb = behind(1, g, h, b)
                    act.wait_ge(rs2, l + 1)
                    need(act, st_h[lb], 16 * lh)
                    need(act, t2, J * (l - 1))
                if on(2):
                    l2, l2h, l2b = behind(2, g, h, b)
                for j in range(J + 1):
                    for k in range(2 * j, min(2 * j + 2, J)):
                        if on(1):
                            u = lb * J + k
                            nc.scalar.activation(B(u), A(u), ACT.Relu, bias=nm[:, lb, k:k + 1],
                                                 scale=rs[:, lb, k:k + 1]).then_inc(h2r, 1)
                    if on(2) and j < J:
                        u = l2b * J + j
                        act.wait_ge(t2, J * l2 + j + 1)
                        need(act, qp, J * l2 + j - 1)
                        nc.scalar.copy(hT[u % 2], bank[4 + u % 2][:, 0:D]
                                       .rearrange("p (c e) -> p c e", c=NC)).then_inc(hT2, 1)
                    if on(2) and j > 0:
                        u = l2b * J + j - 1
                        act.wait_ge(qp, J * l2 + j)
                        for part, (lo, _) in enumerate(PARTS):
                            if j - 1 == lo:
                                need(act, st_q[part], 16 * l2)
                        nc.scalar.copy(C(J + j - 1), bank[6 + u % 2][:, 0:D]).then_inc(q2, 1)
                    if not on(1) and on(2) and j < J:
                        if j == 0:
                            act.wait_ge(st_x[0][0], 16 * (G // 2))
                            act.wait_ge(st_x[1][0], 16 * (G // 2))
                        nc.scalar.activation(A(j)[:, None, :], store3[:, j:j + 1, :], ACT.Copy).then_inc(c3, 1)
                    if on(-1) and j < J:
                        a, ah, ab = behind(-1, g, h, b)
                        need(act, ag, J * (a - 1) + j + 1)
                        hold(act)
                        nc.scalar.activation(C(j)[:, None, :],
                                             store3[:, bass.ds(J * a + j, 1), :], ACT.Copy).then_inc(hs, 1)
                if on(0):
                    act.wait_ge(var2, g + 1)
                    nc.scalar.activation(sd[:, b, :], mv[:, b, :, 1], ACT.Sqrt, bias=epsc[:, :]).then_inc(sd2, 1)
            turns(act, phase2, ahead=1, behind=2)
            for i in range(2):
                act.wait_ge(st_x[0][i], 16 * (G // 2))
                act.wait_ge(st_x[1][i], 16 * (G // 2))

            def phase3(g, h, b, on):
                def copy_rows(j):
                    if on(0) and j < J and not (isinstance(g, int) and g == 0):
                        need(act, t3, J * (g - 2) + j + 1)
                        hold(act)
                        nc.scalar.activation(A(b * J + j)[:, None, :],
                                             store3[:, bass.ds(J * g + j, 1), :], ACT.Copy).then_inc(c3, 1)
                for j in range(J + 1):
                    l, _, lb = behind(1, g, h, b)
                    u = lb * J + j
                    if on(1) and j < J:
                        act.wait_ge(t3, J * l + j + 1)
                        need(act, kv, J * l + j - 1)
                        nc.scalar.copy(hT[u % 2], bank[4 + u % 2][:, 0:D]
                                       .rearrange("p (c e) -> p c e", c=NC)).then_inc(hT3, 1)
                    if on(1) and j > 0:
                        act.wait_ge(kv, J * l + j)
                        hold(act)
                        nc.scalar.activation(store3[:, bass.ds(J * l + j - 1, 1), :],
                                             bank[2 + (u - 1) % 2][:, None, 0:D], ACT.Copy).then_inc(v3, 1)
                    copy_rows(2 * j)
                    copy_rows(2 * j + 1)
            turns(act, phase3)
            act.wait_ge(act_sm, 1)
            nc.scalar.activation(ex, xs, ACT.Exp).then_inc(act_sm, 1)

        @block.vector
        def _(dve):
            pro = Chain(dve, pdve)
            pro.start(0)
            nc.vector.memset(ones[:, :], 1.0)
            nc.vector.memset(epsc[:, :], EPS)
            nc.vector.memset(w_zero, 0.0)
            dve.wait_ge(s_idx, 64)
            nc.vector.tensor_copy(w_src, src_i[:, :])
            nc.vector.tensor_copy(w_dstf, dst_i[:, :])
            pro.link(nc.vector.tensor_copy(w_nxt, nxt_i[:, :]))
            pro.link(nc.vector.tensor_tensor(w_eq, w_dstf, w_nxt, ALU.is_equal))
            pro.link(nc.vector.scalar_tensor_tensor(w_fin, w_eq, SKIP, w_dstf, ALU.mult, ALU.add))
            pro.link(nc.vector.tensor_scalar(w_key[:, 0:P - 1], w_eq[:, 0:P - 1], -1.0, 1.0, ALU.mult, ALU.add))
            pro.link(nc.vector.scalar_tensor_tensor(w_key[:, 0:P - 1], w_dstf[:, 0:P - 1], 1.0, w_key[:, 0:P - 1],
                                                    ALU.add, ALU.mult))
            nc.vector.tensor_copy(w_key[:, P - 1:P], w_dstf[:, P - 1:P])
            pro.link(nc.vector.tensor_scalar(w_key[:, 0:P - 1], w_key[:, 0:P - 1], -1.0, None, ALU.add))
            dve.wait_ge(s_cst, 4)
            for k in range(4):
                sel = ident[0:T, 0:T] if k < 2 else anti[:, :]
                endcol = w_dstf[:, 0:1] if k % 2 == 0 else w_dstf[:, P - 1:P]
                nc.vector.tensor_scalar(w_diag[:, k * T:(k + 1) * T], sel, endcol, None, ALU.mult)
            nc.vector.tensor_copy(iota1[:, :], iota_i).then_inc(s_key[0], 1)
            dve.wait_ge(s_tr, 9)
            nc.vector.tensor_copy(dcol, bank[0][:, 0:T])
            nc.vector.tensor_copy(scol[:, :], bank[0][:, T:2 * T])
            nc.vector.tensor_copy(sg_i[:, :], bank[0][:, T:2 * T])
            nc.vector.tensor_copy(wcol, bank[0][:, 2 * T:3 * T])
            nc.vector.tensor_copy(out_i[:, :], bank[0][:, 3 * T:4 * T])
            nc.vector.tensor_scalar(dg_i[:, :], bank[0][:, 0:T], float(N - 1), None, ALU.min)
            nc.vector.memset(DP[:, 0:1], -1.0)
            nc.vector.tensor_copy(DP[:, 1:T], bank[1][:, T:2 * T - 1])
            nc.vector.tensor_copy(per_tile[:, 2:4, :], bank[1][:, 0:2 * T].rearrange("p (k t) -> p k t", k=2))
            pro.link(nc.vector.tensor_copy(ends_r[:, :, :], bank[1][:, 2 * T:4 * T].rearrange("p (k t) -> p k t", k=2)))
            first_r, last_r = ends_r[:, 0, :], ends_r[:, 1, :]
            nc.vector.memset(cnt[:, 2, 0:1], 0.0)
            nc.vector.tensor_tensor(cnt[:, 0, :], first, DP, ALU.is_equal)
            nc.vector.tensor_tensor(cnt[:, 2, 1:T], last_r[:, 1:T], first_r[:, 0:T - 1], ALU.is_equal)
            nc.vector.tensor_tensor(cnt[:, 1, :], first, last, ALU.is_equal)
            pro.link(nc.vector.tensor_tensor(cnt[:, 3, :], first_r, last_r, ALU.is_equal))
            nc.vector.tensor_tensor(cnt[:, 1, :], cnt[:, 1, :], cnt[:, 0, :], ALU.mult)
            nc.vector.tensor_tensor(cnt[:, 3, :], cnt[:, 3, :], cnt[:, 2, :], ALU.mult)
            nc.vector.tensor_tensor(edge_w[:, :, 0], dcol, first, ALU.is_equal)
            pro.link(nc.vector.tensor_tensor(edge_w[:, :, 1], dcol, last, ALU.is_equal))
            pro.link(nc.vector.tensor_tensor(edge_w[:, :, :], edge_w[:, :, :],
                                             wcol[:, :, None].to_broadcast([P, T, 2]), ALU.mult))
            nc.vector.tensor_copy(key_step, bank[2][0:T, 0:P])
            pro.link(nc.vector.tensor_tensor(last_before[0:T, :], w_dstf[:, P - 1:P], bank[2][0:T, P - 1:P], ALU.subtract))
            nc.vector.memset(last_before[0:1, :], -1.0)
            pro.link(nc.vector.memset(pick[:, :, :, :], 0.0))
            for j in range(J):
                ins = nc.vector.memset(pick[:, j, j, :], 1.0)
            pro.link(ins)
            nc.vector.memset(carry[:, :], 0.0).then_inc(s_pro, 1)
            dve.wait_ge(s_wts, 160)

            lead_c, lag_c = Chain(dve, lead1), Chain(dve, lag1)

            def phase1(g, h, b, on):
                if on(0):
                    dve.wait_ge(sr_in[b], 16 * (h + 1))
                    need(dve, keys, g - 1)
                    nc.vector.tensor_scalar(above[b], src_row[b], last_before[0:T, :], None, ALU.is_gt).then_inc(abv, 1)
                if on(2):
                    l2, l2h, l2b = behind(2, g, h, b)
                    dve.wait_ge(fl, l2 + 1)
                    need(dve, st_s[l2b], 16 * l2h)
                    nc.vector.tensor_copy(end_sums[l2b], bank[0][0:2 * J, 0:D]).then_inc(fl_sb, 1)
                if on(1):
                    l, lh, lb = behind(1, g, h, b)
                    need(dve, st_b[lb], 16 * lh)
                    dve.wait_ge(b_ps, 2 * l + 2)
                    for half in range(2):
                        nc.vector.tensor_scalar(biasT[lb][:, half * (GE // 2):(half + 1) * (GE // 2)],
                                                bias_ps[half], b2c[:, :], None, ALU.add).then_inc(bT_sb, 1)
                    lag_c.start(l)
                    dve.wait_ge(keys, l + 1)
                    for j in range(J):
                        ins = nc.vector.scalar_tensor_tensor(keys_ps(j), keys_ps(j), scol[:, bass.ds(J * l + j, 1)],
                                                             iota1[:, :], ALU.is_equal, ALU.mult,
                                                             accum_out=pm[:, j:j + 1])
                    lag_c.link(ins)
                    lag_c.link(nc.vector.tensor_scalar(pz[:, :], pm[:, :], 0.0, SKIP, ALU.is_equal, ALU.mult))
                    lag_c.link(nc.vector.scalar_tensor_tensor(pm[:, :], tauf[:, bass.ds(J * l, J)], float(P), pm[:, :],
                                                              ALU.mult, ALU.add))
                    nc.vector.scalar_tensor_tensor(slot_i[:, bass.ds(J * l, J)], pm[:, :], -1.0, pz[:, :],
                                                   ALU.add, ALU.add).then_inc(slots_done, 1)
                    lag_c.end()
                if on(0):
                    lead_c.start(g)
                    lead_c.link(nc.vector.tensor_tensor(
                        taucmp, last[:, None, :].to_broadcast([P, J, T]),
                        scol[:, bass.ds(J * g, J)][:, :, None].to_broadcast([P, J, T]), ALU.is_lt))
                    nc.vector.tensor_reduce(tauf[:, bass.ds(J * g, J)], taucmp, AX, ALU.add)
                    own = edge_w[:, bass.ds(J * g, J), :][:, :, None, :].to_broadcast([P, J, J, 2])
                    nc.vector.tensor_tensor(pick_w[:, b, :, :, :], pick[:, :, :, :], own, ALU.mult).then_inc(pk, 1)
                    dve.wait_ge(x_in[b], 16 * J * (h + 1))
                    for j in range(J):
                        ins = nc.vector.bn_stats(st6[:, j, :], A(b * J + j))
                    lead_c.link(ins)
                    for j in range(J):
                        ins = nc.vector.bn_aggr(mv[:, b, j, :], st6[:, j, :])
                    ins.then_inc(var1, 1)
                    dve.wait_ge(sd1, g + 1)
                    lead_c.link(nc.vector.reciprocal(rs[:, b, :], sd[:, b, :]))
                    nc.vector.scalar_tensor_tensor(nm[:, b, :], mv[:, b, :, 0], -1.0, rs[:, b, :],
                                                   ALU.mult, ALU.mult).then_inc(rs1, 1)
                    lead_c.end()
            turns(dve, phase1, behind=2)

            cc = Chain(dve, s_carr)
            cc.start(0)
            dve.wait_ge(sumsT, 4)
            for i in range(2):
                dve.wait_ge(st_b[i], 16 * (G // 2))
            v = bank[0][:, 0:4 * T].rearrange("p (k c t) -> p k c t", k=2, c=NC)
            nc.vector.tensor_copy(sums[:, 0, :, :], v[:, 1, :, :])
            cc.link(nc.vector.tensor_copy(sums[:, 1, :, :], v[:, 0, :, ::-1]))
            nc.vector.memset(per_tile[:, 5:7, 0:1], 0.0)
            nc.vector.memset(per_tile[:, 7:9, T - 1:T], 0.0)
            for k in range(2):
                for c in range(NC):
                    ins = nc.vector.tensor_tensor_scan(carr[:, k, c, :], cnt[:, 2 * k + 1, :], sums[:, k, c, :],
                                                       0.0, ALU.mult, ALU.add)
            cc.link(ins)
            for c in range(NC):
                nc.vector.tensor_tensor(per_tile[:, 5 + c, 1:T], carr[:, 0, c, 0:T - 1], cnt[:, 0, 1:T], ALU.mult)
                ins = nc.vector.tensor_tensor(per_tile[:, 7 + c, 0:T - 1][:, ::-1], carr[:, 1, c, 0:T - 1],
                                              cnt[:, 2, 1:T], ALU.mult)
            cc.link(ins)

            def fetch(g, b):
                return nc.vector.tensor_copy(here[:, b, :, :], per_tile[:, :, bass.ds(J * g, J)])
            lead_2, lag_2, ahead_2 = Chain(dve, lead2), Chain(dve, lag2), Chain(dve, fetched2)

            def phase2(g, h, b, on):
                a, ah, ab = behind(-1, g, h, b)
                if on(1):
                    lg, lh, lb = behind(1, g, h, b)
                    lag_2.start(lg)
                    dve.wait_ge(sd2, lg + 1)
                    lag_2.link(nc.vector.reciprocal(rs[:, lb, :], sd[:, lb, :]))
                    nc.vector.scalar_tensor_tensor(nm[:, lb, :], mv[:, lb, :, 0], -1.0, rs[:, lb, :],
                                                   ALU.mult, ALU.mult).then_inc(rs2, 1)
                    lag_2.end()
                def mark_ends(j):
                    t, u = J * g + j, b * J + j
                    need(dve, aT2, t - 1)
                    nc.vector.tensor_scalar(indF(u), row[b][:, j * P:(j + 1) * P],
                                            here[:, b, 2, j:j + 1], None, ALU.is_equal)
                    marked[j] = lead_2.mark(nc.vector.tensor_scalar(indL(u), row[b][:, j * P:(j + 1) * P],
                                                                    here[:, b, 3, j:j + 1], None, ALU.is_equal))

                def same_segment(k):
                    if not on(-1) or not 0 <= k < J:
                        return
                    if k == 0:
                        ahead_2.start(a)
                        ahead_2.link(fetch(a, ab))
                        ahead_2.end()
                        dve.wait_ge(row_in[ab], 16 * (ah + 1))
                    nc.vector.tensor_scalar(S(ab * J + k), row[ab][:, k * P:(k + 1) * P],
                                            here[:, ab, 0, k:k + 1], here[:, ab, 1, k:k + 1],
                                            ALU.is_equal, ALU.mult).then_inc(S2, 1)
                marked = {}
                if on(0):
                    lead_2.start(g)
                    mark_ends(0)
                for j in range(J + 3):
                    u, t = b * J + j, J * g + j
                    if on(0) and j < J:
                        lead_2.wait(marked[j])
                        dve.wait_ge(ag, t + 1)
                        for c in range(NC):
                            ins = nc.vector.scalar_tensor_tensor(
                                aT[u % 2][:, c, :], indF(u), here[:, b, 5 + c, j:j + 1],
                                bank[u % 2][:, c * P:(c + 1) * P], ALU.mult, ALU.add)
                        added = lead_2.mark(ins)
                    same_segment(2 * (j - 3))
                    if on(0) and j + 1 < J:
                        mark_ends(j + 1)
                    if on(0) and j > 2:
                        dve.wait_ge(x1r, J * g + j - 2)
                        ins = nc.vector.bn_stats(st6[:, j - 3, :], A(u - 3))
                    if on(0) and j < J:
                        lead_2.wait(added)
                        for c in range(NC):
                            ins2 = nc.vector.scalar_tensor_tensor(
                                aT[u % 2][:, c, :], indL(u), here[:, b, 7 + c, j:j + 1],
                                aT[u % 2][:, c, :], ALU.mult, ALU.add)
                        ins2.then_inc(aT2, 1)
                    if on(0) and 1 < j < J + 2:
                        if j == 2:
                            dve.wait_ge(xd_in[b], 16 * J * (h + 1))
                        dve.wait_ge(w2p, J * g + j - 1)
                        nc.vector.scalar_tensor_tensor(A(u - 2), bank[2 + (u - 2) % 2][:, 0:D], 0.0,
                                                       A(u - 2), ALU.max, ALU.add).then_inc(x1r, 1)
                    same_segment(2 * (j - 3) + 1)
                if on(0):
                    lead_2.link(ins)
                    for j in range(J):
                        ins = nc.vector.bn_aggr(mv[:, b, j, :], st6[:, j, :])
                    ins.then_inc(var2, 1)
                    lead_2.end()
            turns(dve, phase2, ahead=1, behind=1)

            dve.wait_ge(s_flag, 32)
            nc.vector.tensor_scalar(neg_cont, f_cont, -1.0, BIG, ALU.add, ALU.mult)
            nc.vector.tensor_scalar(neg_next, f_next, -1.0, BIG, ALU.add, ALU.mult)
            nc.vector.tensor_reduce(col[:, 2:3], f_cont, AX, ALU.min)
            nc.vector.tensor_reduce(col[:, 3:4], f_next, AX, ALU.min)

            def phase3(g, h, b, on):
                if on(1):
                    g, h, b = behind(1, g, h, b)
                    dve.wait_ge(ql[b], 16 * (h + 1))
                    for j in range(J + 1):
                        u = b * J + j
                        if j < J:
                            dve.wait_ge(kv, J * g + j + 1)
                            nc.vector.tensor_tensor(prod[:, j, :], bank[6 + u % 2][:, 0:D], C(u), ALU.mult).then_inc(k3, 1)
                        if j > 0:
                            dve.wait_ge(k3, J * g + j)
                            nc.vector.tensor_reduce(ssum[:, (j - 1) * H:j * H],
                                                    prod[:, j - 1, :].rearrange("p (n e) -> p n e", e=HD),
                                                    AX, ALU.add).then_inc(lag3, 1)
                    dve.wait_ge(lag3, J * (g + 1))
                    hold(dve)
                    nc.vector.tensor_copy(sc_all[:, :, bass.ds(g, 1), :],
                                          ssum[:, :].rearrange("p (j o n) -> p j o n", o=1, n=H)).then_inc(x_sb, 1)
            turns(dve, phase3)
            last_k = BULK - 1
            dve.wait_ge(bulk_ld[0], 16 * (last_k // 2 + 1))
            v = bulk[0][:, :].rearrange("p (r d) -> p r d", d=D)
            nc.vector.tensor_tensor(v, v, bob[:, None, :].to_broadcast([P, BR, D]), ALU.add).then_inc(bulk_rest, 1)
            dve.wait_ge(bulk_ld[1], 16 * (last_k // 2 + 2))
            v = bulk[1][:, 0:REST * D].rearrange("p (r d) -> p r d", d=D)
            nc.vector.tensor_tensor(v, v, bob[:, None, :].to_broadcast([P, REST, D]), ALU.add).then_inc(bulk_rest, 1)
            v = bulk[1][0:TAIL, REST * D:(REST + 1) * D]
            nc.vector.tensor_tensor(v, v, bob[0:TAIL, :], ALU.add).then_inc(bulk_rest, 1)

            sm = Chain(dve, s_sm)
            sm.start(0)
            dve.wait_ge(x_ps, 2)
            dve.wait_ge(s_bias, 16)
            for lo, hi, k in ((0, 512, 0), (512, GE, 1)):
                ins = nc.vector.scalar_tensor_tensor(xs[:, lo:hi], bank[k][0:GH, 0:hi - lo], float(1.0 / np.sqrt(HD)),
                                                     bias_all[:, lo:hi], ALU.mult, ALU.add)
            sm.link(ins)
            passes = [0]

            def both_scans(values, is_max):
                flags = (neg_cont, neg_next) if is_max else (f_cont, f_next)
                o0, o1, init = (ALU.add, ALU.max, -BIG) if is_max else (ALU.mult, ALU.add, 0.0)

                def scans(first_f, first_b):
                    nc.vector.tensor_tensor_scan(fwd, flags[0], values, first_f, o0, o1)
                    sm.link(nc.vector.tensor_tensor_scan(bwd[:, ::-1], flags[1][:, ::-1], values[:, ::-1], first_b, o0, o1))
                scans(init, init)
                nc.vector.tensor_copy(col[:, 0:1], fwd[:, GE - 1:GE])
                nc.vector.tensor_copy(col[:, 1:2], bwd[:, 0:1]).then_inc(pe_sm, 1)
                passes[0] += 1
                dve.wait_ge(al_ps, 2 * passes[0] - 1)
                for i in range(4):
                    v = bank[2][0:1, i * GH:(i + 1) * GH].rearrange("o (g n) -> o n g", n=H)
                    v = v[:, :, ::-1] if i % 2 else v
                    ins = nc.vector.tensor_copy(lin_in[:, i, :].rearrange("o (n g) -> o n g", n=H), v)
                sm.link(ins)
                sm.link(nc.vector.memset(lin_in[:, 2:4, :].rearrange("o k (n g) -> o (k n) g", g=G)[:, :, 0:1], 0.0))
                if is_max:
                    sm.link(nc.vector.tensor_scalar(lin_in[:, 2:4, :], lin_in[:, 2:4, :], -1.0, BIG, ALU.add, ALU.mult))
                nc.vector.memset(lin_carry[:, :, :], init)
                for i in range(2):
                    ins = nc.vector.tensor_tensor_scan(lin_out[:, i, :], lin_in[:, 2 + i, :], lin_in[:, i, :], init, o0, o1)
                sm.link(ins)
                for i in range(2):
                    v = lin_carry[:, i, :].rearrange("o (g n) -> o n g", n=H)
                    v = v[:, :, ::-1] if i else v
                    ins = nc.vector.tensor_copy(v[:, :, 1:G], lin_out[:, i, :].rearrange("o (n g) -> o n g", n=H)[:, :, 0:G - 1])
                ins.then_inc(pe_sm, 1)
                dve.wait_ge(al_ps, 2 * passes[0])
                sm.link(nc.vector.tensor_copy(carry[:, :], bank[3][0:GH, 0:2]))
                scans(carry[:, 0:1], carry[:, 1:2])

            both_scans(xs, True)
            sm.link(nc.vector.tensor_tensor(total, fwd, bwd, ALU.max))
            nc.vector.tensor_tensor(xs, xs, total, ALU.subtract).then_inc(act_sm, 1)
            dve.wait_ge(act_sm, 2)
            both_scans(ex, False)
            sm.link(nc.vector.tensor_tensor(bwd, bwd, ex, ALU.subtract))
            sm.link(nc.vector.tensor_tensor(total, fwd, bwd, ALU.add))
            sm.link(nc.vector.reciprocal(total, total))
            sm.link(nc.vector.tensor_tensor(xs, ex, total, ALU.mult))
            nc.vector.engine_nop().then_inc(pe_sm, 1)
            dve.wait_ge(al_ps, 2 * passes[0] + 1)
            nc.vector.memset(aT[1], 0.0)
            nc.vector.tensor_copy(sc_all[:, 0:4, :, :], bank[4][:, 0:4 * GH].rearrange("p (j g n) -> p j g n", j=4, n=H))
            sm.link(nc.vector.tensor_copy(sc_all[:, 4:J, :, :], bank[5][:, 0:3 * GH].rearrange("p (j g n) -> p j g n", j=3, n=H)))
            nc.vector.engine_nop().then_inc(s_al, 1)


            dve.wait_ge(bulk_st[0], 16 * ((BULK + 1) // 2))
            ahead_4 = Chain(dve, fetched4)

            def phase4(g, h, b, on):
                a, ah, ab = behind(-1, g, h, b)

                def weigh(k):
                    if not on(-1) or not 0 <= k < J:
                        return
                    if k == 0:
                        ahead_4.start(a)
                        nc.vector.tensor_copy(al_here[:, ab, :, None, :], sc_all[:, :, bass.ds(a, 1), :])
                        ahead_4.link(fetch(a, ab))
                        ahead_4.end()
                        need(dve, aT4, J * (a - 1))
                        dve.wait_ge(row4[ab], 16 * (ah + 1))
                    u = ab * J + k
                    rowk = row[ab][:, k * P:(k + 1) * P]
                    nc.vector.tensor_scalar(S(u), rowk, here[:, ab, 0, k:k + 1], None, ALU.is_equal)
                    nc.vector.tensor_scalar(runs_on(u), rowk, here[:, ab, 4, k:k + 1], None, ALU.is_equal)
                    al = al_here[:, ab, k, :, None].to_broadcast([P, H, HD])
                    nc.vector.tensor_tensor(A(u).rearrange("p (n e) -> p n e", n=H),
                                            store[:, bass.ds((J * a + k) * D, D)].rearrange("p (n e) -> p n e", n=H),
                                            al, ALU.mult).then_inc(s4, 1)
                for j in range(J + 2):
                    u, t = b * J + j, J * g + j
                    if on(0) and j < J:
                        if j == 0:
                            dve.wait_ge(s4, J * (g + 1))
                        need(dve, aT4, t)
                        dve.wait_ge(ag4, t + 1)
                        for c in range(NC):
                            ins = nc.vector.scalar_tensor_tensor(
                                aT[u % 2][:, c, :], runs_on(u), aT[(u + 1) % 2][:, c, P - 1:P],
                                bank[u % 2][:, c * P:(c + 1) * P], ALU.mult, ALU.add)
                        ins.then_inc(aT4, 1)
                    weigh(j)
                    if on(0) and j > 1:
                        if j == 2:
                            dve.wait_ge(bo4, g + 1)
                            need(dve, sc_out[b], 16 * J * h)
                        dve.wait_ge(wo, J * g + j - 1)
                        nc.vector.tensor_tensor(C(u - 2), bank[2 + (u - 2) % 2][:, 0:D], B(u - 2),
                                                ALU.add).then_inc(o4, 1)
            turns(dve, phase4, ahead=1, behind=0)

        @block.tensor
        def _(pe):
            def mm(o, lhsT, rhs, start=True, stop=True):
                return nc.tensor.matmul(o, lhsT, rhs, start=start, stop=stop)

            pe.wait_ge(s_key[0], 1)
            for k, r in enumerate((w_dstf, w_src, w_r[:, :], w_fin)):
                nc.tensor.transpose(bank[0][:, k * T:(k + 1) * T], r, ident[0:T, 0:T]).then_inc(s_tr, 1)
            for k in range(4):
                mm(bank[1][:, k * T:(k + 1) * T], ones[0:T, :], w_diag[:, k * T:(k + 1) * T]).then_inc(s_tr, 1)
            mm(bank[2][0:T, 0:P], diff, w_key).then_inc(s_tr, 1)
            pe.wait_ge(s_wts, 160)
            pe.wait_ge(s_pro, 1)

            def phase1(g, h, b, on):
                def hidden(m):
                    c, half = m // 2, m % 2
                    need(pe, hid_sb, 4 * g + m - 1)
                    mm(bank[3 + m % 2][:, 0:GE // 2], W1sb[:, c * P:(c + 1) * P],
                       eT[:, half * (GE // 2):(half + 1) * (GE // 2)]).then_inc(hid_ps, 1)
                if on(0):
                    pe.wait_ge(eT_sb, g + 1)
                    hidden(0)
                    hidden(1)
                if on(1):
                    l, lh, lb = behind(1, g, h, b)
                    need(pe, fl_sb, l)
                    pe.wait_ge(pk, l + 1)
                    for j in range(J):
                        pe.wait_ge(h1a, J * l + j + 1)
                        ins = mm(bank[0][0:2 * J, 0:D], pick_w[:, lb, j, :, :].rearrange("p i k -> p (i k)"),
                                 A(lb * J + j), start=(j == 0), stop=(j == J - 1))
                    ins.then_inc(fl, 1)
                if on(0):
                    hidden(2)
                    hidden(3)
                if on(-1):
                    a, ah, ab = behind(-1, g, h, b)
                    pe.wait_ge(ef_in[ab], 16 * (ah + 1))
                    need(pe, bT_sb, 2 * g)
                    hold(pe)
                    for j in range(J):
                        ins = nc.tensor.transpose(bank[1 + j // 4][0:FE, (j % 4) * P:(j % 4 + 1) * P],
                                                  ef[ab][:, j * FE:(j + 1) * FE], ident[:, :])
                    ins.then_inc(eT_ps, 1)
                if on(0):
                    pe.wait_ge(abv, g + 1)
                    need(pe, slots_done, g)
                    hold(pe)
                    for j in range(J):
                        ins = mm(keys_ps(j), above[b][:, j * P:(j + 1) * P], key_step)
                    ins.then_inc(keys, 1)
                    for half in range(2):
                        if half == 0:
                            need(pe, bT_sb, 2 * g)
                        elif on(-1):
                            pe.wait_ge(eT_sb, g + 2)
                        pe.wait_ge(hid_sb, 4 * g + 3 + half)
                        for c in range(NC):
                            ins = mm(bias_ps[half], W2sb[:, c, :],
                                     hid[:, c, half * (GE // 2):(half + 1) * (GE // 2)],
                                     start=(c == 0), stop=(c == NC - 1))
                        ins.then_inc(b_ps, 1)
            turns(pe, phase1, ahead=1)
            pe.wait_ge(fl_sb, G)
            pe.wait_ge(s_sums, 16)
            for k in range(2 * NC):
                nc.tensor.transpose(bank[0][:, k * T:(k + 1) * T], sums_in[:, k * P:(k + 1) * P],
                                    ident[0:T, 0:T]).then_inc(sumsT, 1)
            pe.wait_ge(s_carr, 1)
            pe.wait_ge(bT_sb, 2 * G)

            def phase2(g, h, b, on):
                lg, lh, lb = behind(2, g, h, b)
                for j in range(J + 1):
                    u, lu = b * J + j, lb * J + j
                    if on(0) and j < J:
                        t = J * g + j
                        pe.wait_ge(S2, t + 1)
                        pe.wait_ge(hs, t + 1)
                        need(pe, aT2, t - 1)
                        for c in range(NC):
                            ins = mm(bank[u % 2][:, c * P:(c + 1) * P], C(j)[:, c * P:(c + 1) * P], S(u))
                        ins.then_inc(ag, 1)
                    if on(2) and j < J:
                        t = J * lg + j
                        pe.wait_ge(h2r, t + 1)
                        need(pe, hT2, t - 1)
                        for c in range(NC):
                            ins = nc.tensor.transpose(bank[4 + lu % 2][:, c * P:(c + 1) * P],
                                                      B(lu)[:, c * P:(c + 1) * P], ident[:, :])
                        ins.then_inc(t2, 1)
                    if on(0) and j > 0:
                        t, v = J * g + j - 1, u - 1
                        pe.wait_ge(aT2, t + 1)
                        need(pe, x1r, t - 1)
                        for c in range(NC):
                            ins = mm(bank[2 + v % 2][:, 0:D], aT[v % 2][:, c, :], Wsb[:, c, :],
                                     start=(c == 0), stop=(c == NC - 1))
                        ins.then_inc(w2p, 1)
                    if on(2) and j > 0:
                        t, v = J * lg + j - 1, lu - 1
                        pe.wait_ge(hT2, t + 1)
                        need(pe, q2, t - 1)
                        for c in range(NC):
                            ins = mm(bank[6 + v % 2][:, 0:D], hT[v % 2][:, c, :], Wqsb[:, c, :],
                                     start=(c == 0), stop=(c == NC - 1))
                        ins.then_inc(qp, 1)
            turns(pe, phase2, ahead=0, behind=2)
            pe.wait_ge(q2, T)

            def phase3(g, h, b, on):
                if on(1):
                    g, h, b = behind(1, g, h, b)
                    pe.wait_ge(o_in[b], 16 * J * (h + 1))
                    for j in range(J + 1):
                        u = b * J + j
                        if j < J:
                            t = J * g + j
                            need(pe, hT3, t - 1)
                            for c in range(NC):
                                ins = nc.tensor.transpose(bank[4 + u % 2][:, c * P:(c + 1) * P],
                                                          A(u)[:, c * P:(c + 1) * P], ident[:, :])
                            ins.then_inc(t3, 1)
                        if j > 0:
                            t, v = J * g + j - 1, u - 1
                            pe.wait_ge(hT3, t + 1)
                            need(pe, k3, t - 1)
                            need(pe, v3, t - 1)
                            for c in range(NC):
                                mm(bank[6 + v % 2][:, 0:D], hT[v % 2][:, c, :], Wkv[:, c, 0:D],
                                   start=(c == 0), stop=(c == NC - 1))
                                ins = mm(bank[2 + v % 2][:, 0:D], hT[v % 2][:, c, :], Wkv[:, c, D:2 * D],
                                         start=(c == 0), stop=(c == NC - 1))
                            ins.then_inc(kv, 1)
            turns(pe, phase3)
            pe.wait_ge(x_sb, G)
            pe.wait_ge(v3, T)
            for j in range(J):
                ins = nc.tensor.transpose(bank[j // 4][0:GH, (j % 4) * P:(j % 4 + 1) * P],
                                          sc_all[:, j, :, :].rearrange("p g n -> p (g n)"), ident[:, :])
                if j in (3, J - 1):
                    ins.then_inc(x_ps, 1)
            for k in range(2):
                pe.wait_ge(pe_sm, 2 * k + 1)
                for i in range(4):
                    ins = mm(bank[2][0:1, i * GH:(i + 1) * GH], col[:, i:i + 1], ident[0:GH, 0:GH])
                ins.then_inc(al_ps, 1)
                pe.wait_ge(pe_sm, 2 * k + 2)
                for i in range(2):
                    ins = mm(bank[3][0:GH, i:i + 1], lin_carry[:, i, :], ones[0:1, 0:1])
                ins.then_inc(al_ps, 1)
            pe.wait_ge(pe_sm, 5)
            for j in range(J):
                ins = nc.tensor.transpose(bank[4 + j // 4][:, (j % 4) * GH:(j % 4 + 1) * GH],
                                          xs[:, j * P:(j + 1) * P], ident[0:GH, 0:GH])
            ins.then_inc(al_ps, 1)

            def phase4(g, h, b, on):
                if on(0):
                    for j in range(J + 1):
                        u = b * J + j
                        if j < J:
                            t = J * g + j
                            pe.wait_ge(s4, t + 1)
                            need(pe, aT4, t - 1)
                            for c in range(NC):
                                ins = mm(bank[u % 2][:, c * P:(c + 1) * P], A(u)[:, c * P:(c + 1) * P], S(u))
                            ins.then_inc(ag4, 1)
                        if j > 0:
                            t, v = J * g + j - 1, u - 1
                            pe.wait_ge(aT4, t + 1)
                            need(pe, o4, t - 1)
                            for c in range(NC):
                                ins = mm(bank[2 + v % 2][:, 0:D], aT[v % 2][:, c, :], Wosb[:, c, :],
                                         start=(c == 0), stop=(c == NC - 1))
                            ins.then_inc(wo, 1)
            turns(pe, phase4, ahead=0, behind=0)


def kernel(**inputs):
    import numpy as _np
    import concourse.bacc as _bacc
    from concourse import mybir as _mybir
    from concourse.bass_utils import run_bass_kernel_spmd as _run

    a = {k: _np.ascontiguousarray(v) for k, v in inputs.items()}
    pad = EP - E
    dst = _np.full(EP + 1, PAD_DST, a['dst'].dtype)
    dst[0:E] = a['dst']
    dst[EP] = -1
    src = _np.zeros(EP, a['src'].dtype)
    src[0:E] = a['src']
    wgt = _np.zeros(EP, a['edge_weight'].dtype)
    wgt[0:E] = a['edge_weight']
    eattr = _np.zeros((EP, FE), a['edge_attr_64'].dtype)
    eattr[0:E] = a['edge_attr_64']
    arrays = {'x': a['x'], 'dst': dst, 'src': src, 'wgt': wgt, 'eattr': eattr, 'W': a['L0_gnn_weight']}
    for n in ('Wq', 'Wk', 'Wv', 'W1', 'b1', 'W2', 'b2', 'Wo', 'bo'):
        arrays[n] = a['L1_gnn_' + n]
    nc = _bacc.Bacc("TRN2", target_bir_lowering=False, num_devices=1)
    arrays = {'in_' + k: v for k, v in arrays.items()}
    args = [nc.dram_tensor(k, v.shape, _mybir.dt.from_np(v.dtype), kind="ExternalInput").ap() for k, v in arrays.items()]
    out = nc.dram_tensor("out_x", (N, D), _mybir.dt.float32, kind="ExternalOutput").ap()
    gnn_program(nc, *args, out)
    r = _run(nc, [arrays], core_ids=[0])
    return r.results[0]["out_x"]
```

```python
import concourse.bass as bass
import numpy as np
from concourse import mybir
from contextlib import ExitStack

N, E, D, H, FE = 50000, 12500, 256, 8, 64
HD = D // H
P = 128
J = 7
T = -(-E // P)
G = T // J
EP = T * P
GE = J * P
NC = D // P
GH = G * H
EPS = 1e-5
BIG = 1e30
PAD_DST = 65535
SKIP = 1000000.0
BR = 9
NROW = N // P
BULK = NROW // BR
REST = NROW - BULK * BR
TAIL = N - NROW * P
DVE_ROWS = 1
PARTS = ((0, 4), (4, J))


def gnn_program(nc, x, dst, src, wgt, eattr, W, Wq, Wk, Wv, W1, b1, W2, b2, Wo, bo, out):
    f32 = mybir.dt.float32
    i32 = mybir.dt.int32
    ALU = mybir.AluOpType
    ACT = mybir.ActivationFunctionType
    AX = mybir.AxisListType.X

    x1_d = nc.dram_tensor("x1", (EP, D), f32, kind="Internal").ap()
    h2_d = nc.dram_tensor("h2", (EP, D), f32, kind="Internal").ap()
    q_d = nc.dram_tensor("q", (EP, D), f32, kind="Internal").ap()
    dstf_d = nc.dram_tensor("dst_f", (T, P), f32, kind="Internal").ap()
    srcf_d = nc.dram_tensor("src_f", (T, P), f32, kind="Internal").ap()
    on_d = nc.dram_tensor("runs_on", (T, P), f32, kind="Internal").ap()
    sums_d = nc.dram_tensor("end_sums", (T, 2 * D), f32, kind="Internal").ap()
    bias_d = nc.dram_tensor("bias_t", (G, H, GE), f32, kind="Internal").ap()
    cont_d = nc.dram_tensor("cont", (EP + 1,), f32, kind="Internal").ap()

    ctx = ExitStack()
    with ctx:
        def sb(name, shape, dt=f32):
            return ctx.enter_context(nc.sbuf_tensor(name, shape, dt))

        def pb(name, shape, dt=f32):
            return ctx.enter_context(nc.psum_tensor(name, shape, dt))

        def sem(name):
            return ctx.enter_context(nc.semaphore(name))

        def sem2(name):
            return [sem(name + "_0"), sem(name + "_1")]

        store = sb("store", [P, T * D])
        ringA = sb("ringA", [P, 2 * J * D])
        ringB = sb("ringB", [P, 2 * J * D])
        ringC = sb("ringC", [P, 2 * J * D])
        bulk = [sb(f"bulk{i}", [P, BR * D]) for i in range(2)]
        Wsb, Wqsb, Wosb = (sb(n, [P, NC, D]) for n in ("W_sb", "Wq_sb", "Wo_sb"))
        Wkv = sb("Wkv_sb", [P, NC, 2 * D])
        W1sb = sb("W1_sb", [FE, D])
        W2sb = sb("W2_sb", [P, NC, H])
        b1c = sb("b1_col", [P, NC])
        b2c = sb("b2_col", [H, 1])
        bob = sb("bo_all", [P, D])
        ident = sb("ident", [P, P])
        ones = sb("ones", [P, P])
        iota1 = sb("iota1", [P, P])
        epsc = sb("eps", [P, 1])
        rows = sb("rows", [P, 2 * GE])
        Sr = sb("Sr", [P, 2 * GE])
        small = sb("small", [P, 4 * D])
        ind = sb("ind", [P, 4 * P])
        scol = sb("src_col", [P, T])
        dg_i = sb("dst_gather", [P, T], i32)
        sg_i = sb("src_gather", [P, T], i32)
        out_i = sb("out_scatter", [P, T], i32)
        slot_i = sb("slot_gather", [P, T], i32)
        tauf = sb("tau", [P, T])
        per_tile = sb("per_tile", [P, 9, T])
        here = sb("here", [P, 2, 9, J])
        al_here = sb("al_here", [P, 2, J, H])
        ends_r = sb("ends_r", [P, 2, T])
        pick = sb("pick", [P, J, J, 2])
        pick_w = sb("pick_w", [P, 2, J, J, 2])
        cnt = sb("cnt", [P, 4, T])
        edge_w = sb("edge_w", [P, T, 2])
        sc_all = sb("scores", [P, J, G, H])
        st6 = sb("st6", [P, J, 6])
        mv = sb("mv", [P, 2, J, 2])
        sd = sb("sd", [P, 2, J])
        rs = sb("rs", [P, 2, J])
        nm = sb("nm", [P, 2, J])
        pm = sb("pm", [P, J])
        pz = sb("pz", [P, J])
        ist = sb("ist", [P, 2 * J], i32)
        last_before = sb("last_before", [P, 1])
        ssum = sb("ssum", [P, J * H])
        col = sb("col", [GH, 4])
        carry = sb("carry", [GH, 2])

        dcol, wcol, first, last, DP = (per_tile[:, k, :] for k in range(5))
        store3 = store[:, :].rearrange("p (t d) -> p t d", d=D)
        aT = [small[:, i * D:(i + 1) * D].rearrange("p (c e) -> p c e", c=NC) for i in range(2)]
        hT = [small[:, (2 + i) * D:(3 + i) * D].rearrange("p (c e) -> p c e", c=NC) for i in range(2)]
        taucmp = small[:, 0:J * T].rearrange("p (j t) -> p j t", t=T)
        hid = Sr[:, :].rearrange("p (c e) -> p c e", c=NC)
        eT = rows[0:FE, 0:GE]
        ef = [rows[:, GE + i * J * FE:GE + (i + 1) * J * FE] for i in range(2)]
        row = [rows[:, i * GE:(i + 1) * GE] for i in range(2)]
        prod = Sr[:, :].rearrange("p (j d) -> p j d", d=D)

        w_dstf, w_src, w_nxt, w_eq, w_fin, w_key = (ringB[0:T, k * P:(k + 1) * P] for k in range(6))
        w_zero = ringB[0:1, 6 * P:6 * P + 1]
        key_step = ringB[0:T, 15 * P:16 * P]
        w_diag = ringB[0:T, 7 * P:7 * P + 4 * T]
        anti = ringB[0:T, 14 * P:14 * P + T]
        diff = ringB[0:T, 20 * P:20 * P + T]
        dst_i, nxt_i, src_i = (ringB[0:T, k * P:(k + 1) * P].bitcast(i32) for k in (16, 17, 18))
        w_r = ringB[0:T, 19 * P:20 * P]
        iota_i = ringB[:, 12 * P:13 * P].bitcast(i32)
        src_row = [ringC[0:T, i * GE:(i + 1) * GE] for i in range(2)]
        above = [ringC[0:T, (2 + i) * GE:(3 + i) * GE] for i in range(2)]
        biasT = [ringB[0:H, i * GE:(i + 1) * GE] for i in range(2)]
        end_sums = [ringB[0:2 * J, (20 + 2 * i) * P:(22 + 2 * i) * P] for i in range(2)]
        sums_in = ringB[0:T, 24 * P:28 * P]
        w_on = ringB[0:T, 24 * P:25 * P]
        sums = ringB[:, 0:4 * T].rearrange("p (m c t) -> p m c t", m=2, c=NC)
        carr = ringB[:, 14 * P:14 * P + 4 * T].rearrange("p (m c t) -> p m c t", m=2, c=NC)
        bias_all = rows[0:GH, 0:GE]
        f_cont, f_next, neg_cont, neg_next = (ringB[0:GH, k * GE:(k + 1) * GE] for k in range(4))
        xs, fwd, bwd, total = (ringC[0:GH, k * GE:(k + 1) * GE] for k in range(4))
        ex = ringA[0:GH, 0:GE]
        lin_in = small[0:1, 0:4 * GH].rearrange("o (k r) -> o k r", k=4)
        lin_out = small[0:1, 4 * GH:6 * GH].rearrange("o (k r) -> o k r", k=2)
        lin_carry = small[0:1, 6 * GH:8 * GH].rearrange("o (k r) -> o k r", k=2)

        def indF(u):
            return ind[:, (u % 2) * P:(u % 2 + 1) * P]

        def indL(u):
            return ind[:, (2 + u % 2) * P:(3 + u % 2) * P]

        def keys_ps(j):
            return bank[5 + j // 4 * 2][:, (j % 4) * P:(j % 4 + 1) * P]

        def runs_on(u):
            return bulk[0][:, u * P:(u + 1) * P]

        def S(u):
            return Sr[:, u * P:(u + 1) * P]

        def A(u):
            return ringA[:, u * D:(u + 1) * D]

        def B(u):
            return ringB[:, u * D:(u + 1) * D]

        def C(u):
            return ringC[:, u * D:(u + 1) * D]

        def group(ring, b):
            return ring[:, b * J * D:(b + 1) * J * D].rearrange("p (j d) -> p j d", d=D)

        bank = [pb(f"bank{i}", [P, 512]) for i in range(8)]
        bias_ps = [bank[6][0:H, 0:GE // 2], bank[2][0:H, 0:GE // 2]]

        s_idx, s_wts = sem("index_rows_in"), sem("weights_in")
        s_mlp, s_first = sem("edge_mlp_weights_in"), sem2("first_src_in")
        s_cst, s_cst2 = sem("constants"), sem("constants_step")
        s_key = sem("rows_for_dram"), sem("rows_in_dram")
        s_tr = sem("columns_in_psum")
        s_pro = sem("columns_ready")
        pdve = sem("dve_prologue")
        ef_in, x_in, sr_in = sem2("ef_in"), sem2("xsrc_in"), sem2("src_rows_in")
        eT_ps, eT_sb, hid_ps, hid_sb = sem("eT_in_psum"), sem("eT_in_sbuf"), sem("hid_in_psum"), sem("hid_in_sbuf")
        b_ps = sem("bias_in_psum")
        var1, sd1, rs1, h1a, h1, fl = (sem(n) for n in (
            "var1", "sd1", "rstd1", "h1_written", "h1_stored", "end_sums_in_psum"))
        abv, keys, cp = sem("above_ready"), sem("keys_in_psum"), sem("pool_index_copied")
        lead1, lag1 = sem("dve_lead1"), sem("dve_lag1")
        bulk_ld, bulk_st = sem2("bulk_loaded"), sem2("bulk_stored")
        bulk_add, bulk_add_dve, bulk_rest = sem("bulk_added"), sem("bulk_rows_added_by_dve"), sem("bulk_rest_added")
        s_carr = sem("dve_carries")
        st_b, st_s, bT_sb, fl_sb, pk = (sem2("bias_stored"), sem2("end_sums_stored"), sem("biasT_ready"),
                                        sem("end_sums_ready"), sem("pick_ready"))
        s_sums, s_bias, sumsT = sem("end_sums_loaded"), sem("bias_loaded"), sem("sumsT_in_psum")
        row_in, xd_in = sem2("rows_in"), sem2("xdst_in")
        hs, S2, ag, aT2, w2p, x1r = (sem(n) for n in (
            "h_copied", "S_ready", "agg_in_psum", "aggT_ready", "l0_in_psum", "x1_ready"))
        var2, sd2, rs2, h2r, t2, hT2, qp, q2, bo4 = (sem(n) for n in (
            "var2", "sd2", "rstd2", "h2_ready", "h2T_in_psum", "h2T_ready", "q_in_psum", "q_ready", "bo_added"))
        st_x = [sem2("x1_stored_part0"), sem2("x1_stored_part1")]
        st_h = [sem2("h2_stored_part0"), sem2("h2_stored_part1")]
        st_q = sem2("q_stored_part")
        fetched2, fetched4 = sem("per_tile_fetched2"), sem("per_tile_fetched4")
        marked, added, lag2 = sem("ends_marked"), sem("first_carry_added"), sem("dve_lag2")
        c3, t3, hT3, kv, v3, k3 = (sem(n) for n in (
            "hsrc_copied", "hsrcT_in_psum", "hsrcT_ready", "kv_in_psum", "v_stored", "k_used"))
        o_in, ql = sem2("h2_overlaid"), sem2("q_loaded")
        lag3 = sem("dve_lag3")
        s_flag, x_ps, x_sb, s_sm, pe_sm, act_sm, al_ps = (sem(n) for n in (
            "flags_in", "scoresT_in_psum", "scoresT_ready", "dve_softmax", "pe_softmax", "act_softmax",
            "alpha_in_psum"))
        row4, x4 = sem2("rows4_in"), sem2("x1_loaded")
        on_rdy, on_st, on4 = sem("runs_on_ready"), sem("runs_on_stored"), sem2("runs_on_in")
        s4, ag4, aT4, wo, o4 = (sem(n) for n in (
            "weighted_v_ready", "attn_in_psum", "attnT_ready", "wo_in_psum", "out_rows_ready"))
        sc_out, slots_done = sem2("rows_scattered"), sem("slots_ready")

        def need(eng, s, value):
            if isinstance(value, int) and value <= 0:
                return
            eng.wait_ge(s, value)

        def hold(eng):
            eng.nop(nofuse=True)

        class Chain:

            def __init__(self, eng, s):
                self.eng, self.s, self.per, self.n = eng, s, None, 0

            def start(self, g):
                self.base = 0 if self.per is None else g * self.per
                self.n = 0

            def link(self, ins):
                self.n += 1
                ins.then_inc(self.s, 1)
                self.eng.wait_ge(self.s, self.base + self.n)
                if not isinstance(self.base, int):
                    hold(self.eng)

            def end(self):
                assert self.per in (None, self.n)
                self.per = self.n

        def turns(eng, turn, ahead=0, behind=1):
            first = 2 + behind // 2 * 2
            pairs = (G - ahead - first) // 2

            def peeled(g):
                turn(g, g // 2, g % 2, lambda k: 0 <= g - k < G)
            for g in range(-ahead, first):
                peeled(g)
            with eng.Fori(first // 2, first // 2 + pairs) as h:
                turn(2 * h, h, 0, lambda k: True)
                turn(2 * h + 1, h, 1, lambda k: True)
            for g in range(first + 2 * pairs, G + behind):
                peeled(g)

        def behind(k, g, h, b):
            return g - k, h + (b - k) // 2, (b - k) % 2

        def edge_rows(dram, g):
            return dram.rearrange("(t p) d -> p t d", p=P)[:, bass.ds(g * J, J), :]

        xb = x[0:NROW * P, :].rearrange("(p n) d -> p (n d)", p=P)
        ob = out[0:NROW * P, :].rearrange("(p n) d -> p (n d)", p=P)

        def load_bulk(sp, base, g, h, b):
            need(sp, bulk_st[b], 16 * (base // 2 + h) if not (base == 0 and isinstance(h, int)) else 16 * h)
            sp.dma_start(bulk[b][:, :], xb[:, bass.ds((base + g) * (BR * D), BR * D)]).then_inc(bulk_ld[b], 16)

        def bulk_io(sp, base, g, h, b):
            load_bulk(sp, base, g, h, b)
            if not (isinstance(g, int) and base + g == 0):
                sp.wait_ge(bulk_add, base + g)
                if base == 0:
                    sp.wait_ge(bulk_add_dve, g)
                elif isinstance(g, int) and g == 0:
                    sp.wait_ge(bulk_add_dve, G)
                sp.dma_start(ob[:, bass.ds((base + g - 1) * (BR * D), BR * D)],
                             bulk[1 - b][:, :]).then_inc(bulk_st[1 - b], 16)

        def bulk_bo(pool, base, h, b, lo=0):
            pool.wait_ge(bulk_ld[b], 16 * (base // 2 + h + 1))
            v = bulk[b][:, lo * D:BR * D].rearrange("p (r d) -> p r d", d=D)
            nc.gpsimd.tensor_tensor(v, v, bob[:, None, :].to_broadcast([P, BR - lo, D]), ALU.add).then_inc(bulk_add, 1)

        block = ctx.enter_context(nc.Block())

        @block.sync
        def _(sp):
            sp.dma_start(dst_i[:, :], dst[0:EP].rearrange("(t p) -> t p", p=P)).then_inc(s_idx, 16)
            sp.dma_start(nxt_i[:, :], dst[1:EP + 1].rearrange("(t p) -> t p", p=P)).then_inc(s_idx, 16)
            sp.dma_start(src_i[:, :], src.rearrange("(t p) -> t p", p=P)).then_inc(s_idx, 16)
            sp.dma_start(w_r[:, :], wgt.rearrange("(t p) -> t p", p=P)).then_inc(s_idx, 16)
            for i in range(2):
                sp.dma_start(ist[:, i * J:(i + 1) * J], src[i * GE:(i + 1) * GE].rearrange("(j p) -> p j", p=P),
                             allow_slow_non_contiguous=True).then_inc(s_first[i], 16)
            sp.dma_start(W1sb[:, :], W1).then_inc(s_mlp, 16)
            sp.dma_start(W2sb[:, :, :], W2.rearrange("(c p) n -> p c n", p=P)).then_inc(s_mlp, 16)
            sp.dma_start(b1c[:, :], b1.rearrange("(c p) -> p c", p=P), allow_slow_non_contiguous=True).then_inc(s_mlp, 16)
            sp.dma_start(b2c[:, :], b2.rearrange("(n o) -> n o", o=1), allow_slow_non_contiguous=True).then_inc(s_mlp, 16)
            sp.dma_start(bob[:, :], bo[None, :].to_broadcast([P, D])).then_inc(s_mlp, 16)
            sp.dma_start(ef[0].rearrange("p (j f) -> p j f", f=FE), edge_rows(eattr, 0)).then_inc(ef_in[0], 16)
            sp.wait_ge(s_key[0], 1)
            sp.dma_start(dstf_d, w_dstf[:, :]).then_inc(s_key[1], 16)
            sp.dma_start(srcf_d, w_src).then_inc(s_key[1], 16)
            sp.dma_start(cont_d[1:EP + 1].rearrange("(t p) -> t p", p=P), w_eq[:, :]).then_inc(s_key[1], 16)
            sp.dma_start(cont_d[0:1].rearrange("(a b) -> a b", a=1), w_zero[0:1, 0:1]).then_inc(s_key[1], 16)

            def phase1(g, h, b, on):
                if on(-1):
                    a, _, ab = behind(-1, g, h, b)
                    if not (isinstance(a, int) and a == 0):
                        need(sp, eT_ps, a - 1)
                        sp.dma_start(ef[ab].rearrange("p (j f) -> p j f", f=FE),
                                     edge_rows(eattr, a)).then_inc(ef_in[ab], 16)
                    if isinstance(a, int) and a == 0:
                        sp.wait_ge(s_key[1], 64)
                    need(sp, abv, a - 1)
                    sp.dma_start(src_row[ab], srcf_d.rearrange("t p -> (t p)")[bass.ds(a * GE, GE)][None, :]
                                 .to_broadcast([T, GE])).then_inc(sr_in[ab], 16)
                if isinstance(g, int) and g == 0:
                    for m, sbuf in ((W, Wsb[:, :, :]), (Wq, Wqsb[:, :, :]), (Wo, Wosb[:, :, :]),
                                    (Wk, Wkv[:, :, 0:D]), (Wv, Wkv[:, :, D:2 * D])):
                        sp.dma_start(sbuf, m.rearrange("(c p) n -> p c n", p=P)).then_inc(s_wts, 16)
                    sp.wait_ge(on_rdy, 1)
                    sp.dma_start(on_d, w_on).then_inc(on_st, 16)
                if on(0):
                    bulk_io(sp, 0, g, h, b)
                if on(1):
                    l, _, lb = behind(1, g, h, b)
                    sp.wait_ge(bT_sb, 2 * l + 2)
                    sp.dma_start(bias_d[bass.ds(l, 1)].rearrange("o n e -> (o n) e"), biasT[lb]).then_inc(st_b[lb], 16)
                if on(2):
                    l, _, lb = behind(2, g, h, b)
                    sp.wait_ge(fl_sb, l + 1)
                    sp.dma_start(sums_d.rearrange("(g j) (k d) -> g (j k) d", j=J, k=2)[bass.ds(l, 1)]
                                 .rearrange("o r d -> (o r) d"), end_sums[lb]).then_inc(st_s[lb], 16)
            turns(sp, phase1, ahead=1, behind=2)

            sp.wait_ge(eT_ps, G)
            sp.wait_ge(b_ps, 2 * G)

            def phase2(g, h, b, on):
                if on(-1):
                    a, _, ab = behind(-1, g, h, b)
                    need(sp, aT2, J * (a - 1))
                    sp.dma_start(row[ab], dstf_d.rearrange("t p -> (t p)")[bass.ds(a * GE, GE)][None, :]
                                 .to_broadcast([P, GE])).then_inc(row_in[ab], 16)
                if isinstance(g, int) and g == -1:
                    for i in range(2):
                        sp.wait_ge(st_s[i], 16 * (G // 2))
                    sp.wait_ge(on_st, 16)
                    sp.dma_start(sums_in, sums_d).then_inc(s_sums, 16)
                def store_q(part, k):
                    if on(k):
                        l, _, lb = behind(k, g, h, b)
                        lo, hi = PARTS[part]
                        sp.wait_ge(q2, J * l + hi)
                        hold(sp)
                        sp.dma_start(edge_rows(q_d, l)[:, lo:hi, :], group(ringC, 1)[:, lo:hi, :]).then_inc(st_q[part], 16)

                def store_x1(part, k):
                    if on(k):
                        l, _, lb = behind(k, g, h, b)
                        lo, hi = PARTS[part]
                        sp.wait_ge(x1r, J * l + hi)
                        hold(sp)
                        sp.dma_start(edge_rows(x1_d, l)[:, lo:hi, :],
                                     group(ringB, lb)[:, lo:hi, :]).then_inc(st_x[part][lb], 16)

                def store_h2(part):
                    if on(1):
                        l, _, lb = behind(1, g, h, b)
                        lo, hi = PARTS[part]
                        sp.wait_ge(h2r, J * l + hi)
                        hold(sp)
                        sp.dma_start(edge_rows(h2_d, l)[:, lo:hi, :],
                                     group(ringB, lb)[:, lo:hi, :]).then_inc(st_h[part][lb], 16)
                store_q(1, 3)
                store_x1(1, 1)
                if on(0) or isinstance(g, int) and g == G:
                    bulk_io(sp, G, g, h, b)
                elif isinstance(g, int) and g == G + 1:
                    load_bulk(sp, G, g, h, b)
                store_h2(0)
                store_x1(0, 0)
                store_q(0, 2)
                store_h2(1)
            turns(sp, phase2, ahead=1, behind=3)

            for i in range(2):
                sp.wait_ge(st_q[i], 16 * G)
                for part in range(2):
                    sp.wait_ge(st_h[part][i], 16 * (G // 2))
            sp.wait_ge(aT2, T)

            def phase3(g, h, b, on):
                if on(0):
                    need(sp, k3, J * (g - 1))
                    sp.dma_start(group(ringC, b), edge_rows(q_d, g)).then_inc(ql[b], 16)
                    sp.wait_ge(bulk_add, 2 * G + g + 1)
                    sp.dma_start(ob[:, bass.ds((2 * G + g) * (BR * D), BR * D)], bulk[b][:, :]).then_inc(bulk_st[b], 16)
                    if not (isinstance(g, int) and 2 * G + 2 + g >= BULK):
                        load_bulk(sp, 2 * G + 2, g, h, b)
                if isinstance(g, int) and g == 0:
                    for i in range(2):
                        sp.wait_ge(st_b[i], 16 * (G // 2))
                    sp.dma_start(bias_all, bias_d.rearrange("g n e -> (g n) e")).then_inc(s_bias, 16)
                    for k, flags in enumerate((f_cont, f_next)):
                        sp.dma_start(flags, cont_d[k:EP + k].rearrange("(g e) -> g e", g=G)[:, None, :]
                                     .to_broadcast([G, H, GE])).then_inc(s_flag, 16)
            turns(sp, phase3, ahead=2)
            last = BULK - 1
            sp.wait_ge(bulk_st[1], 16 * ((last + 1) // 2))
            sp.dma_start(bulk[1][:, 0:REST * D], xb[:, BULK * BR * D:NROW * D]).then_inc(bulk_ld[1], 16)
            sp.dma_start(bulk[1][0:TAIL, REST * D:(REST + 1) * D], x[NROW * P:N, :]).then_inc(bulk_ld[1], 16)
            sp.wait_ge(bulk_rest, 1)
            sp.dma_start(ob[:, last * BR * D:BULK * BR * D], bulk[0][:, :]).then_inc(bulk_st[0], 16)
            sp.wait_ge(bulk_rest, 3)
            sp.dma_start(ob[:, BULK * BR * D:NROW * D], bulk[1][:, 0:REST * D]).then_inc(bulk_st[1], 16)
            sp.dma_start(out[NROW * P:N, :], bulk[1][0:TAIL, REST * D:(REST + 1) * D]).then_inc(bulk_st[1], 16)

            sp.wait_ge(act_sm, 1)

            def phase4(g, h, b, on):
                if on(-1):
                    a, ah, ab = behind(-1, g, h, b)
                    need(sp, s4, J * (a - 1))
                    sp.dma_start(row[ab], dstf_d.rearrange("t p -> (t p)")[bass.ds(a * GE, GE)][None, :]
                                 .to_broadcast([P, GE])).then_inc(row4[ab], 16)
                    if isinstance(a, int) and a == 0:
                        sp.wait_ge(bulk_st[0], 16 * ((BULK + 1) // 2))
                    need(sp, aT4, J * (a - 1))
                    sp.dma_start(bulk[0][:, ab * GE:(ab + 1) * GE], on_d.rearrange("t p -> (t p)")[bass.ds(a * GE, GE)][None, :]
                                 .to_broadcast([P, GE])).then_inc(on4[ab], 16)
                    if isinstance(a, int) and a == 0:
                        sp.wait_ge(pe_sm, 5)
                    need(sp, o4, J * (a - 1))
                    sp.dma_start(group(ringB, ab), edge_rows(x1_d, a)).then_inc(x4[ab], 16)
            turns(sp, phase4, ahead=1, behind=0)

        @block.gpsimd
        def _(pool):
            nc.gpsimd.memset(ident[:, :], 0.0).then_inc(s_cst2, 1)
            nc.gpsimd.memset(anti[:, :], 0.0).then_inc(s_cst2, 1)
            nc.gpsimd.iota(iota_i, pattern=[[1, P]], base=1, channel_multiplier=0).then_inc(s_cst2, 1)
            nc.gpsimd.memset(diff, 0.0).then_inc(s_cst2, 1)
            pool.wait_ge(s_cst2, 4)
            nc.gpsimd.affine_select(out=ident[:, :], in_=ident[:, :], compare_op=ALU.not_equal, fill=1.0, base=0,
                                    pattern=[[-1, P]], channel_multiplier=1).then_inc(s_cst, 1)
            nc.gpsimd.affine_select(out=anti[:, :], in_=anti[:, :], compare_op=ALU.not_equal, fill=1.0, base=-(T - 1),
                                    pattern=[[1, T]], channel_multiplier=1).then_inc(s_cst, 1)
            nc.gpsimd.affine_select(out=diff, in_=diff, compare_op=ALU.not_equal, fill=1.0, base=0,
                                    pattern=[[-1, T]], channel_multiplier=1).then_inc(s_cst, 1)
            pool.wait_ge(s_cst, 3)
            nc.gpsimd.affine_select(out=diff, in_=diff, compare_op=ALU.not_equal, fill=-1.0, base=1,
                                    pattern=[[-1, T]], channel_multiplier=1).then_inc(s_cst, 1)
            copies = [-2]

            def indices(table, g, b):
                nc.gpsimd.tensor_copy(ist[:, b * J:(b + 1) * J], table[:, bass.ds(g * J, J)]).then_inc(cp, 1)
                pool.wait_ge(cp, copies[0] + g + 1)
                pool.nop(nofuse=True)

            def phase1(g, h, b, on):
                if on(0):
                    need(pool, fl, g - 1)
                    need(pool, h1, J * (g - 1))
                    if isinstance(g, int) and g < 2:
                        pool.wait_ge(s_first[b], 16)
                        pool.nop(nofuse=True)
                    else:
                        if isinstance(g, int) and g == 2:
                            pool.wait_ge(s_pro, 1)
                        indices(sg_i, g, b)
                    for j in range(J):
                        pool.indirect_dma_start(A(b * J + j), None, x, bass.IndirectOffsetOnAxis(
                            ap=ist[:, b * J + j:b * J + j + 1], axis=0)).then_inc(x_in[b], 16)
                if on(1):
                    _, lh, lb = behind(1, g, h, b)
                    bulk_bo(pool, 0, lh, lb, DVE_ROWS)
            turns(pool, phase1)
            copies[0] += G

            def phase2(g, h, b, on):
                if on(0):
                    if isinstance(g, int) and g < 2:
                        pool.wait_ge(fl, G - 1 + g)
                        pool.wait_ge(h1, J * (G - 1 + g))
                    else:
                        pool.wait_ge(x1r, J * (g - 1))
                    indices(dg_i, g, b)
                    for j in range(J):
                        pool.indirect_dma_start(A(b * J + j), None, x, bass.IndirectOffsetOnAxis(
                            ap=ist[:, b * J + j:b * J + j + 1], axis=0)).then_inc(xd_in[b], 16)
                if on(1):
                    _, lh, lb = behind(1, g, h, b)
                    bulk_bo(pool, G, lh, lb)
            turns(pool, phase2)
            copies[0] += G
            for i in range(2):
                for part in range(2):
                    pool.wait_ge(st_h[part][i], 16 * (G // 2))

            def phase3(g, h, b, on):
                if on(0):
                    indices(slot_i, g, b)
                    for j in range(J):
                        pool.wait_ge(c3, J * g + j + 1)
                        pool.nop(nofuse=True)
                        pool.indirect_dma_start(A(b * J + j), None, h2_d, bass.IndirectOffsetOnAxis(
                            ap=ist[:, b * J + j:b * J + j + 1], axis=0), bounds_check=EP - 1,
                            oob_is_err=False).then_inc(o_in[b], 16)
                    bulk_bo(pool, 2 * G, h, b)
            turns(pool, phase3)
            last_k = BULK - 1
            pool.wait_ge(bulk_ld[0], 16 * (last_k // 2 + 1))
            v = bulk[0][:, :].rearrange("p (r d) -> p r d", d=D)
            nc.gpsimd.tensor_tensor(v, v, bob[:, None, :].to_broadcast([P, BR, D]), ALU.add).then_inc(bulk_rest, 1)
            pool.wait_ge(bulk_ld[1], 16 * (last_k // 2 + 2))
            v = bulk[1][:, 0:REST * D].rearrange("p (r d) -> p r d", d=D)
            nc.gpsimd.tensor_tensor(v, v, bob[:, None, :].to_broadcast([P, REST, D]), ALU.add).then_inc(bulk_rest, 1)
            v = bulk[1][0:TAIL, REST * D:(REST + 1) * D]
            nc.gpsimd.tensor_tensor(v, v, bob[0:TAIL, :], ALU.add).then_inc(bulk_rest, 1)
            copies[0] += G
            pool.wait_ge(bulk_st[0], 16 * ((BULK + 1) // 2))
            pool.wait_ge(bulk_st[1], 16 * ((BULK - 1) // 2 + 2))

            def phase4(g, h, b, on):
                if on(0):
                    need(pool, sc_out[b], 16 * J * h)
                    indices(out_i, g, b)
                for j in range(J):
                    if on(-1) and j == 3:
                        _, ah, ab = behind(-1, g, h, b)
                        pool.wait_ge(x4[ab], 16 * (ah + 1))
                        v = group(ringB, ab)
                        nc.gpsimd.tensor_tensor(v, v, bob[:, None, :].to_broadcast([P, J, D]), ALU.add).then_inc(bo4, 1)
                    if on(0):
                        pool.wait_ge(o4, J * g + j + 1)
                        pool.nop(nofuse=True)
                        pool.indirect_dma_start(out, bass.IndirectOffsetOnAxis(
                            ap=ist[:, b * J + j:b * J + j + 1], axis=0), C(b * J + j), None,
                            bounds_check=N - 1, oob_is_err=False).then_inc(sc_out[b], 16)
            turns(pool, phase4, ahead=1, behind=0)
            for i in range(2):
                pool.wait_ge(sc_out[i], 16 * J * (G // 2))

        @block.scalar
        def _(act):
            act.wait_ge(s_mlp, 80)

            def phase1(g, h, b, on):
                def hidden(m):
                    act.wait_ge(hid_ps, 4 * g + m + 1)
                    c, half = m // 2, m % 2
                    nc.scalar.activation(hid[:, c, half * (GE // 2):(half + 1) * (GE // 2)],
                                         bank[3 + m % 2][:, 0:GE // 2], ACT.Relu,
                                         bias=b1c[:, c:c + 1]).then_inc(hid_sb, 1)
                if on(1):
                    l, lh, lb = behind(1, g, h, b)
                    act.wait_ge(rs1, l + 1)
                    for j in range(J):
                        nc.scalar.activation(A(lb * J + j), A(lb * J + j), ACT.Relu, bias=nm[:, lb, j:j + 1],
                                             scale=rs[:, lb, j:j + 1]).then_inc(h1a, 1)
                    act.wait_ge(h1a, J * (l + 1))
                    hold(act)
                    for j in range(J):
                        nc.scalar.activation(store3[:, bass.ds(J * l + j, 1), :],
                                             A(lb * J + j)[:, None, :], ACT.Copy).then_inc(h1, 1)
                if on(0):
                    need(act, b_ps, 2 * g)
                    for m in range(4):
                        hidden(m)
                    act.wait_ge(var1, g + 1)
                    nc.scalar.activation(sd[:, b, :], mv[:, b, :, 1], ACT.Sqrt, bias=epsc[:, :]).then_inc(sd1, 1)
                if on(-1):
                    act.wait_ge(eT_ps, g + 2)
                    need(act, hid_ps, 4 * (g + 1))
                    nc.scalar.copy(eT[:, 0:512], bank[1][0:FE, :])
                    nc.scalar.copy(eT[:, 512:GE], bank[2][0:FE, 0:GE - 512]).then_inc(eT_sb, 1)
            turns(act, phase1, ahead=1)

            act.wait_ge(keys, G)
            act.wait_ge(abv, G)

            def phase2(g, h, b, on):
                l, lh, lb = behind(1, g, h, b)
                l2, _, l2b = behind(2, g, h, b)
                l3, _, l3b = behind(3, g, h, b)

                def copy_q(l, lb, j):
                    act.wait_ge(qp, J * l + j + 1)
                    for part, (lo, _) in enumerate(PARTS):
                        if j == lo:
                            need(act, st_q[part], 16 * l)
                    nc.scalar.copy(C(J + j), bank[6 + (lb * J + j) % 2][:, 0:D]).then_inc(q2, 1)

                for j in range(J):
                    if on(-1):
                        a, ah, ab = behind(-1, g, h, b)
                        need(act, ag, J * (a - 1) + j + 1)
                        hold(act)
                        nc.scalar.activation(C(j)[:, None, :], store3[:, bass.ds(J * a + j, 1), :], ACT.Copy,
                                             scale=wcol[:, bass.ds(J * a + j, 1)]).then_inc(hs, 1)
                    if on(2):
                        u = l2b * J + j
                        act.wait_ge(t2, J * l2 + j + 1)
                        need(act, qp, J * l2 + j - 1)
                        nc.scalar.copy(hT[u % 2], bank[4 + u % 2][:, 0:D]
                                       .rearrange("p (c e) -> p c e", c=NC)).then_inc(hT2, 1)
                    if j == 0 and on(3):
                        copy_q(l3, l3b, J - 1)
                    if j > 0 and on(2):
                        copy_q(l2, l2b, j - 1)
                    if j == 2 and on(1):
                        act.wait_ge(var2, l + 1)
                        nc.scalar.activation(sd[:, lb, :], mv[:, lb, :, 1], ACT.Sqrt, bias=epsc[:, :]).then_inc(sd2, 1)
                    if j > 2 and on(1):
                        if j == 3:
                            act.wait_ge(rs2, l + 1)
                        for k in range(2 * j - 6, min(2 * j - 4, J)):
                            u = lb * J + k
                            for part, (lo, _) in enumerate(PARTS):
                                if k == lo:
                                    act.wait_ge(st_x[part][lb], 16 * (lh + 1))
                            nc.scalar.activation(B(u), B(u), ACT.Relu, bias=nm[:, lb, k:k + 1],
                                                 scale=rs[:, lb, k:k + 1]).then_inc(h2r, 1)
                    if not on(1) and on(2):
                        if j == 0:
                            act.wait_ge(x1r, J * (G - 1))
                        nc.scalar.activation(A(j)[:, None, :], store3[:, j:j + 1, :], ACT.Copy).then_inc(c3, 1)
            turns(act, phase2, ahead=1, behind=3)
            act.wait_ge(x1r, T)

            def phase3(g, h, b, on):
                def copy_rows(j):
                    if on(0) and j < J and not (isinstance(g, int) and g == 0):
                        need(act, t3, J * (g - 2) + j + 1)
                        hold(act)
                        nc.scalar.activation(A(b * J + j)[:, None, :],
                                             store3[:, bass.ds(J * g + j, 1), :], ACT.Copy).then_inc(c3, 1)
                for j in range(J + 1):
                    l, _, lb = behind(1, g, h, b)
                    u = lb * J + j
                    if on(1) and j < J:
                        act.wait_ge(t3, J * l + j + 1)
                        need(act, kv, J * l + j - 1)
                        nc.scalar.copy(hT[u % 2], bank[4 + u % 2][:, 0:D]
                                       .rearrange("p (c e) -> p c e", c=NC)).then_inc(hT3, 1)
                    if on(1) and j > 0:
                        act.wait_ge(kv, J * l + j)
                        hold(act)
                        nc.scalar.activation(store3[:, bass.ds(J * l + j - 1, 1), :],
                                             bank[2 + (u - 1) % 2][:, None, 0:D], ACT.Copy).then_inc(v3, 1)
                    copy_rows(2 * j)
                    copy_rows(2 * j + 1)
            turns(act, phase3)
            act.wait_ge(act_sm, 1)
            nc.scalar.activation(ex, xs, ACT.Exp).then_inc(act_sm, 1)

        @block.vector
        def _(dve):
            pro = Chain(dve, pdve)
            pro.start(0)
            nc.vector.memset(ones[:, :], 1.0)
            nc.vector.memset(epsc[:, :], EPS)
            nc.vector.memset(w_zero, 0.0)
            dve.wait_ge(s_idx, 64)
            nc.vector.tensor_copy(w_src, src_i[:, :])
            nc.vector.tensor_copy(w_dstf, dst_i[:, :])
            pro.link(nc.vector.tensor_copy(w_nxt, nxt_i[:, :]))
            pro.link(nc.vector.tensor_tensor(w_eq, w_dstf, w_nxt, ALU.is_equal))
            pro.link(nc.vector.scalar_tensor_tensor(w_fin, w_eq, SKIP, w_dstf, ALU.mult, ALU.add))
            pro.link(nc.vector.tensor_scalar(w_key[:, 0:P - 1], w_eq[:, 0:P - 1], -1.0, 1.0, ALU.mult, ALU.add))
            pro.link(nc.vector.scalar_tensor_tensor(w_key[:, 0:P - 1], w_dstf[:, 0:P - 1], 1.0, w_key[:, 0:P - 1],
                                                    ALU.add, ALU.mult))
            nc.vector.tensor_copy(w_key[:, P - 1:P], w_dstf[:, P - 1:P])
            pro.link(nc.vector.tensor_scalar(w_key[:, 0:P - 1], w_key[:, 0:P - 1], -1.0, None, ALU.add))
            dve.wait_ge(s_cst, 4)
            for k in range(4):
                sel = ident[0:T, 0:T] if k < 2 else anti[:, :]
                endcol = w_dstf[:, 0:1] if k % 2 == 0 else w_dstf[:, P - 1:P]
                nc.vector.tensor_scalar(w_diag[:, k * T:(k + 1) * T], sel, endcol, None, ALU.mult)
            nc.vector.tensor_copy(iota1[:, :], iota_i).then_inc(s_key[0], 1)
            dve.wait_ge(s_tr, 9)
            nc.vector.tensor_copy(dcol, bank[5][:, 0:T])
            nc.vector.tensor_copy(scol[:, :], bank[5][:, T:2 * T])
            nc.vector.tensor_copy(sg_i[:, :], bank[5][:, T:2 * T])
            nc.vector.tensor_copy(wcol, bank[5][:, 2 * T:3 * T])
            nc.vector.tensor_copy(out_i[:, :], bank[5][:, 3 * T:4 * T])
            nc.vector.tensor_scalar(dg_i[:, :], bank[5][:, 0:T], float(N - 1), None, ALU.min)
            nc.vector.memset(DP[:, 0:1], -1.0)
            nc.vector.tensor_copy(DP[:, 1:T], bank[6][:, T:2 * T - 1])
            nc.vector.tensor_copy(per_tile[:, 2:4, :], bank[6][:, 0:2 * T].rearrange("p (k t) -> p k t", k=2))
            pro.link(nc.vector.tensor_copy(ends_r[:, :, :], bank[6][:, 2 * T:4 * T].rearrange("p (k t) -> p k t", k=2)))
            first_r, last_r = ends_r[:, 0, :], ends_r[:, 1, :]
            nc.vector.memset(cnt[:, 2, 0:1], 0.0)
            nc.vector.tensor_tensor(cnt[:, 0, :], first, DP, ALU.is_equal)
            nc.vector.tensor_tensor(cnt[:, 2, 1:T], last_r[:, 1:T], first_r[:, 0:T - 1], ALU.is_equal)
            nc.vector.tensor_tensor(cnt[:, 1, :], first, last, ALU.is_equal)
            pro.link(nc.vector.tensor_tensor(cnt[:, 3, :], first_r, last_r, ALU.is_equal))
            nc.vector.tensor_tensor(cnt[:, 1, :], cnt[:, 1, :], cnt[:, 0, :], ALU.mult)
            nc.vector.tensor_tensor(cnt[:, 3, :], cnt[:, 3, :], cnt[:, 2, :], ALU.mult)
            nc.vector.tensor_tensor(edge_w[:, :, 0], dcol, first, ALU.is_equal)
            pro.link(nc.vector.tensor_tensor(edge_w[:, :, 1], dcol, last, ALU.is_equal))
            pro.link(nc.vector.tensor_tensor(edge_w[:, :, :], edge_w[:, :, :],
                                             wcol[:, :, None].to_broadcast([P, T, 2]), ALU.mult))
            nc.vector.tensor_copy(key_step, bank[7][0:T, 0:P])
            pro.link(nc.vector.tensor_tensor(last_before[0:T, :], w_dstf[:, P - 1:P], bank[7][0:T, P - 1:P], ALU.subtract))
            pro.link(nc.vector.memset(last_before[0:1, :], -1.0))
            nc.vector.tensor_scalar(w_on, w_dstf, last_before[0:T, :], None, ALU.is_equal).then_inc(on_rdy, 1)
            pro.link(nc.vector.memset(pick[:, :, :, :], 0.0))
            for j in range(J):
                ins = nc.vector.memset(pick[:, j, j, :], 1.0)
            pro.link(ins)
            nc.vector.engine_nop().then_inc(s_pro, 1)
            dve.wait_ge(s_mlp, 80)
            dve.wait_ge(s_key[1], 64)

            lead_c, lag_c = Chain(dve, lead1), Chain(dve, lag1)

            def phase1(g, h, b, on):
                if on(0):
                    dve.wait_ge(sr_in[b], 16 * (h + 1))
                    need(dve, keys, g - 1)
                    nc.vector.tensor_scalar(above[b], src_row[b], last_before[0:T, :], None, ALU.is_gt).then_inc(abv, 1)
                if on(2):
                    l2, l2h, l2b = behind(2, g, h, b)
                    dve.wait_ge(fl, l2 + 1)
                    need(dve, st_s[l2b], 16 * l2h)
                    nc.vector.tensor_copy(end_sums[l2b], bank[0][0:2 * J, 0:D]).then_inc(fl_sb, 1)
                if on(1):
                    l, lh, lb = behind(1, g, h, b)
                    need(dve, st_b[lb], 16 * lh)
                    dve.wait_ge(b_ps, 2 * l + 2)
                    for half in range(2):
                        nc.vector.tensor_scalar(biasT[lb][:, half * (GE // 2):(half + 1) * (GE // 2)],
                                                bias_ps[half], b2c[:, :], None, ALU.add).then_inc(bT_sb, 1)
                    lag_c.start(l)
                    dve.wait_ge(keys, l + 1)
                    for j in range(J):
                        ins = nc.vector.scalar_tensor_tensor(keys_ps(j), keys_ps(j), scol[:, bass.ds(J * l + j, 1)],
                                                             iota1[:, :], ALU.is_equal, ALU.mult,
                                                             accum_out=pm[:, j:j + 1])
                    lag_c.link(ins)
                    lag_c.link(nc.vector.tensor_scalar(pz[:, :], pm[:, :], 0.0, SKIP, ALU.is_equal, ALU.mult))
                    lag_c.link(nc.vector.scalar_tensor_tensor(pm[:, :], tauf[:, bass.ds(J * l, J)], float(P), pm[:, :],
                                                              ALU.mult, ALU.add))
                    nc.vector.scalar_tensor_tensor(slot_i[:, bass.ds(J * l, J)], pm[:, :], -1.0, pz[:, :],
                                                   ALU.add, ALU.add).then_inc(slots_done, 1)
                    lag_c.end()
                if on(0):
                    lead_c.start(g)
                    lead_c.link(nc.vector.tensor_tensor(
                        taucmp, last[:, None, :].to_broadcast([P, J, T]),
                        scol[:, bass.ds(J * g, J)][:, :, None].to_broadcast([P, J, T]), ALU.is_lt))
                    nc.vector.tensor_reduce(tauf[:, bass.ds(J * g, J)], taucmp, AX, ALU.add)
                    own = edge_w[:, bass.ds(J * g, J), :][:, :, None, :].to_broadcast([P, J, J, 2])
                    nc.vector.tensor_tensor(pick_w[:, b, :, :, :], pick[:, :, :, :], own, ALU.mult).then_inc(pk, 1)
                    dve.wait_ge(x_in[b], 16 * J * (h + 1))
                    for j in range(J):
                        ins = nc.vector.bn_stats(st6[:, j, :], A(b * J + j))
                    lead_c.link(ins)
                    for j in range(J):
                        ins = nc.vector.bn_aggr(mv[:, b, j, :], st6[:, j, :])
                    ins.then_inc(var1, 1)
                    dve.wait_ge(sd1, g + 1)
                    lead_c.link(nc.vector.reciprocal(rs[:, b, :], sd[:, b, :]))
                    nc.vector.scalar_tensor_tensor(nm[:, b, :], mv[:, b, :, 0], -1.0, rs[:, b, :],
                                                   ALU.mult, ALU.mult).then_inc(rs1, 1)
                    lead_c.end()
                if on(1):
                    dve.wait_ge(bulk_ld[lb], 16 * (lh + 1))
                    v = bulk[lb][:, 0:DVE_ROWS * D].rearrange("p (r d) -> p r d", d=D)
                    nc.vector.tensor_tensor(v, v, bob[:, None, :].to_broadcast([P, DVE_ROWS, D]),
                                            ALU.add).then_inc(bulk_add_dve, 1)
            turns(dve, phase1, behind=2)

            def carries():
                cc = Chain(dve, s_carr)
                cc.start(0)
                dve.wait_ge(sumsT, 4)
                for i in range(2):
                    dve.wait_ge(st_b[i], 16 * (G // 2))
                v = bank[0][:, 0:4 * T].rearrange("p (k c t) -> p k c t", k=2, c=NC)
                nc.vector.tensor_copy(sums[:, 0, :, :], v[:, 1, :, :])
                cc.link(nc.vector.tensor_copy(sums[:, 1, :, :], v[:, 0, :, ::-1]))
                nc.vector.memset(per_tile[:, 5:7, 0:1], 0.0)
                nc.vector.memset(per_tile[:, 7:9, T - 1:T], 0.0)
                for k in range(2):
                    for c in range(NC):
                        ins = nc.vector.tensor_tensor_scan(carr[:, k, c, :], cnt[:, 2 * k + 1, :], sums[:, k, c, :],
                                                           0.0, ALU.mult, ALU.add)
                cc.link(ins)
                for c in range(NC):
                    nc.vector.tensor_tensor(per_tile[:, 5 + c, 1:T], carr[:, 0, c, 0:T - 1], cnt[:, 0, 1:T], ALU.mult)
                    ins = nc.vector.tensor_tensor(per_tile[:, 7 + c, 0:T - 1][:, ::-1], carr[:, 1, c, 0:T - 1],
                                                  cnt[:, 2, 1:T], ALU.mult)
                cc.link(ins)
                cc.link(nc.vector.tensor_copy(here[:, 0, 5:9, :], per_tile[:, 5:9, 0:J]))

            def fetch(g, b):
                n = 5 if isinstance(g, int) and g == 0 else 9
                return nc.vector.tensor_copy(here[:, b, 0:n, :], per_tile[:, 0:n, bass.ds(J * g, J)])
            lag_2, ahead_2 = Chain(dve, lag2), Chain(dve, fetched2)

            def phase2(g, h, b, on):
                a, ah, ab = behind(-1, g, h, b)
                l, lh, lb = behind(1, g, h, b)
                if isinstance(g, int) and g == 0:
                    carries()

                def mark_ends(g, h, b, j):
                    u = b * J + j
                    need(dve, aT2, J * g + j - 1)
                    nc.vector.tensor_scalar(indF(u), row[b][:, j * P:(j + 1) * P],
                                            here[:, b, 2, j:j + 1], None, ALU.is_equal)
                    nc.vector.tensor_scalar(indL(u), row[b][:, j * P:(j + 1) * P],
                                            here[:, b, 3, j:j + 1], None, ALU.is_equal).then_inc(marked, 1)

                def add_x(g, h, b, j):
                    u = b * J + j
                    if j == 0:
                        dve.wait_ge(xd_in[b], 16 * J * (h + 1))
                    for part, (lo, _) in enumerate(PARTS):
                        if j == lo:
                            need(dve, st_h[part][b], 16 * h)
                    need(dve, t2, J * (g - 2) + j + 1)
                    dve.wait_ge(w2p, J * g + j + 1)
                    nc.vector.scalar_tensor_tensor(B(u), bank[2 + u % 2][:, 0:D], 0.0,
                                                   A(u), ALU.max, ALU.add).then_inc(x1r, 1)

                def stats(g, b, j):
                    dve.wait_ge(x1r, J * g + j + 1)
                    return nc.vector.bn_stats(st6[:, j, :], B(b * J + j))

                def same_segment(k):
                    if on(-1) and 0 <= k < J:
                        if k == 0:
                            dve.wait_ge(row_in[ab], 16 * (ah + 1))
                        nc.vector.tensor_scalar(S(ab * J + k), row[ab][:, k * P:(k + 1) * P],
                                                here[:, ab, 0, k:k + 1], None, ALU.is_equal).then_inc(S2, 1)

                for j in range(J):
                    u, t = b * J + j, J * g + j
                    if on(0):
                        dve.wait_ge(marked, t + 1)
                        dve.wait_ge(ag, t + 1)
                        for c in range(NC):
                            ins = nc.vector.scalar_tensor_tensor(
                                aT[u % 2][:, c, :], indF(u), here[:, b, 5 + c, j:j + 1],
                                bank[u % 2][:, c * P:(c + 1) * P], ALU.mult, ALU.add)
                        ins.then_inc(added, 1)
                    if j == 3 and on(-1):
                        ahead_2.start(a)
                        ahead_2.link(fetch(a, ab))
                        ahead_2.end()
                    same_segment(2 * (j - 3))
                    if on(0) and j + 1 < J:
                        mark_ends(g, h, b, j + 1)
                    if on(-1) and j + 1 == J:
                        mark_ends(a, ah, ab, 0)
                    if j == 3 and on(1):
                        dve.wait_ge(sd2, l + 1)
                        lag_2.link(nc.vector.reciprocal(rs[:, lb, :], sd[:, lb, :]))
                        nc.vector.scalar_tensor_tensor(nm[:, lb, :], mv[:, lb, :, 0], -1.0, rs[:, lb, :],
                                                       ALU.mult, ALU.mult).then_inc(rs2, 1)
                        lag_2.end()
                    if j < 3 and on(1):
                        ins = stats(l, lb, J - 3 + j)
                        if j == 2:
                            lag_2.start(l)
                            lag_2.link(ins)
                            for k in range(J):
                                ins = nc.vector.bn_aggr(mv[:, lb, k, :], st6[:, k, :])
                            ins.then_inc(var2, 1)
                    if j >= 3 and on(0):
                        stats(g, b, j - 3)
                    if on(0):
                        dve.wait_ge(added, t + 1)
                        for c in range(NC):
                            ins = nc.vector.scalar_tensor_tensor(
                                aT[u % 2][:, c, :], indL(u), here[:, b, 7 + c, j:j + 1],
                                aT[u % 2][:, c, :], ALU.mult, ALU.add)
                        ins.then_inc(aT2, 1)
                    if j < 2 and on(1):
                        add_x(l, lh, lb, J - 2 + j)
                    same_segment(2 * (j - 3) + 1)
                    if j >= 2 and on(0):
                        add_x(g, h, b, j - 2)
            turns(dve, phase2, ahead=1, behind=2)

            def phase3(g, h, b, on):
                if isinstance(g, int) and g == 2:
                    dve.wait_ge(s_flag, 32)
                    nc.vector.tensor_scalar(neg_cont, f_cont, -1.0, BIG, ALU.add, ALU.mult)
                    nc.vector.tensor_scalar(neg_next, f_next, -1.0, BIG, ALU.add, ALU.mult)
                    nc.vector.tensor_reduce(col[:, 2:3], f_cont, AX, ALU.min)
                    nc.vector.tensor_reduce(col[:, 3:4], f_next, AX, ALU.min)
                if on(1):
                    g, h, b = behind(1, g, h, b)
                    dve.wait_ge(ql[b], 16 * (h + 1))
                    for j in range(J + 1):
                        u = b * J + j
                        if j < J:
                            dve.wait_ge(kv, J * g + j + 1)
                            nc.vector.tensor_tensor(prod[:, j, :], bank[6 + u % 2][:, 0:D], C(u), ALU.mult).then_inc(k3, 1)
                        if j > 0:
                            dve.wait_ge(k3, J * g + j)
                            nc.vector.tensor_reduce(ssum[:, (j - 1) * H:j * H],
                                                    prod[:, j - 1, :].rearrange("p (n e) -> p n e", e=HD),
                                                    AX, ALU.add).then_inc(lag3, 1)
                    dve.wait_ge(lag3, J * (g + 1))
                    hold(dve)
                    nc.vector.tensor_copy(sc_all[:, :, bass.ds(g, 1), :],
                                          ssum[:, :].rearrange("p (j o n) -> p j o n", o=1, n=H)).then_inc(x_sb, 1)
            turns(dve, phase3, behind=2)
            sm = Chain(dve, s_sm)
            sm.start(0)
            dve.wait_ge(x_ps, 2)
            dve.wait_ge(s_bias, 16)
            for lo, hi, k in ((0, 512, 0), (512, GE, 1)):
                ins = nc.vector.scalar_tensor_tensor(xs[:, lo:hi], bank[k][0:GH, 0:hi - lo], float(1.0 / np.sqrt(HD)),
                                                     bias_all[:, lo:hi], ALU.mult, ALU.add)
            sm.link(ins)
            passes = [0]

            def both_scans(values, is_max):
                flags = (neg_cont, neg_next) if is_max else (f_cont, f_next)
                o0, o1, init = (ALU.add, ALU.max, -BIG) if is_max else (ALU.mult, ALU.add, 0.0)

                def scans(first_f, first_b):
                    nc.vector.tensor_tensor_scan(fwd, flags[0], values, first_f, o0, o1)
                    sm.link(nc.vector.tensor_tensor_scan(bwd[:, ::-1], flags[1][:, ::-1], values[:, ::-1], first_b, o0, o1))
                scans(init, init)
                nc.vector.tensor_copy(col[:, 0:1], fwd[:, GE - 1:GE])
                nc.vector.tensor_copy(col[:, 1:2], bwd[:, 0:1]).then_inc(pe_sm, 1)
                passes[0] += 1
                dve.wait_ge(al_ps, 2 * passes[0] - 1)
                for i in range(4):
                    v = bank[2][0:1, i * GH:(i + 1) * GH].rearrange("o (g n) -> o n g", n=H)
                    v = v[:, :, ::-1] if i % 2 else v
                    ins = nc.vector.tensor_copy(lin_in[:, i, :].rearrange("o (n g) -> o n g", n=H), v)
                sm.link(ins)
                sm.link(nc.vector.memset(lin_in[:, 2:4, :].rearrange("o k (n g) -> o (k n) g", g=G)[:, :, 0:1], 0.0))
                if is_max:
                    sm.link(nc.vector.tensor_scalar(lin_in[:, 2:4, :], lin_in[:, 2:4, :], -1.0, BIG, ALU.add, ALU.mult))
                nc.vector.memset(lin_carry[:, :, :], init)
                for i in range(2):
                    ins = nc.vector.tensor_tensor_scan(lin_out[:, i, :], lin_in[:, 2 + i, :], lin_in[:, i, :], init, o0, o1)
                sm.link(ins)
                for i in range(2):
                    v = lin_carry[:, i, :].rearrange("o (g n) -> o n g", n=H)
                    v = v[:, :, ::-1] if i else v
                    ins = nc.vector.tensor_copy(v[:, :, 1:G], lin_out[:, i, :].rearrange("o (n g) -> o n g", n=H)[:, :, 0:G - 1])
                ins.then_inc(pe_sm, 1)
                dve.wait_ge(al_ps, 2 * passes[0])
                sm.link(nc.vector.tensor_copy(carry[:, :], bank[3][0:GH, 0:2]))
                scans(carry[:, 0:1], carry[:, 1:2])

            both_scans(xs, True)
            sm.link(nc.vector.tensor_tensor(total, fwd, bwd, ALU.max))
            nc.vector.tensor_tensor(xs, xs, total, ALU.subtract).then_inc(act_sm, 1)
            dve.wait_ge(act_sm, 2)
            both_scans(ex, False)
            sm.link(nc.vector.tensor_tensor(bwd, bwd, ex, ALU.subtract))
            sm.link(nc.vector.tensor_tensor(total, fwd, bwd, ALU.add))
            sm.link(nc.vector.reciprocal(total, total))
            sm.link(nc.vector.tensor_tensor(xs, ex, total, ALU.mult))
            nc.vector.engine_nop().then_inc(pe_sm, 1)
            dve.wait_ge(al_ps, 2 * passes[0] + 1)
            nc.vector.memset(aT[1], 0.0)
            nc.vector.tensor_copy(sc_all[:, 0:4, :, :], bank[4][:, 0:4 * GH].rearrange("p (j g n) -> p j g n", j=4, n=H))
            sm.link(nc.vector.tensor_copy(sc_all[:, 4:J, :, :], bank[5][:, 0:3 * GH].rearrange("p (j g n) -> p j g n", j=3, n=H)))


            ahead_4 = Chain(dve, fetched4)

            def phase4(g, h, b, on):
                a, ah, ab = behind(-1, g, h, b)

                def weigh(k):
                    if not on(-1) or not 0 <= k < J:
                        return
                    if k == 0:
                        ahead_4.start(a)
                        nc.vector.tensor_copy(al_here[:, ab, :, None, :], sc_all[:, :, bass.ds(a, 1), :])
                        ahead_4.link(nc.vector.tensor_copy(here[:, ab, 0, :], dcol[:, bass.ds(J * a, J)]))
                        ahead_4.end()
                        dve.wait_ge(row4[ab], 16 * (ah + 1))
                    u = ab * J + k
                    nc.vector.tensor_scalar(S(u), row[ab][:, k * P:(k + 1) * P], here[:, ab, 0, k:k + 1], None,
                                            ALU.is_equal)
                    al = al_here[:, ab, k, :, None].to_broadcast([P, H, HD])
                    nc.vector.tensor_tensor(A(u).rearrange("p (n e) -> p n e", n=H),
                                            store[:, bass.ds((J * a + k) * D, D)].rearrange("p (n e) -> p n e", n=H),
                                            al, ALU.mult).then_inc(s4, 1)
                def add_x1(g, h, b, j):
                    u = b * J + j
                    if j == 0:
                        dve.wait_ge(bo4, g + 1)
                        need(dve, sc_out[b], 16 * J * h)
                    dve.wait_ge(wo, J * g + j + 1)
                    nc.vector.tensor_tensor(C(u), bank[2 + u % 2][:, 0:D], B(u), ALU.add).then_inc(o4, 1)

                for j in range(J):
                    u, t = b * J + j, J * g + j
                    if on(0):
                        if j == 0:
                            dve.wait_ge(on4[b], 16 * (h + 1))
                        need(dve, aT4, t)
                        dve.wait_ge(ag4, t + 1)
                        for c in range(NC):
                            ins = nc.vector.scalar_tensor_tensor(
                                aT[u % 2][:, c, :], runs_on(u), aT[(u + 1) % 2][:, c, P - 1:P],
                                bank[u % 2][:, c * P:(c + 1) * P], ALU.mult, ALU.add)
                        ins.then_inc(aT4, 1)
                    weigh(j)
                    if j < 2 and on(1):
                        add_x1(*behind(1, g, h, b), J - 2 + j)
                    if j >= 2 and on(0):
                        add_x1(g, h, b, j - 2)
            turns(dve, phase4, ahead=1, behind=1)

        @block.tensor
        def _(pe):
            def mm(o, lhsT, rhs, start=True, stop=True):
                return nc.tensor.matmul(o, lhsT, rhs, start=start, stop=stop)

            pe.wait_ge(s_key[0], 1)
            for k, r in enumerate((w_dstf, w_src, w_r[:, :], w_fin)):
                nc.tensor.transpose(bank[5][:, k * T:(k + 1) * T], r, ident[0:T, 0:T]).then_inc(s_tr, 1)
            for k in range(4):
                mm(bank[6][:, k * T:(k + 1) * T], ones[0:T, :], w_diag[:, k * T:(k + 1) * T]).then_inc(s_tr, 1)
            mm(bank[7][0:T, 0:P], diff, w_key).then_inc(s_tr, 1)
            pe.wait_ge(s_mlp, 80)

            def phase1(g, h, b, on):
                def hidden(m):
                    c, half = m // 2, m % 2
                    need(pe, hid_sb, 4 * g + m - 1)
                    mm(bank[3 + m % 2][:, 0:GE // 2], W1sb[:, c * P:(c + 1) * P],
                       eT[:, half * (GE // 2):(half + 1) * (GE // 2)]).then_inc(hid_ps, 1)
                if on(0):
                    pe.wait_ge(eT_sb, g + 1)
                    hidden(0)
                    hidden(1)
                if on(1):
                    l, lh, lb = behind(1, g, h, b)
                    need(pe, fl_sb, l)
                    pe.wait_ge(pk, l + 1)
                    for j in range(J):
                        pe.wait_ge(h1a, J * l + j + 1)
                        ins = mm(bank[0][0:2 * J, 0:D], pick_w[:, lb, j, :, :].rearrange("p i k -> p (i k)"),
                                 A(lb * J + j), start=(j == 0), stop=(j == J - 1))
                    ins.then_inc(fl, 1)
                if on(0):
                    hidden(2)
                    hidden(3)
                if on(-1):
                    a, ah, ab = behind(-1, g, h, b)
                    pe.wait_ge(ef_in[ab], 16 * (ah + 1))
                    need(pe, bT_sb, 2 * g)
                    hold(pe)
                    for j in range(J):
                        ins = nc.tensor.transpose(bank[1 + j // 4][0:FE, (j % 4) * P:(j % 4 + 1) * P],
                                                  ef[ab][:, j * FE:(j + 1) * FE], ident[:, :])
                    ins.then_inc(eT_ps, 1)
                if on(0):
                    pe.wait_ge(abv, g + 1)
                    need(pe, slots_done, g)
                    hold(pe)
                    for j in range(J):
                        ins = mm(keys_ps(j), above[b][:, j * P:(j + 1) * P], key_step)
                    ins.then_inc(keys, 1)
                    for half in range(2):
                        if half == 0:
                            need(pe, bT_sb, 2 * g)
                        elif on(-1):
                            pe.wait_ge(eT_sb, g + 2)
                        pe.wait_ge(hid_sb, 4 * g + 3 + half)
                        for c in range(NC):
                            ins = mm(bias_ps[half], W2sb[:, c, :],
                                     hid[:, c, half * (GE // 2):(half + 1) * (GE // 2)],
                                     start=(c == 0), stop=(c == NC - 1))
                        ins.then_inc(b_ps, 1)
            turns(pe, phase1, ahead=1)
            pe.wait_ge(fl_sb, G)
            pe.wait_ge(s_sums, 16)
            for k in range(2 * NC):
                nc.tensor.transpose(bank[0][:, k * T:(k + 1) * T], sums_in[:, k * P:(k + 1) * P],
                                    ident[0:T, 0:T]).then_inc(sumsT, 1)
            pe.wait_ge(s_carr, 1)
            pe.wait_ge(bT_sb, 2 * G)

            pe.wait_ge(s_wts, 80)

            def phase2(g, h, b, on):
                l, _, lb = behind(1, g, h, b)
                l2, _, l2b = behind(2, g, h, b)
                l3, _, l3b = behind(3, g, h, b)

                def layer0(g, b, j):
                    t, v = J * g + j, b * J + j
                    pe.wait_ge(aT2, t + 1)
                    need(pe, x1r, t - 1)
                    for c in range(NC):
                        ins = mm(bank[2 + v % 2][:, 0:D], aT[v % 2][:, c, :], Wsb[:, c, :],
                                 start=(c == 0), stop=(c == NC - 1))
                    ins.then_inc(w2p, 1)

                def queries(g, b, j):
                    t, v = J * g + j, b * J + j
                    pe.wait_ge(hT2, t + 1)
                    need(pe, q2, t - 1)
                    for c in range(NC):
                        ins = mm(bank[6 + v % 2][:, 0:D], hT[v % 2][:, c, :], Wqsb[:, c, :],
                                 start=(c == 0), stop=(c == NC - 1))
                    ins.then_inc(qp, 1)

                for j in range(J):
                    if on(0):
                        u, t = b * J + j, J * g + j
                        pe.wait_ge(S2, t + 1)
                        pe.wait_ge(hs, t + 1)
                        need(pe, aT2, t - 1)
                        for c in range(NC):
                            ins = mm(bank[u % 2][:, c * P:(c + 1) * P], C(j)[:, c * P:(c + 1) * P], S(u))
                        ins.then_inc(ag, 1)
                    if on(2):
                        u, t = l2b * J + j, J * l2 + j
                        pe.wait_ge(h2r, t + 1)
                        need(pe, hT2, t - 1)
                        for c in range(NC):
                            ins = nc.tensor.transpose(bank[4 + u % 2][:, c * P:(c + 1) * P],
                                                      B(u)[:, c * P:(c + 1) * P], ident[:, :])
                        ins.then_inc(t2, 1)
                    if j == 0 and on(1):
                        layer0(l, lb, J - 1)
                    if j > 0 and on(0):
                        layer0(g, b, j - 1)
                    if j == 0 and on(3):
                        queries(l3, l3b, J - 1)
                    if j > 0 and on(2):
                        queries(l2, l2b, j - 1)
            turns(pe, phase2, ahead=0, behind=3)
            pe.wait_ge(q2, T)

            def phase3(g, h, b, on):
                if on(1):
                    g, h, b = behind(1, g, h, b)
                    pe.wait_ge(o_in[b], 16 * J * (h + 1))
                    for j in range(J + 1):
                        u = b * J + j
                        if j < J:
                            t = J * g + j
                            need(pe, hT3, t - 1)
                            for c in range(NC):
                                ins = nc.tensor.transpose(bank[4 + u % 2][:, c * P:(c + 1) * P],
                                                          A(u)[:, c * P:(c + 1) * P], ident[:, :])
                            ins.then_inc(t3, 1)
                        if j > 0:
                            t, v = J * g + j - 1, u - 1
                            pe.wait_ge(hT3, t + 1)
                            need(pe, k3, t - 1)
                            need(pe, v3, t - 1)
                            for c in range(NC):
                                mm(bank[6 + v % 2][:, 0:D], hT[v % 2][:, c, :], Wkv[:, c, 0:D],
                                   start=(c == 0), stop=(c == NC - 1))
                                ins = mm(bank[2 + v % 2][:, 0:D], hT[v % 2][:, c, :], Wkv[:, c, D:2 * D],
                                         start=(c == 0), stop=(c == NC - 1))
                            ins.then_inc(kv, 1)
            turns(pe, phase3)
            pe.wait_ge(x_sb, G)
            pe.wait_ge(v3, T)
            for j in range(J):
                ins = nc.tensor.transpose(bank[j // 4][0:GH, (j % 4) * P:(j % 4 + 1) * P],
                                          sc_all[:, j, :, :].rearrange("p g n -> p (g n)"), ident[:, :])
                if j in (3, J - 1):
                    ins.then_inc(x_ps, 1)
            for k in range(2):
                pe.wait_ge(pe_sm, 2 * k + 1)
                for i in range(4):
                    ins = mm(bank[2][0:1, i * GH:(i + 1) * GH], col[:, i:i + 1], ident[0:GH, 0:GH])
                ins.then_inc(al_ps, 1)
                pe.wait_ge(pe_sm, 2 * k + 2)
                for i in range(2):
                    ins = mm(bank[3][0:GH, i:i + 1], lin_carry[:, i, :], ones[0:1, 0:1])
                ins.then_inc(al_ps, 1)
            pe.wait_ge(pe_sm, 5)
            for j in range(J):
                ins = nc.tensor.transpose(bank[4 + j // 4][:, (j % 4) * GH:(j % 4 + 1) * GH],
                                          xs[:, j * P:(j + 1) * P], ident[0:GH, 0:GH])
            ins.then_inc(al_ps, 1)

            def phase4(g, h, b, on):
                def project(g, b, j):
                    t, v = J * g + j, b * J + j
                    pe.wait_ge(aT4, t + 1)
                    need(pe, o4, t - 1)
                    for c in range(NC):
                        ins = mm(bank[2 + v % 2][:, 0:D], aT[v % 2][:, c, :], Wosb[:, c, :],
                                 start=(c == 0), stop=(c == NC - 1))
                    ins.then_inc(wo, 1)

                for j in range(J):
                    if on(0):
                        u, t = b * J + j, J * g + j
                        pe.wait_ge(s4, t + 1)
                        need(pe, aT4, t - 1)
                        for c in range(NC):
                            ins = mm(bank[u % 2][:, c * P:(c + 1) * P], A(u)[:, c * P:(c + 1) * P], S(u))
                        ins.then_inc(ag4, 1)
                    if j == 0 and on(1):
                        l, _, lb = behind(1, g, h, b)
                        project(l, lb, J - 1)
                    if j > 0 and on(0):
                        project(g, b, j - 1)
            turns(pe, phase4, ahead=0, behind=1)


def kernel(**inputs):
    import numpy as _np
    import concourse.bacc as _bacc
    from concourse import mybir as _mybir
    from concourse.bass_utils import run_bass_kernel_spmd as _run

    a = {k: _np.ascontiguousarray(v) for k, v in inputs.items()}
    pad = EP - E
    dst = _np.full(EP + 1, PAD_DST, a['dst'].dtype)
    dst[0:E] = a['dst']
    dst[EP] = -1
    src = _np.zeros(EP, a['src'].dtype)
    src[0:E] = a['src']
    wgt = _np.zeros(EP, a['edge_weight'].dtype)
    wgt[0:E] = a['edge_weight']
    eattr = _np.zeros((EP, FE), a['edge_attr_64'].dtype)
    eattr[0:E] = a['edge_attr_64']
    arrays = {'x': a['x'], 'dst': dst, 'src': src, 'wgt': wgt, 'eattr': eattr, 'W': a['L0_gnn_weight']}
    for n in ('Wq', 'Wk', 'Wv', 'W1', 'b1', 'W2', 'b2', 'Wo', 'bo'):
        arrays[n] = a['L1_gnn_' + n]
    nc = _bacc.Bacc("TRN2", target_bir_lowering=False, num_devices=1)
    arrays = {'in_' + k: v for k, v in arrays.items()}
    args = [nc.dram_tensor(k, v.shape, _mybir.dt.from_np(v.dtype), kind="ExternalInput").ap() for k, v in arrays.items()]
    out = nc.dram_tensor("out_x", (N, D), _mybir.dt.float32, kind="ExternalOutput").ap()
    gnn_program(nc, *args, out)
    r = _run(nc, [arrays], core_ids=[0])
    return r.results[0]["out_x"]
```
